# Optimizing a Trainium2 kernel written in Bass

```python
import numpy as np
import jax
import jax.numpy as jnp

def _softmax(x, axis=-1):
    return jax.nn.softmax(x, axis=axis)

def _gelu(x):
    return jax.nn.gelu(x, approximate=True)

def _silu(x):
    return jax.nn.silu(x)

def _sigmoid(x):
    return jax.nn.sigmoid(x)

def _layernorm(x, axis=-1, eps=1e-05):
    m = jnp.mean(x, axis=axis, keepdims=True)
    v = jnp.var(x, axis=axis, keepdims=True)
    return (x - m) / jnp.sqrt(v + eps)

def _scatter_add(tgt, idx, src, axis=0):
    return tgt.at[idx].add(src)

def _segment_sum(src, seg, n):
    return jax.ops.segment_sum(src, seg, n)
kernel_name = 'mk_vit_tower_d1_tok_img768_r4_1ceb34'

def setup_inputs(seed: int=0):
    np.random.seed(seed)
    _w = jnp.asarray

    def _rec_inputs():
        import jax
        import jax.numpy as jnp
        _rk = jax.random.key(seed)
        x = -0.000222058 + 0.999998 * jax.random.normal(jax.random.fold_in(_rk, 1), (16, 3, 112, 112), jnp.float32)
        return x
    x = _rec_inputs()

    def _L0_tok_setup():
        import jax, jax.numpy as jnp
        import numpy as np
        DIM = 192
        HEADS = 12
        HEAD_DIM = DIM // HEADS
        MLP_HIDDEN = DIM * 4
        PATCH = 16
        IMG = 128
        CH = 3
        BATCH = 32
        WINDOW = 128
        MAX_FREQ = 10.0
        LN_EPS = 1e-05
        TOKEN_SELF_ATTN_VALUE = -50000.0

        def layernorm(x, g, b):
            mu = jnp.mean(x, -1, keepdims=True)
            var = jnp.var(x, -1, keepdims=True)
            return (x - mu) * jax.lax.rsqrt(var + LN_EPS) * g + b

        def swiglu(x, w1, w2, w3):
            return jax.nn.silu(x @ w1) * (x @ w3) @ w2

        def axial_rotary_sin(n, dim):
            scales = jnp.linspace(1.0, MAX_FREQ / 2, dim // 4)
            seq = jnp.linspace(-1.0, 1.0, n)[:, None] * scales[None, :] * jnp.pi
            x_sinu = jnp.broadcast_to(seq[:, None, :], (n, n, dim // 4))
            y_sinu = jnp.broadcast_to(seq[None, :, :], (n, n, dim // 4))
            sin = jnp.concatenate([jnp.sin(x_sinu), jnp.sin(y_sinu)], -1).reshape(n * n, dim // 2)
            return jnp.repeat(sin, 2, axis=-1)[None]

        def rotate_half(t):
            t1, t2 = jnp.split(t, 2, axis=-1)
            return jnp.concatenate([-t2, t1], axis=-1)

        def local_attention(q, k, v):
            b, n0, d = q.shape
            inv_freq = 1.0 / 10000.0 ** (jnp.arange(0, d, 2, dtype=jnp.float32) / d)
            freqs = jnp.arange(n0, dtype=jnp.float32)[:, None] * inv_freq[None, :]
            freqs = jnp.concatenate([freqs, freqs], -1)
            cos_f, sin_f = (jnp.cos(freqs), jnp.sin(freqs))
            q = q * cos_f + rotate_half(q) * sin_f
            k = k * cos_f + rotate_half(k) * sin_f
            pad = -n0 % WINDOW
            if pad:
                q, k, v = (jnp.pad(t, ((0, 0), (0, pad), (0, 0))) for t in (q, k, v))
            n = n0 + pad
            w = n // WINDOW
            k = k / jnp.maximum(jnp.linalg.norm(k, axis=-1, keepdims=True), 1e-12)
            bq = q.reshape(b, w, WINDOW, d)
            bk = k.reshape(b, w, WINDOW, d)
            bv = v.reshape(b, w, WINDOW, d)

            def look_around(t, pad_value):
                pad_cfg = [(0, 0), (1, 0)] + [(0, 0)] * (t.ndim - 2)
                padded = jnp.pad(t, pad_cfg, constant_values=pad_value)
                return jnp.concatenate([padded[:, :w], padded[:, 1:w + 1]], axis=2)
            bk = look_around(bk, -1.0)
            bv = look_around(bv, -1.0)
            seq = jnp.arange(n).reshape(1, w, WINDOW)
            i_idx = seq[..., :, None]
            j_idx = look_around(seq, -1)[..., None, :]
            sim = jnp.einsum('bwie,bwje->bwij', bq, bk) * d ** (-0.5)
            neg = -jnp.finfo(sim.dtype).max
            sim = jnp.where(i_idx == j_idx, TOKEN_SELF_ATTN_VALUE, sim)
            sim = jnp.where(i_idx < j_idx, neg, sim)
            sim = jnp.where(j_idx == -1, neg, sim)
            attn = jax.nn.softmax(sim, -1)
            out = jnp.einsum('bwij,bwje->bwie', attn, bv).reshape(b, n, d)
            return out[:, :n0]

        def mqa(x, wqkv, bqkv, wo, bo):
            b, n, d = x.shape
            qkv = x @ wqkv + bqkv
            q = qkv[..., :DIM].reshape(b, n, HEADS, HEAD_DIM)
            kk = qkv[..., DIM:DIM + HEAD_DIM]
            vv = qkv[..., DIM + HEAD_DIM:]
            scores = jnp.einsum('bihd,bjd->bhij', q, kk) * (1.0 / np.sqrt(HEAD_DIM))
            causal = jnp.arange(n)[:, None] >= jnp.arange(n)[None, :]
            scores = jnp.where(causal, scores, jnp.finfo(scores.dtype).min)
            attn = jax.nn.softmax(scores, -1)
            out = jnp.einsum('bhij,bjd->bihd', attn, vv).reshape(b, n, d)
            return out @ wo + bo

        def _forward(x, patch_w, patch_b, ln_g, ln_b, w1, w2, w3, wqkv, bqkv, wo, bo):
            b, c, h, wd = x.shape
            hh, ww = (h // PATCH, wd // PATCH)
            patches = x.reshape(b, c, hh, PATCH, ww, PATCH).transpose(0, 2, 4, 3, 5, 1)
            patches = patches.reshape(b, hh * ww, PATCH * PATCH * c)
            tok = patches @ patch_w + patch_b
            skip1 = tok
            n_side = int(np.sqrt(hh * ww))
            sin = axial_rotary_sin(n_side, DIM)
            _ = layernorm(tok, ln_g, ln_b)
            y = local_attention(sin, sin, sin) + skip1
            skip2 = y
            y = layernorm(y, ln_g, ln_b)
            y = swiglu(y, w1, w2, w3) + skip2
            _ = layernorm(y, ln_g, ln_b)
            z = mqa(sin, wqkv, bqkv, wo, bo) + skip1
            skip3 = z
            z = layernorm(z, ln_g, ln_b)
            return swiglu(z, w1, w2, w3) + skip3
        key = jax.random.key(seed)
        ks = jax.random.split(key, 8)
        patch_dim = CH * PATCH * PATCH
        s = lambda fan_in: 1.0 / np.sqrt(fan_in)
        return {'x': jax.random.normal(ks[0], (BATCH, CH, IMG, IMG), jnp.float32), 'patch_w': jax.random.normal(ks[1], (patch_dim, DIM), jnp.float32) * s(patch_dim), 'patch_b': jnp.zeros((DIM,), jnp.float32), 'ln_g': jnp.ones((DIM,), jnp.float32), 'ln_b': jnp.zeros((DIM,), jnp.float32), 'w1': jax.random.normal(ks[2], (DIM, MLP_HIDDEN), jnp.float32) * s(DIM), 'w2': jax.random.normal(ks[3], (MLP_HIDDEN, DIM), jnp.float32) * s(MLP_HIDDEN), 'w3': jax.random.normal(ks[4], (DIM, MLP_HIDDEN), jnp.float32) * s(DIM), 'wqkv': jax.random.normal(ks[5], (DIM, DIM + 2 * HEAD_DIM), jnp.float32) * s(DIM), 'bqkv': jnp.zeros((DIM + 2 * HEAD_DIM,), jnp.float32), 'wo': jax.random.normal(ks[6], (DIM, DIM), jnp.float32) * s(DIM), 'bo': jnp.zeros((DIM,), jnp.float32)}
    _L0_tok_all = _L0_tok_setup()
    _L0_tok_in = {k: v for k, v in _L0_tok_all.items() if k in ('patch_w', 'patch_b', 'ln_g', 'ln_b', 'w1', 'w2', 'w3', 'wqkv', 'bqkv', 'wo', 'bo')}
    del _L0_tok_all

    def _L0_attn_setup():
        import jax, jax.numpy as jnp
        import numpy as np
        B, N, DIM = (8, 256, 192)
        H = 12
        HD = DIM // H
        key = jax.random.key(seed)
        k1, k2, k3 = jax.random.split(key, 3)
        x = jax.random.normal(k1, (B, N, DIM), dtype=jnp.float32)
        scale = 1.0 / np.sqrt(DIM)
        Wq = jax.random.uniform(k2, (H * HD, DIM), dtype=jnp.float32, minval=-scale, maxval=scale)
        Wk = jax.random.uniform(k3, (H * HD, DIM), dtype=jnp.float32, minval=-scale, maxval=scale)
        betas = jnp.full((H,), HD ** (-0.5), dtype=jnp.float32)
        return {'x': x, 'Wq': Wq, 'Wk': Wk, 'betas': betas}
    _L0_attn_all = _L0_attn_setup()
    _L0_attn_in = {k: v for k, v in _L0_attn_all.items() if k in ('Wq', 'Wk', 'betas')}
    del _L0_attn_all

    def _L0_ffn_setup():
        import jax, jax.numpy as jnp
        import numpy as np
        D = 192
        M = 768
        G = 4
        E = 8
        KG = 2
        KE = 4
        EPS = 1e-06

        def _topk_gates(logits, k):
            top, idx = jax.lax.top_k(logits, k)
            gates = jax.nn.softmax(top, axis=-1)
            gates = jnp.where(gates >= EPS, gates, jnp.zeros_like(gates))
            return (gates, idx)
        key = jax.random.key(seed)
        ks = jax.random.split(key, 9)
        x = jax.random.normal(ks[0], (1, 256, D), dtype=jnp.float32)
        Wg = jax.random.normal(ks[1], (D, G), dtype=jnp.float32) * 0.02
        bg = jax.random.normal(ks[2], (G,), dtype=jnp.float32) * 0.01
        We = jax.random.normal(ks[3], (G, D, E), dtype=jnp.float32) * 0.02
        be = jax.random.normal(ks[4], (G, E), dtype=jnp.float32) * 0.01
        W1 = jax.random.normal(ks[5], (G, E, D, M), dtype=jnp.float32) * 0.02
        b1 = jax.random.normal(ks[6], (G, E, M), dtype=jnp.float32) * 0.01
        W2 = jax.random.normal(ks[7], (G, E, M, D), dtype=jnp.float32) * 0.02
        b2 = jax.random.normal(ks[8], (G, E, D), dtype=jnp.float32) * 0.01
        return {'x': x, 'Wg': Wg, 'bg': bg, 'We': We, 'be': be, 'W1': W1, 'b1': b1, 'W2': W2, 'b2': b2}
    _L0_ffn_all = _L0_ffn_setup()
    _L0_ffn_in = {k: v for k, v in _L0_ffn_all.items() if k in ('Wg', 'bg', 'We', 'be', 'W1', 'b1', 'W2', 'b2')}
    del _L0_ffn_all
    return {'x': x, 'L0_tok_patch_w': _L0_tok_in['patch_w'], 'L0_tok_patch_b': _L0_tok_in['patch_b'], 'L0_tok_ln_g': _L0_tok_in['ln_g'], 'L0_tok_ln_b': _L0_tok_in['ln_b'], 'L0_tok_w1': _L0_tok_in['w1'], 'L0_tok_w2': _L0_tok_in['w2'], 'L0_tok_w3': _L0_tok_in['w3'], 'L0_tok_wqkv': _L0_tok_in['wqkv'], 'L0_tok_bqkv': _L0_tok_in['bqkv'], 'L0_tok_wo': _L0_tok_in['wo'], 'L0_tok_bo': _L0_tok_in['bo'], 'L0_attn_Wq': _L0_attn_in['Wq'], 'L0_attn_Wk': _L0_attn_in['Wk'], 'L0_attn_betas': _L0_attn_in['betas'], 'L0_ffn_Wg': _L0_ffn_in['Wg'], 'L0_ffn_bg': _L0_ffn_in['bg'], 'L0_ffn_We': _L0_ffn_in['We'], 'L0_ffn_be': _L0_ffn_in['be'], 'L0_ffn_W1': _L0_ffn_in['W1'], 'L0_ffn_b1': _L0_ffn_in['b1'], 'L0_ffn_W2': _L0_ffn_in['W2'], 'L0_ffn_b2': _L0_ffn_in['b2']}

def reference(x, L0_tok_patch_w, L0_tok_patch_b, L0_tok_ln_g, L0_tok_ln_b, L0_tok_w1, L0_tok_w2, L0_tok_w3, L0_tok_wqkv, L0_tok_bqkv, L0_tok_wo, L0_tok_bo, L0_attn_Wq, L0_attn_Wk, L0_attn_betas, L0_ffn_Wg, L0_ffn_bg, L0_ffn_We, L0_ffn_be, L0_ffn_W1, L0_ffn_b1, L0_ffn_W2, L0_ffn_b2):
    import jax
    import jax.numpy as jnp

    def _L0_tok_ref(x, patch_w, patch_b, ln_g, ln_b, w1, w2, w3, wqkv, bqkv, wo, bo):
        import jax, jax.numpy as jnp
        import numpy as np
        DIM = 192
        HEADS = 12
        HEAD_DIM = DIM // HEADS
        MLP_HIDDEN = DIM * 4
        PATCH = 16
        IMG = 128
        CH = 3
        BATCH = 32
        WINDOW = 128
        MAX_FREQ = 10.0
        LN_EPS = 1e-05
        TOKEN_SELF_ATTN_VALUE = -50000.0

        def layernorm(x, g, b):
            mu = jnp.mean(x, -1, keepdims=True)
            var = jnp.var(x, -1, keepdims=True)
            return (x - mu) * jax.lax.rsqrt(var + LN_EPS) * g + b

        def swiglu(x, w1, w2, w3):
            return jax.nn.silu(x @ w1) * (x @ w3) @ w2

        def axial_rotary_sin(n, dim):
            scales = jnp.linspace(1.0, MAX_FREQ / 2, dim // 4)
            seq = jnp.linspace(-1.0, 1.0, n)[:, None] * scales[None, :] * jnp.pi
            x_sinu = jnp.broadcast_to(seq[:, None, :], (n, n, dim // 4))
            y_sinu = jnp.broadcast_to(seq[None, :, :], (n, n, dim // 4))
            sin = jnp.concatenate([jnp.sin(x_sinu), jnp.sin(y_sinu)], -1).reshape(n * n, dim // 2)
            return jnp.repeat(sin, 2, axis=-1)[None]

        def rotate_half(t):
            t1, t2 = jnp.split(t, 2, axis=-1)
            return jnp.concatenate([-t2, t1], axis=-1)

        def local_attention(q, k, v):
            b, n0, d = q.shape
            inv_freq = 1.0 / 10000.0 ** (jnp.arange(0, d, 2, dtype=jnp.float32) / d)
            freqs = jnp.arange(n0, dtype=jnp.float32)[:, None] * inv_freq[None, :]
            freqs = jnp.concatenate([freqs, freqs], -1)
            cos_f, sin_f = (jnp.cos(freqs), jnp.sin(freqs))
            q = q * cos_f + rotate_half(q) * sin_f
            k = k * cos_f + rotate_half(k) * sin_f
            pad = -n0 % WINDOW
            if pad:
                q, k, v = (jnp.pad(t, ((0, 0), (0, pad), (0, 0))) for t in (q, k, v))
            n = n0 + pad
            w = n // WINDOW
            k = k / jnp.maximum(jnp.linalg.norm(k, axis=-1, keepdims=True), 1e-12)
            bq = q.reshape(b, w, WINDOW, d)
            bk = k.reshape(b, w, WINDOW, d)
            bv = v.reshape(b, w, WINDOW, d)

            def look_around(t, pad_value):
                pad_cfg = [(0, 0), (1, 0)] + [(0, 0)] * (t.ndim - 2)
                padded = jnp.pad(t, pad_cfg, constant_values=pad_value)
                return jnp.concatenate([padded[:, :w], padded[:, 1:w + 1]], axis=2)
            bk = look_around(bk, -1.0)
            bv = look_around(bv, -1.0)
            seq = jnp.arange(n).reshape(1, w, WINDOW)
            i_idx = seq[..., :, None]
            j_idx = look_around(seq, -1)[..., None, :]
            sim = jnp.einsum('bwie,bwje->bwij', bq, bk) * d ** (-0.5)
            neg = -jnp.finfo(sim.dtype).max
            sim = jnp.where(i_idx == j_idx, TOKEN_SELF_ATTN_VALUE, sim)
            sim = jnp.where(i_idx < j_idx, neg, sim)
            sim = jnp.where(j_idx == -1, neg, sim)
            attn = jax.nn.softmax(sim, -1)
            out = jnp.einsum('bwij,bwje->bwie', attn, bv).reshape(b, n, d)
            return out[:, :n0]

        def mqa(x, wqkv, bqkv, wo, bo):
            b, n, d = x.shape
            qkv = x @ wqkv + bqkv
            q = qkv[..., :DIM].reshape(b, n, HEADS, HEAD_DIM)
            kk = qkv[..., DIM:DIM + HEAD_DIM]
            vv = qkv[..., DIM + HEAD_DIM:]
            scores = jnp.einsum('bihd,bjd->bhij', q, kk) * (1.0 / np.sqrt(HEAD_DIM))
            causal = jnp.arange(n)[:, None] >= jnp.arange(n)[None, :]
            scores = jnp.where(causal, scores, jnp.finfo(scores.dtype).min)
            attn = jax.nn.softmax(scores, -1)
            out = jnp.einsum('bhij,bjd->bihd', attn, vv).reshape(b, n, d)
            return out @ wo + bo

        def _forward(x, patch_w, patch_b, ln_g, ln_b, w1, w2, w3, wqkv, bqkv, wo, bo):
            b, c, h, wd = x.shape
            hh, ww = (h // PATCH, wd // PATCH)
            patches = x.reshape(b, c, hh, PATCH, ww, PATCH).transpose(0, 2, 4, 3, 5, 1)
            patches = patches.reshape(b, hh * ww, PATCH * PATCH * c)
            tok = patches @ patch_w + patch_b
            skip1 = tok
            n_side = int(np.sqrt(hh * ww))
            sin = axial_rotary_sin(n_side, DIM)
            _ = layernorm(tok, ln_g, ln_b)
            y = local_attention(sin, sin, sin) + skip1
            skip2 = y
            y = layernorm(y, ln_g, ln_b)
            y = swiglu(y, w1, w2, w3) + skip2
            _ = layernorm(y, ln_g, ln_b)
            z = mqa(sin, wqkv, bqkv, wo, bo) + skip1
            skip3 = z
            z = layernorm(z, ln_g, ln_b)
            return swiglu(z, w1, w2, w3) + skip3
        return _forward(x, patch_w, patch_b, ln_g, ln_b, w1, w2, w3, wqkv, bqkv, wo, bo)

    def _L0_attn_ref(x, Wq, Wk, betas):
        import jax, jax.numpy as jnp
        import numpy as np
        B, N, DIM = (8, 256, 192)
        H = 12
        HD = DIM // H
        Q = jnp.einsum('bnd,hzd->bhnz', x, Wq.reshape(H, HD, DIM))
        K = jnp.einsum('bnd,hzd->bhnz', x, Wk.reshape(H, HD, DIM))
        Wqr = Wq.reshape(H, HD, DIM)
        Wkr = Wk.reshape(H, HD, DIM)
        F1 = jnp.einsum('hzd,bhkz->bkhd', Wqr, K)
        F2 = jnp.einsum('hzd,bhqz->bqhd', Wkr, Q)
        scores = jnp.einsum('bhqz,bhkz->bhqk', Q, K) * betas[None, :, None, None]
        attn = jax.nn.softmax(scores, axis=-1)
        T1 = jnp.einsum('bkhd,bhqk->bqd', F1, attn)
        T2 = jnp.einsum('bqhd,bhqk->bkd', F2, attn)
        return T1 + T2

    def _L0_ffn_ref(x, Wg, bg, We, be, W1, b1, W2, b2):
        import jax, jax.numpy as jnp
        import numpy as np
        D = 192
        M = 768
        G = 4
        E = 8
        KG = 2
        KE = 4
        EPS = 1e-06

        def _topk_gates(logits, k):
            top, idx = jax.lax.top_k(logits, k)
            gates = jax.nn.softmax(top, axis=-1)
            gates = jnp.where(gates >= EPS, gates, jnp.zeros_like(gates))
            return (gates, idx)
        orig_shape = x.shape
        xf = x.reshape(-1, D)
        glog = xf @ Wg + bg
        ggates, gidx = _topk_gates(glog, KG)
        gw = jnp.einsum('nk,nkg->ng', ggates, jax.nn.one_hot(gidx, G, dtype=xf.dtype))
        elog = jnp.einsum('nd,gde->nge', xf, We) + be
        egates, eidx = _topk_gates(elog, KE)
        ew = jnp.einsum('ngk,ngke->nge', egates, jax.nn.one_hot(eidx, E, dtype=xf.dtype))
        combine = gw[:, :, None] * ew
        y = jnp.zeros_like(xf)
        for g in range(G):
            h = jax.nn.gelu(jnp.einsum('nd,edm->enm', xf, W1[g]) + b1[g][:, None, :], approximate=False)
            o = jnp.einsum('enm,emd->end', h, W2[g]) + b2[g][:, None, :]
            y = y + jnp.einsum('end,ne->nd', o, combine[:, g, :])
        return y.reshape(orig_shape)
    h = _L0_tok_ref(x, L0_tok_patch_w, L0_tok_patch_b, L0_tok_ln_g, L0_tok_ln_b, L0_tok_w1, L0_tok_w2, L0_tok_w3, L0_tok_wqkv, L0_tok_bqkv, L0_tok_wo, L0_tok_bo)
    h = h + _L0_attn_ref(_layernorm(h, axis=-1), L0_attn_Wq, L0_attn_Wk, L0_attn_betas)
    h = h + _L0_ffn_ref(_layernorm(h, axis=-1), L0_ffn_Wg, L0_ffn_bg, L0_ffn_We, L0_ffn_be, L0_ffn_W1, L0_ffn_b1, L0_ffn_W2, L0_ffn_b2)
    return h

_drawn_inputs = setup_inputs


def setup_inputs(seed=0):
    import zlib

    import numpy as np

    out = dict(_drawn_inputs(seed))
    spreads = {'L0_tok_patch_b': (0.0, 0.1),
     'L0_tok_ln_g': (1.0, 0.2),
     'L0_tok_ln_b': (0.0, 0.1),
     'L0_tok_bqkv': (0.0, 0.1),
     'L0_tok_bo': (0.0, 0.1),
     'L0_attn_betas': (0.25, 0.6)}
    factors = {'L0_ffn_Wg': 3.401,
     'L0_ffn_bg': 58.101,
     'L0_ffn_We': 3.443,
     'L0_ffn_be': 64.0,
     'L0_ffn_b1': 55.055,
     'L0_ffn_b2': 8.0}
    for name, (base, spread) in spreads.items():
        noise = np.random.default_rng([zlib.crc32(name.encode()), seed]).standard_normal(out[name].shape)
        drawn = base * np.exp(spread * noise) if base else spread * noise
        out[name] = jnp.asarray(drawn.astype(out[name].dtype))
    for name, factor in factors.items():
        out[name] = (out[name] * factor).astype(out[name].dtype)
    return out
```

```python
import numpy as np
from contextlib import ExitStack

import concourse.bass as bass
from concourse import mybir

BATCH, CHANNELS, IMG, PATCH = 16, 3, 112, 16
SIDE = IMG // PATCH
SEQ = SIDE * SIDE
TOKENS = BATCH * SEQ
DIM, HEADS = 192, 12
HEAD_DIM = DIM // HEADS
HIDDEN = 4 * DIM
GROUPS, EXPERTS, TOP_G, TOP_E = 4, 8, 2, 4
ALL_E = GROUPS * EXPERTS
PICKS = TOP_G * TOP_E
LN_EPS, GATE_EPS = 1e-5, 1e-6

KC = 2
DC = DIM // KC
HC = HEADS // KC
NP = 2
TC = NP * SEQ
NC = TOKENS // TC
LANE = 64
SPAN = LANE + SEQ
MC = HIDDEN // 128
HALF = TOKENS // 2
ROWS = BATCH * SIDE
QC = CHANNELS * 2

SLOTS = 128
TILES = (TOKENS * PICKS - ALL_E) // SLOTS + ALL_E
RING = 4
TABLE = TILES + RING
MAX_STEPS = -(-TOKENS // SLOTS)
LIST_W = 8
assert TILES % RING == 0

FIELDS = dict(ident=128, sin=KC * SEQ, earlier=TC, headmask=HC, causal=SEQ, slot=SLOTS,
              token=NC * 3, tie_e=EXPERTS * EXPERTS, tie_g=GROUPS * GROUPS, steps=MAX_STEPS,
              tile=1, spare=2, picked=NC, first=TABLE, eps=1, ones=128)
AT, _at = {}, 0
for _name, _width in FIELDS.items():
    AT[_name] = (_at, _at + _width)
    _at += _width
CONST_W = _at

def constants():
    c = np.zeros((128, CONST_W), np.float32)

    def put(name, value):
        value = np.asarray(value, np.float32)
        value = value.reshape(value.shape[0], -1)
        a, _ = AT[name]
        c[:value.shape[0], a:a + value.shape[1]] = value

    put("ident", np.eye(128))
    scales = np.linspace(1.0, 5.0, DIM // 4)
    seq = np.linspace(-1.0, 1.0, SIDE)[:, None] * scales[None, :] * np.pi
    a = np.broadcast_to(seq[:, None, :], (SIDE, SIDE, DIM // 4))
    b = np.broadcast_to(seq[None, :, :], (SIDE, SIDE, DIM // 4))
    table = np.repeat(np.concatenate([np.sin(a), np.sin(b)], -1).reshape(SEQ, DIM // 2), 2, axis=-1)
    sin = np.zeros((DC + 1, KC, SEQ))
    sin[:DC] = table.T.reshape(KC, DC, SEQ).transpose(1, 0, 2)
    sin[DC, KC - 1] = 1.0
    put("sin", sin)
    t = np.arange(TC)
    put("earlier", t[:, None] < t[None, :])
    put("headmask", np.arange(DC)[:, None] // HEAD_DIM == np.arange(HC)[None, :])
    s = np.arange(SEQ)
    put("causal", np.where(s[:, None] >= s[None, :], 0.0, -1e30))
    put("slot", np.broadcast_to(np.arange(SLOTS), (128, SLOTS)))
    token = np.zeros((TC, NC, 3))
    token[:, :, 0] = t[:, None]
    token[:, :, 1] = np.arange(NC)[None, :]
    token[:, :, 2] = 1.0
    put("token", token)
    e, g = np.arange(EXPERTS), np.arange(GROUPS)
    put("tie_e", np.broadcast_to((e[None, :] < e[:, None]).ravel(), (128, EXPERTS ** 2)))
    put("tie_g", np.broadcast_to((g[None, :] < g[:, None]).ravel(), (128, GROUPS ** 2)))
    put("steps", np.broadcast_to(SLOTS * np.arange(MAX_STEPS), (128, MAX_STEPS)))
    put("tile", np.arange(128)[:, None])
    put("spare", PICKS * TOKENS + np.arange(128)[:, None] + SLOTS * np.arange(2)[None, :])
    put("picked", np.broadcast_to(PICKS * np.arange(NC), (128, NC)))
    put("first", np.broadcast_to(SLOTS * np.arange(TABLE), (128, TABLE)))
    put("eps", np.full((128, 1), LN_EPS))
    put("ones", np.ones((128, 128)))
    return c

def vit_moe_program(nc, x, patch_w, patch_b, ln_g, ln_b, w1, w2, w3, wqkv, bqkv, wo, bo,
                    attn_wq, attn_wk, betas, wg, bg, we, be, ew1, eb1, ew2, eb2, consts, out):
    F32, BF16, I32 = mybir.dt.float32, mybir.dt.bfloat16, mybir.dt.int32
    ALU, ACT, X = mybir.AluOpType, mybir.ActivationFunctionType, mybir.AxisListType.X

    with ExitStack() as ctx:
        def sb(name, shape, dt=F32):
            return ctx.enter_context(nc.sbuf_tensor(name, shape, dt))

        def sem(name):
            return ctx.enter_context(nc.semaphore(name))

        early = ExitStack()

        def sb_early(name, shape, dt=F32):
            return early.enter_context(nc.sbuf_tensor(name, shape, dt))

        front = ExitStack()

        def sb_front(name, shape, dt=F32):
            return front.enter_context(nc.sbuf_tensor(name, shape, dt))

        xn_dram = nc.dram_tensor("xn_dram", [TOKENS, DIM], F32, kind="Internal").ap()
        picks_dram = nc.dram_tensor("picks_dram", [PICKS * TOKENS + 2 * SLOTS, DIM], F32, kind="Internal").ap()

        cst = sb("cst", [128, CONST_W])
        wqk_sb = sb("wqk_sb", [DC, 2, KC, DIM])
        wqk_t = sb("wqk_t", [DC, 2, KC, DIM])
        beta_bc = sb("beta_bc", [DC, HEADS])
        beta_mask = sb("beta_mask", [DC, KC, HC])
        wr_sb = sb("wr_sb", [DC, KC, GROUPS + ALL_E])
        rb_sb = sb("rb_sb", [TC, GROUPS + ALL_E])
        b2_sb = sb("b2_sb", [ALL_E, DIM])
        h = sb("h", [TC, NC, DIM])
        hn = sb("hn", [TC, NC, DIM])
        xt = sb("xt", [DC + 1, 2, KC, SLOTS])
        stats = sb("stats", [TC, NC, 6])
        mv = sb("mv", [TC, NC, 2])
        std = sb("std", [TC, NC])
        rstd = sb("rstd", [TC, NC])
        hn_t = sb("hn_t", [DC, KC, TOKENS])
        patch_w_sb = sb_early("patch_w_sb", [128, CHANNELS, 2, DIM])
        w1_sb = sb_early("w1_sb", [DC, KC, HIDDEN])
        w3_sb = sb_early("w3_sb", [DC, KC, HIDDEN])
        w2_sb = sb_early("w2_sb", [128, MC, DIM])
        ln_gb = sb_early("ln_gb", [DC, 2, KC])
        base = sb_early("base", [TC, DIM])
        patch_t = sb_early("patch_t", [128, QC, TOKENS])
        silu_sb = sb_early("silu_sb", [128, 2, HALF])
        u_t = sb_early("u_t", [128, MC, TOKENS])
        spread_t = sb_early("spread_t", [DC, KC, NC, 128])
        q_t = sb_early("q_t", [DC, KC, NC, 128])
        k_t = sb_early("k_t", [DC, KC, NC, 128])
        pixels = sb_front("pixels", [ROWS, CHANNELS, PATCH * IMG])
        patches = sb_front("patches", [ROWS, CHANNELS, SIDE, PATCH, PATCH])
        wqkv_sb = sb_front("wqkv_sb", [DC + 1, KC, DIM + 2 * HEAD_DIM])
        wkv_rep = sb_front("wkv_rep", [DC + 1, KC, 2, HC, HEAD_DIM])
        wo_sb = sb_front("wo_sb", [DC, KC, DIM])
        row_bias = sb_front("row_bias", [2, DIM])
        pos_qt = sb_front("pos_qt", [DC, KC, SEQ])
        pos_kexp = sb_front("pos_kexp", [DC, HC, SEQ])
        pos_v = sb_front("pos_v", [SEQ, DC])
        pos_e = sb_front("pos_e", [SEQ, HEADS, SEQ])
        pos_max = sb_front("pos_max", [SEQ, 2, HEADS])
        pos_et = sb_front("pos_et", [SEQ, KC, HC * SEQ])
        pos_f = sb_front("pos_f", [DC, KC, HC, SEQ])
        pos_ot = sb_front("pos_ot", [DC, KC, SEQ])
        pos_ot2 = sb_front("pos_ot2", [DC, KC, NP, SEQ])
        front.close()
        q_n = sb_early("q_n", [SPAN, NC, DIM])
        k_n = sb_early("k_n", [SEQ, NC, NP, DIM])
        k_exp = sb_early("k_exp", [DC, 2, KC, NP, HC, SEQ])
        e_sb = sb_early("e_sb", [SPAN, 2, KC, HC, SEQ])
        e_max = sb_early("e_max", [SPAN, HEADS])
        e_rz = sb_early("e_rz", [SPAN, 2, HEADS])
        e_t = sb_early("e_t", [SEQ, 3, 4, SPAN])
        f_sb = sb_early("f_sb", [DC, 2, KC, HC, SEQ])
        vu_t = sb_early("vu_t", [DC, 2, 2, KC, NP, SEQ])
        early.close()
        logit_g = sb("logit_g", [TC, NC, GROUPS])
        logit_e = sb("logit_e", [TC, NC, GROUPS, EXPERTS])
        cmp_a = sb("cmp_a", [TC, NC * GROUPS, EXPERTS, EXPERTS])
        cmp_b = sb("cmp_b", [TC, NC * GROUPS, EXPERTS, EXPERTS])
        sel_g = sb("sel_g", [TC, NC, GROUPS])
        rank_e = sb("rank_e", [TC, NC, GROUPS, EXPERTS])
        rank_g = sb("rank_g", [TC, NC, GROUPS])
        red_e = sb("red_e", [TC, NC, GROUPS])
        red_g = sb("red_g", [TC, NC])
        gate_e = sb("gate_e", [TC, NC, GROUPS, EXPERTS])
        gate_g = sb("gate_g", [TC, NC, GROUPS])
        gate_tmp = sb("gate_tmp", [TC, NC, GROUPS, EXPERTS])
        sel = sb("sel", [TC, NC, GROUPS, EXPERTS])
        sel_bf = sb("sel_bf", [TC, NC, ALL_E], BF16)
        comb = sb("comb", [TC, NC, GROUPS, EXPERTS])
        comb_t = sb("comb_t", [ALL_E, TOKENS])
        zeros = sb("zeros", [TC, NC * ALL_E])
        order = sb("order", [TC, NC, ALL_E])
        earlier_bf = sb("earlier_bf", [TC, TC], BF16)
        ones_bf = sb("ones_bf", [TC, TC], BF16)
        tile_cmp = sb("tile_cmp", [TC, ALL_E, MAX_STEPS])
        tiles_of = sb("tiles_of", [TC, ALL_E])
        tiles_end = sb("tiles_end", [TC, ALL_E])
        first_slot = sb("first_slot", [TC, ALL_E])
        slot_of = sb("slot_of", [TC, ALL_E, NC])
        slot_tmp = sb("slot_tmp", [TC, NC, ALL_E])
        list_src = sb("list_src", [TC, ALL_E, NC, LIST_W], BF16)
        owner_cmp = sb("owner_cmp", [TABLE, ALL_E])
        owner = sb("owner", [TABLE, 1])
        table = sb("table", [1, TABLE + 1], I32)
        slot_rel = sb("slot_rel", [TC, NC])
        place = sb("place", [TC, 2, NC, SLOTS], BF16)
        list_col = sb("list_col", [TC, 2, NC, LIST_W], BF16)
        list_sb = sb("list_sb", [SLOTS, 2, LIST_W])
        fetch_f = sb("fetch_f", [SLOTS, 2])
        fetch = sb("fetch", [SLOTS, 2], I32)
        store_f = sb("store_f", [SLOTS, 2, 2])
        store = sb("store", [SLOTS, RING], I32)
        gate = sb("gate", [SLOTS, RING])
        xg = sb("xg", [SLOTS, 2, DIM])
        ew1_sb = sb("ew1_sb", [DC + 1, 2, KC, HIDDEN])
        ew2_sb = sb("ew2_sb", [128, 2, MC, DIM])
        ht = sb("ht", [128, 2, MC, SLOTS])
        o_sb = sb("o_sb", [SLOTS, 2, DIM])
        picks = sb("picks", [TC, NC, PICKS, DIM])
        total = sb("total", [TC, NC, DIM])

        ps = ctx.enter_context(nc.psum_tensor("ps", [128, 8, 512], F32))

        def c(name, parts=128):
            a, b = AT[name]
            return cst[0:parts, a:b]

        ident = c("ident")
        headmask = c("headmask", DC)

        ld_const, ld_qkv, ld_pixels, ld_patch_w, ld_wo = (sem(n) for n in (
            "ld_const", "ld_qkv", "ld_pixels", "ld_patch_w", "ld_wo"))
        ld_ln, ld_w13, ld_w2, ld_wqk, ld_beta, ld_router, ld_b2 = (sem(n) for n in (
            "ld_ln", "ld_w13", "ld_w2", "ld_wqk", "ld_beta", "ld_router", "ld_b2"))
        var_ready, std_ready = sem("var_ready"), sem("std_ready")
        dve_chain, small_chain, pool_chain = sem("dve_chain"), sem("small_chain"), sem("pool_chain")
        rep_ready, pos_proj, pos_in, pos_s, pos_sub, pos_exp, pos_norm = (sem(n) for n in (
            "rep_ready", "pos_proj", "pos_in", "pos_s", "pos_sub", "pos_exp", "pos_norm"))
        pos_tr, pos_et_ready, pos_f_done, pos_o_ready, base_done, base_ready = (sem(n) for n in (
            "pos_tr", "pos_et_ready", "pos_f_done", "pos_o_ready", "base_done", "base_ready"))
        cut_ready = [sem(f"cut_ready{ch}") for ch in range(CHANNELS)]
        px_done, px_ready, tok_done, h_ready, hn_ready, hnt_done, hnt_ready = (sem(n) for n in (
            "px_done", "px_ready", "tok_done", "h_ready", "hn_ready", "hnt_done", "hnt_ready"))
        up_done, silu_ready, u_ready, down_done, h2_ready = (sem(n) for n in (
            "up_done", "silu_ready", "u_ready", "down_done", "h2_ready"))
        wt_done, wt_ready, hn2_ready, sp_done, sp_ready, sp_zero, proj_done, proj_ready = (sem(n) for n in (
            "wt_done", "wt_ready", "hn2_ready", "sp_done", "sp_ready", "sp_zero", "proj_done", "proj_ready"))
        nat_done, nat_ready, bm_ready, kexp_ready, s_done, sub_ready, exp_ready, norm_ready = (sem(n) for n in (
            "nat_done", "nat_ready", "bm_ready", "kexp_ready", "s_done", "sub_ready", "exp_ready", "norm_ready"))
        et_done, et_ready, f_done, f_ready, vu_ready, t_done, h3_ready = (sem(n) for n in (
            "et_done", "et_ready", "f_done", "f_ready", "vu_ready", "t_done", "h3_ready"))
        xn_ready, xn_stored, xnt_done, xnt_ready, logit_done, logit_ready, gexp_ready = (sem(n) for n in (
            "xn_ready", "xn_stored", "xnt_done", "xnt_ready", "logit_done", "logit_ready", "gexp_ready"))
        sel_ready, rank_done, comb_ready, combt_done, combt_ready, owner_ready, owner_done, table_ready = (
            sem(n) for n in ("sel_ready", "rank_done", "comb_ready", "combt_done", "combt_ready",
                             "owner_ready", "owner_done", "table_ready"))
        place_ready, list_done, fetch_ready, meta_ready, xt_done, xt_ready = (sem(n) for n in (
            "place_ready", "list_done", "fetch_ready", "meta_ready", "xt_done", "xt_ready"))
        xg_ready = [sem(f"xg_ready{u}") for u in range(2)]
        ew1_ready = [sem(f"ew1_ready{u}") for u in range(2)]
        ew2_ready = [sem(f"ew2_ready{u}") for u in range(2)]
        o_free = [sem(f"o_free{u}") for u in range(2)]
        tiles_over, pool_turns = sem("tiles_over"), sem("pool_turns")
        mm1_done, ht_ready, mm2_done, o_ready = (sem(n) for n in ("mm1_done", "ht_ready", "mm2_done", "o_ready"))
        b2_done, total_ready, picks_ready, out_ready, stored = (sem(n) for n in (
            "b2_done", "total_ready", "picks_ready", "out_ready", "stored"))

        def cut(copy, ch):
            return copy(patches[:, ch].rearrange("p j r w -> p r j w"),
                        pixels[:, ch].rearrange("p (r j w) -> p r j w", r=PATCH, w=PATCH)).then_inc(cut_ready[ch], 1)

        def ring_pos(j, off, n):
            return (j + off) % n

        block = ctx.enter_context(nc.Block())

        @block.sync
        def _(sp):
            sp.dma_start(cst[:], consts).then_inc(ld_const, 16)
            sp.dma_start(wqkv_sb[0:DC], wqkv.rearrange("(k p) n -> p k n", p=DC)).then_inc(ld_qkv, 16)
            sp.dma_start(wqkv_sb[DC:DC + 1, KC - 1, :], bqkv.rearrange("(a n) -> a n", a=1)).then_inc(ld_qkv, 16)
            for b in range(BATCH):
                sp.dma_start(pixels[b * SIDE:(b + 1) * SIDE],
                             x[b].rearrange("c (i r) w -> i c (r w)", r=PATCH)).then_inc(ld_pixels, 16)
            sp.dma_start(wo_sb[:], wo.rearrange("(k p) n -> p k n", p=DC)).then_inc(ld_wo, 16)
            sp.dma_start(row_bias[0:1], bo.rearrange("(a n) -> a n", a=1)).then_inc(ld_wo, 16)
            sp.dma_start(row_bias[1:2], patch_b.rearrange("(a n) -> a n", a=1)).then_inc(ld_wo, 16)
            patch_view = patch_w.rearrange("(f p c) n -> c f p n", f=2, c=CHANNELS)
            for ch in range(CHANNELS):
                sp.dma_start(patch_w_sb[:, ch], patch_view[ch].rearrange("f p n -> p f n")).then_inc(ld_patch_w, 16)
            sp.dma_start(ln_gb[:, 0, :], ln_g.rearrange("(k p) -> p k", p=DC), allow_slow_non_contiguous=True).then_inc(ld_ln, 16)
            sp.dma_start(ln_gb[:, 1, :], ln_b.rearrange("(k p) -> p k", p=DC), allow_slow_non_contiguous=True).then_inc(ld_ln, 16)
            sp.dma_start(w1_sb[:], w1.rearrange("(k p) n -> p k n", p=DC)).then_inc(ld_w13, 16)
            sp.dma_start(w3_sb[:], w3.rearrange("(k p) n -> p k n", p=DC)).then_inc(ld_w13, 16)
            sp.dma_start(wqk_sb[:, 0], attn_wq.rearrange("(k p) n -> p k n", p=DC)).then_inc(ld_wqk, 16)
            sp.dma_start(wqk_sb[:, 1], attn_wk.rearrange("(k p) n -> p k n", p=DC)).then_inc(ld_wqk, 16)
            sp.dma_start(w2_sb[:], w2.rearrange("(k p) n -> p k n", p=128)).then_inc(ld_w2, 16)
            sp.dma_start(beta_bc[:], betas.partition_broadcast(DC)).then_inc(ld_beta, 16)
            sp.dma_start(wr_sb[:, :, 0:GROUPS], wg.rearrange("(k p) n -> p k n", p=DC)).then_inc(ld_router, 16)
            for k in range(KC):
                sp.dma_start(wr_sb[:, k, GROUPS:].rearrange("p (g e) -> p g e", g=GROUPS),
                             we[:, k * DC:(k + 1) * DC, :].rearrange("g p e -> p g e")).then_inc(ld_router, 16)
            sp.dma_start(rb_sb[:, 0:GROUPS], bg.partition_broadcast(TC)).then_inc(ld_router, 16)
            sp.dma_start(rb_sb[:, GROUPS:], be.rearrange("g e -> (g e)").partition_broadcast(TC)).then_inc(ld_router, 16)
            sp.dma_start(b2_sb[:], eb2.rearrange("g e n -> (g e) n")).then_inc(ld_b2, 16)

            for g in range(NC):
                sp.wait_ge(xn_ready, g + 1)
                sp.dma_start(xn_dram[g * TC:(g + 1) * TC, :], hn[:, g, :]).then_inc(xn_stored, 16)

            ew1_v = ew1.rearrange("g e (k p) m -> (g e) p k m", p=DC)
            eb1_v = eb1.rearrange("g e m -> (g e) m")
            ew2_v = ew2.rearrange("g e (k p) n -> (g e) p k n", p=128)

            def load_w1(tile, u, *wait):
                e = sp.value_load(table[0:1, bass.ds(tile, 1)], min_val=0, max_val=ALL_E - 1)
                if wait:
                    sp.wait_ge(*wait)
                sp.dma_start(ew1_sb[0:DC, u], ew1_v[bass.ds(e, 1)].rearrange("a p k m -> p (a k) m")).then_inc(ew1_ready[u], 16)
                sp.dma_start(ew1_sb[DC:DC + 1, u, KC - 1, :], eb1_v[bass.ds(e, 1), :]).then_inc(ew1_ready[u], 16)

            def load_w2(tile, u, *wait):
                e = sp.value_load(table[0:1, bass.ds(tile, 1)], min_val=0, max_val=ALL_E - 1)
                if wait:
                    sp.wait_ge(*wait)
                sp.dma_start(ew2_sb[:, u], ew2_v[bass.ds(e, 1)].rearrange("a p k n -> p (a k) n")).then_inc(ew2_ready[u], 16)

            sp.wait_ge(table_ready, 1)
            load_w1(0, 0)
            load_w1(1, 1)
            load_w2(0, 0)
            load_w2(1, 1)
            sp.wait_ge(mm1_done, 2)
            load_w1(2, 0)
            n = sp.value_load(table[0:1, TABLE:TABLE + 1], min_val=0, max_val=TILES)
            after_even, after_others, after_ew2 = (sp.alloc_register(a) for a in ("after_even", "after_others", "after_ew2"))
            sp.reg_alu(after_ew2, n + 1, 1, ALU.logical_shift_right)
            sp.reg_alu(after_ew2, after_ew2, 16, ALU.mult)
            sp.reg_alu(after_ew2, after_ew2, 16, ALU.add)
            sp.reg_alu(after_others, after_ew2, after_ew2, ALU.add)
            sp.reg_alu(after_even, after_others, 32, ALU.add)
            with sp.Fori(0, TILES // RING) as q:
                for half in range(2):
                    with sp.If(q * RING + 2 * half < n):
                        for j in (2 * half, 2 * half + 1):
                            t = q * RING + j
                            load_w1(t + 3, ring_pos(j, 3, 2), mm1_done, t * 2 + 4)
                            load_w2(t + 2, ring_pos(j, 2, 2), mm2_done, t + 1)
            sp.wait_ge(ew1_ready[0], after_even)
            sp.wait_ge(ew1_ready[1], after_others)
            for u in range(2):
                sp.wait_ge(ew2_ready[u], after_ew2)
                sp.wait_ge(o_free[u], after_ew2)
            for g in range(NC):
                sp.dma_start(picks[:, g], picks_dram[0:PICKS * TOKENS, :].rearrange(
                    "(k t) d -> t k d", k=PICKS)[g * TC:(g + 1) * TC]).then_inc(picks_ready, 16)
            out_v = out.rearrange("b s d -> (b s) d")
            for g in range(NC):
                sp.wait_ge(out_ready, g + 1)
                sp.dma_start(out_v[g * TC:(g + 1) * TC, :], total[:, g, :]).then_inc(stored, 16)
            sp.wait_ge(stored, 16 * NC)

        @block.tensor
        def _(pe):
            def mm(o, lhs, rhs, start=True, stop=True):
                return pe.matmul(o, lhs, rhs, start=start, stop=stop)

            pe.wait_ge(ld_const, 16)
            pe.wait_ge(ld_qkv, 32)
            pe.wait_ge(rep_ready, 3)
            sin = c("sin", DC + 1).rearrange("p (k s) -> p k s", k=KC)
            for m in range(KC):
                for k in range(KC):
                    mm(ps[0:DC, 0, m * SEQ:(m + 1) * SEQ], wqkv_sb[:, k, m * DC:(m + 1) * DC], sin[:, k], k == 0, k == 1)
            for k in range(KC):
                mm(ps[0:DC, 0, 2 * SEQ:3 * SEQ], wkv_rep[:, k, 0].rearrange("p h d -> p (h d)"), sin[:, k], k == 0, k == 1)
            for k in range(KC):
                last = mm(ps[0:SEQ, 1, 0:DC], sin[:, k], wkv_rep[:, k, 1].rearrange("p h d -> p (h d)"), k == 0, k == 1)
            last.then_inc(pos_proj, 1)
            pe.wait_ge(pos_in, 3)
            for m in range(KC):
                last = mm(ps[0:SEQ, 2 + m, 0:HC * SEQ], pos_qt[:, m], pos_kexp[:].rearrange("p h s -> p (h s)"))
            last.then_inc(pos_s, 1)

            def pixel_unit(n):
                q, r = divmod(n, 2)
                ch, f = divmod(q, 2)
                pe.wait_ge(cut_ready[ch], 1)
                if n >= 4:
                    pe.wait_ge(px_ready, n - 3)
                js = range(0, 4) if r == 0 else range(4, SIDE)
                for a, jj in enumerate(js):
                    last = pe.transpose(ps[:, 4 + n % 4, a * ROWS:(a + 1) * ROWS],
                                        patches[:, ch, jj, f * 8:f * 8 + 8].rearrange("p r w -> p (r w)"), ident[0:ROWS, 0:ROWS])
                last.then_inc(px_done, 1)

            for n in range(6):
                pixel_unit(n)
            pe.wait_ge(pos_norm, 1)
            for hd in range(HEADS):
                m, a = divmod(hd, HC)
                last = pe.transpose(ps[0:SEQ, m, a * SEQ:(a + 1) * SEQ], pos_e[:, hd, :], ident[0:SEQ, 0:SEQ])
            last.then_inc(pos_tr, 1)
            for n in range(6, 9):
                pixel_unit(n)
            pe.wait_ge(pos_et_ready, 1)
            for m in range(KC):
                last = mm(ps[0:DC, 2 + m, 0:HC * SEQ], pos_v[:], pos_et[:, m])
            last.then_inc(pos_f_done, 1)
            for n in range(9, 12):
                pixel_unit(n)
            pe.wait_ge(pos_o_ready, 1)
            pe.wait_ge(ld_wo, 48)
            for m in range(KC):
                mm(ps[0:TC, 0, 0:DIM], pos_ot2[:, m].rearrange("p a s -> p (a s)"), wo_sb[:, m], m == 0, False)
            mm(ps[0:TC, 0, 0:DIM], c("ones", 2)[:, 0:TC], row_bias[:], False, True).then_inc(base_done, 1)

            pe.wait_ge(ld_patch_w, 48)
            pe.wait_ge(px_ready, 12)
            for g in range(NC):
                if g >= 4:
                    pe.wait_ge(h_ready, g - 3)
                for q in range(QC):
                    last = mm(ps[0:TC, 4 + g % 4, 0:DIM], patch_t[:, q, g * TC:(g + 1) * TC],
                              patch_w_sb[:, q // 2, q % 2, :], q == 0, q == QC - 1)
                last.then_inc(tok_done, 1)
            pe.wait_ge(ld_wqk, 32)
            pe.wait_ge(base_ready, 1)
            for w in range(2):
                for m in range(KC):
                    for k in range(KC):
                        last = pe.transpose(ps[0:DC, w, (k * KC + m) * DC:(k * KC + m + 1) * DC],
                                            wqk_sb[:, w, m, k * DC:(k + 1) * DC], ident[0:DC, 0:DC])
            last.then_inc(wt_done, 1)
            pe.wait_ge(wt_ready, 2)
            for g in range(NC):
                pe.wait_ge(hn_ready, g + 1)
                for k in range(KC):
                    last = pe.transpose(ps[0:DC, k + 2 * (g // 4), (g % 4) * TC:(g % 4 + 1) * TC],
                                        hn[:, g, k * DC:(k + 1) * DC], ident[0:TC, 0:TC])
                last.then_inc(hnt_done, 1)
            pe.wait_ge(ld_w13, 32)
            pe.wait_ge(h_ready, NC)
            for n in range(2 * MC):
                hf, m = divmod(n, MC)
                pe.wait_ge(hnt_ready, 2 * hf + 2)
                if n >= 2:
                    pe.wait_ge(u_ready, n - 1)
                for a, w in enumerate((w1_sb, w3_sb)):
                    for k in range(KC):
                        last = mm(ps[:, 4 + 2 * (n % 2) + a, 0:HALF], w[:, k, m * 128:(m + 1) * 128],
                                  hn_t[:, k, hf * HALF:(hf + 1) * HALF], k == 0, k == 1)
                    last.then_inc(up_done, 1)
            pe.wait_ge(ld_w2, 16)
            pe.wait_ge(hnt_ready, 4)
            for g in range(NC):
                if g >= 4:
                    pe.wait_ge(h2_ready, g - 3)
                pe.wait_ge(u_ready, MC if g < 4 else 2 * MC)
                for m in range(MC):
                    last = mm(ps[0:TC, g % 4, 0:DIM], u_t[:, m, g * TC:(g + 1) * TC], w2_sb[:, m], m == 0, m == MC - 1)
                last.then_inc(down_done, 1)

            for g in range(NC):
                pe.wait_ge(hn2_ready, g + 1)
                if g >= 4:
                    pe.wait_ge(sp_ready, g - 3)
                for k in range(KC):
                    last = pe.transpose(ps[0:DC, 4 + g % 4, k * TC:(k + 1) * TC],
                                        hn[:, g, k * DC:(k + 1) * DC], ident[0:TC, 0:TC])
                last.then_inc(sp_done, 1)
            pe.wait_ge(h2_ready, NC)
            for n in range(8):
                hf, w, m = n // 4, (n // 2) % 2, n % 2
                pe.wait_ge(sp_ready, 4 * hf + 4)
                if n >= 4:
                    pe.wait_ge(proj_ready, n - 3)
                for k in range(KC):
                    last = mm(ps[0:DC, n % 4, 0:4 * SPAN], wqk_t[:, w, k, m * DC:(m + 1) * DC],
                              spread_t[:, k, 4 * hf:4 * hf + 4, 0:SPAN], k == 0, k == 1)
                last.then_inc(proj_done, 1)
            pe.wait_ge(proj_ready, 8)
            pe.wait_ge(sp_ready, NC)
            for g in range(NC):
                if g >= 2:
                    pe.wait_ge(nat_ready, 2 * g - 2)
                for m in range(KC):
                    last = pe.transpose(ps[0:SPAN, 4 + 2 * (g % 2), m * DC:(m + 1) * DC], q_t[:, m, g, 0:SPAN], ident[0:DC, 0:DC])
                for u in range(NP):
                    for m in range(KC):
                        last = pe.transpose(ps[0:SEQ, 5 + 2 * (g % 2), u * DIM + m * DC:u * DIM + (m + 1) * DC],
                                            k_t[:, m, g, u * LANE:u * LANE + SEQ], ident[0:DC, 0:DC])
                last.then_inc(nat_done, 1)

            def scores(g):
                pe.wait_ge(kexp_ready, g + 1)
                if g >= 1:
                    pe.wait_ge(sub_ready, g)
                for m in range(KC):
                    for u in range(NP):
                        rows = LANE if u == 0 else SEQ
                        last = mm(ps[u * LANE:u * LANE + rows, m, 0:HC * SEQ], q_t[:, m, g, u * LANE:u * LANE + rows],
                                  k_exp[:, g % 2, m, u].rearrange("p h s -> p (h s)"))
                last.then_inc(s_done, 1)

            scores(0)
            pe.wait_ge(nat_ready, 2 * NC)
            for g in range(NC):
                if g + 1 < NC:
                    scores(g + 1)
                pe.wait_ge(norm_ready, g + 1)
                for s in range(3):
                    r = 4 * g + s
                    if r >= 2:
                        if s == 0:
                            pe.wait_ge(et_ready, 3 * g)
                        elif s == 1:
                            if g >= 1:
                                pe.wait_ge(h3_ready, g)
                        else:
                            pe.wait_ge(et_ready, 3 * g + 1)
                    for a in range(4):
                        m, hd = divmod(4 * s + a, HC)
                        last = pe.transpose(ps[0:SEQ, 2 + r % 2, a * SPAN:(a + 1) * SPAN], e_sb[:, g % 2, m, hd, :],
                                            ident[0:SPAN, 0:SPAN])
                    last.then_inc(et_done, 1)
                for w in range(4):
                    kind, u = divmod(w, NP)
                    n = 4 * g + w
                    if n >= 2:
                        pe.wait_ge(f_ready, n - 1)
                    if kind == 0:
                        pe.wait_ge(et_ready, 3 * g + 3)
                    for m in range(KC):
                        bank = 4 + 2 * (n % 2) + m
                        if kind == 0:
                            rhs = e_t[:].rearrange("p s a q -> p (s a) q")[:, m * HC:(m + 1) * HC, u * LANE:u * LANE + SEQ]
                            last = mm(ps[0:DC, bank, 0:HC * SEQ], k_n[:, g, u, m * DC:(m + 1) * DC], rhs)
                        else:
                            p0 = u * LANE
                            last = mm(ps[0:DC, bank, 0:HC * SEQ], q_n[p0:p0 + SEQ, g, m * DC:(m + 1) * DC],
                                      e_sb[p0:p0 + SEQ, g % 2, m].rearrange("p h s -> p (h s)"))
                    last.then_inc(f_done, 1)
                pe.wait_ge(vu_ready, 4 * g + 4)
                pe.wait_ge(et_ready, 3 * g + 2)
                for i, (kind, m) in enumerate(((0, 0), (0, 1), (1, 0), (1, 1))):
                    last = mm(ps[0:TC, 3, 0:DIM], vu_t[:, g % 2, kind, m].rearrange("p a s -> p (a s)"),
                              wqk_sb[:, kind, m], i == 0, i == 3)
                last.then_inc(t_done, 1)

            pe.wait_ge(f_ready, 4 * NC)
            for g in range(NC):
                pe.wait_ge(xn_ready, g + 1)
                if g >= 4:
                    pe.wait_ge(xnt_ready, g - 3)
                for k in range(KC):
                    last = pe.transpose(ps[0:DC, 4 + g % 4, k * TC:(k + 1) * TC],
                                        hn[:, g, k * DC:(k + 1) * DC], ident[0:TC, 0:TC])
                last.then_inc(xnt_done, 1)
            pe.wait_ge(ld_router, 80)
            RW = GROUPS + ALL_E
            for g in range(NC):
                pe.wait_ge(xnt_ready, g + 1)
                for k in range(KC):
                    last = mm(ps[0:TC, 0, g * RW:(g + 1) * RW], hn_t[:, k, g * TC:(g + 1) * TC], wr_sb[:, k], k == 0, k == 1)
            last.then_inc(logit_done, 1)
            pe.wait_ge(sel_ready, 1)
            for g in range(NC):
                for b in range(g + 1):
                    mm(ps[0:TC, 1, g * ALL_E:(g + 1) * ALL_E], (earlier_bf if b == g else ones_bf)[:], sel_bf[:, b], b == 0, b == g)
            for b in range(NC):
                last = mm(ps[0:TC, 1, NC * ALL_E:(NC + 1) * ALL_E], ones_bf[:], sel_bf[:, b], b == 0, b == NC - 1)
            last.then_inc(rank_done, 1)
            pe.wait_ge(owner_ready, 1)
            mm(ps[0:1, 2, 0:TABLE], owner[:], ident[0:TABLE, 0:TABLE]).then_inc(owner_done, 1)

            def make_list(tile_no, u):
                pe.wait_ge(place_ready, tile_no + 1)
                for b in range(NC):
                    last = mm(ps[:, 4 + u, 0:LIST_W], place[:, u, b], list_col[:, u, b], b == 0, b == NC - 1)
                last.then_inc(list_done, 1)

            def turn(u):
                for k in range(KC):
                    last = pe.transpose(ps[0:DC, 4 + u, k * SLOTS:(k + 1) * SLOTS], xg[:, u, k * DC:(k + 1) * DC], ident)
                last.then_inc(xt_done, 1)

            def up(u):
                for m in range(MC):
                    o = ps[:, 2 * u + m // 4, (m % 4) * SLOTS:(m % 4 + 1) * SLOTS]
                    mm(o, ew1_sb[0:DC, u, 0, m * 128:(m + 1) * 128], xt[0:DC, u, 0], True, False)
                    last = mm(o, ew1_sb[:, u, 1, m * 128:(m + 1) * 128], xt[:, u, 1], False, True)
                    if m in (3, MC - 1):
                        last.then_inc(mm1_done, 1)

            def down(u):
                for m in range(MC):
                    last = mm(ps[:, 6 + u, 0:DIM], ht[:, u, m], ew2_sb[:, u, m], m == 0, m == MC - 1)
                last.then_inc(mm2_done, 1)

            make_list(0, 0)
            make_list(1, 1)
            pe.wait_ge(fetch_ready, 1)
            pe.wait_ge(xg_ready[0], 16)
            turn(0)
            pe.wait_ge(xt_ready, 1)
            make_list(2, 0)
            pe.wait_ge(fetch_ready, 2)
            pe.wait_ge(xg_ready[1], 16)
            turn(1)
            pe.wait_ge(ew1_ready[0], 32)
            up(0)
            n = pe.value_load(table[0:1, TABLE:TABLE + 1], min_val=0, max_val=TILES)
            with pe.Fori(0, TILES // RING) as q:
                for half in range(2):
                    with pe.If(q * RING + 2 * half < n):
                        for j in (2 * half, 2 * half + 1):
                            t = q * RING + j
                            pe.wait_ge(xt_ready, t + 2)
                            make_list(t + 3, ring_pos(j, 3, 2))
                            pe.wait_ge(fetch_ready, t + 3)
                            pe.wait_ge(xg_ready[ring_pos(j, 2, 2)], q * 32 + 16 * ((j + 2) // 2 + 1))
                            turn(ring_pos(j, 2, 2))
                            u = ring_pos(j, 1, 2)
                            pe.wait_ge(ew1_ready[u], q * 64 + 32 * ((j + 1) // 2 + 1))
                            up(u)
                            u = ring_pos(j, 0, 2)
                            pe.wait_ge(ht_ready, t * 2 + 2)
                            pe.wait_ge(ew2_ready[u], q * 32 + 16 * (j // 2 + 1))
                            pe.wait_ge(o_ready, t + 1)
                            down(u)
            pe.wait_ge(comb_ready, 1)
            pe.wait_ge(tiles_over, 2)
            for g in range(NC):
                last = pe.transpose(ps[0:ALL_E, 4 + g // 4, (g % 4) * TC:(g % 4 + 1) * TC],
                                    comb[:, g].rearrange("p g e -> p (g e)"), ident[0:TC, 0:TC])
            last.then_inc(combt_done, 1)
            pe.wait_ge(combt_ready, 2)
            pe.wait_ge(ld_b2, 16)
            for g in range(NC):
                if g >= 4:
                    pe.wait_ge(total_ready, g - 3)
                mm(ps[0:TC, g % 4, 0:DIM], comb_t[:, g * TC:(g + 1) * TC], b2_sb[:]).then_inc(b2_done, 1)

        @block.scalar
        def _(act):
            act.sem_inc(o_ready, 2)
            act.wait_ge(ld_pixels, 16 * BATCH)
            cut(act.copy, 0)
            act.wait_ge(pos_sub, 1)
            act.activation(pos_e[:], pos_e[:], ACT.Exp, scale=HEAD_DIM ** -0.5).then_inc(pos_exp, 1)
            for n in range(12):
                q, r = divmod(n, 2)
                j0, j1 = (0, 4) if r == 0 else (4, SIDE)
                act.wait_ge(px_done, n + 1)
                act.copy(patch_t[:, q].rearrange("p (b j) -> p j b", j=SIDE)[:, j0:j1],
                         ps[:, 4 + n % 4, 0:(j1 - j0) * ROWS].rearrange("p (j b) -> p j b", b=ROWS)).then_inc(px_ready, 1)
            def deviation(g, norm):
                act.wait_ge(var_ready, norm * NC + g + 1)
                act.activation(std[:, g:g + 1], mv[:, g, 1:2], ACT.Sqrt, bias=c("eps", TC)).then_inc(std_ready, 1)

            for g in range(NC):
                deviation(g, 0)
            act.wait_ge(wt_done, 1)
            for w in range(2):
                act.copy(wqk_t[:, w].rearrange("p k n -> p (k n)"), ps[0:DC, w, 0:KC * DIM]).then_inc(wt_ready, 1)
            for n in range(2 * MC):
                act.wait_ge(up_done, 2 * n + 1)
                if n >= 2:
                    act.wait_ge(u_ready, n - 1)
                act.activation(silu_sb[:, n % 2], ps[:, 4 + 2 * (n % 2), 0:HALF], ACT.Silu).then_inc(silu_ready, 1)
            for g in range(NC):
                deviation(g, 1)
            for n in range(8):
                hf, w, m = n // 4, (n // 2) % 2, n % 2
                act.wait_ge(proj_done, n + 1)
                act.copy((q_t, k_t)[w][:, m, 4 * hf:4 * hf + 4, 0:SPAN],
                         ps[0:DC, n % 4, 0:4 * SPAN].rearrange("p (g s) -> p g s", g=4)).then_inc(proj_ready, 1)
            for g in range(NC):
                act.wait_ge(nat_done, g + 1)
                act.copy(q_n[:, g], ps[0:SPAN, 4 + 2 * (g % 2), 0:DIM]).then_inc(nat_ready, 1)
                act.copy(k_n[:, g].rearrange("p a n -> p (a n)"), ps[0:SEQ, 5 + 2 * (g % 2), 0:NP * DIM]).then_inc(nat_ready, 1)

            def exp(g):
                act.wait_ge(sub_ready, g + 1)
                act.activation(e_sb[:, g % 2], e_sb[:, g % 2], ACT.Exp).then_inc(exp_ready, 1)

            exp(0)
            for g in range(NC):
                for s in range(3):
                    act.wait_ge(et_done, 3 * g + s + 1)
                    if g >= 1 and s == 0:
                        act.wait_ge(f_done, 4 * g - 2)
                    act.copy(e_t[:, s].rearrange("p a q -> p (a q)"), ps[0:SEQ, 2 + (4 * g + s) % 2, 0:4 * SPAN]).then_inc(et_ready, 1)
                if g + 1 < NC:
                    exp(g + 1)
            act.wait_ge(var_ready, 3 * NC)
            act.activation(std[:], mv[:, :, 1], ACT.Sqrt, bias=c("eps", TC)).then_inc(std_ready, 1)
            for g in range(NC):
                act.wait_ge(xnt_done, g + 1)
                act.copy(hn_t[:, :, g * TC:(g + 1) * TC],
                         ps[0:DC, 4 + g % 4, 0:KC * TC].rearrange("p (k t) -> p k t", k=KC)).then_inc(xnt_ready, 1)
            act.wait_ge(logit_ready, 2)
            act.activation(gate_g[:], gate_g[:], ACT.Exp).then_inc(gexp_ready, 1)
            act.activation(gate_e[:], gate_e[:], ACT.Exp).then_inc(gexp_ready, 1)

            def gelu(tile2, u):
                act.wait_ge(mm1_done, tile2 + 1)
                act.activation(ht[:, u, 0:4].rearrange("p m s -> p (m s)"), ps[:, 2 * u, 0:4 * SLOTS], ACT.Gelu).then_inc(ht_ready, 1)
                act.wait_ge(mm1_done, tile2 + 2)
                act.activation(ht[:, u, 4:MC].rearrange("p m s -> p (m s)"), ps[:, 2 * u + 1, 0:(MC - 4) * SLOTS], ACT.Gelu).then_inc(ht_ready, 1)

            act.wait_ge(table_ready, 1)
            gelu(0, 0)
            n = act.value_load(table[0:1, TABLE:TABLE + 1], min_val=0, max_val=TILES)
            with act.Fori(0, TILES // RING) as q:
                for half in range(2):
                    with act.If(q * RING + 2 * half < n):
                        for j in (2 * half, 2 * half + 1):
                            t = q * RING + j
                            gelu(t * 2 + 2, ring_pos(j, 1, 2))
                            u = ring_pos(j, 0, 2)
                            act.wait_ge(mm2_done, t + 1)
                            act.wait_ge(meta_ready, t + 1)
                            act.wait_ge(o_free[u], q * 32 + 16 * (j // 2 + 1))
                            act.activation(o_sb[:, u], ps[:, 6 + u, 0:DIM], ACT.Copy,
                                           scale=gate[:, ring_pos(j, 0, RING):ring_pos(j, 0, RING) + 1]).then_inc(o_ready, 1)
            act.copy(std[:, 0:1], rstd[:, 0:1]).then_inc(tiles_over, 1)

        @block.gpsimd
        def _(pool):
            pool.memset(spread_t[:], 0.0).then_inc(sp_zero, 1)
            pool.memset(xt[DC:DC + 1], 1.0).then_inc(sp_zero, 1)

            pool.wait_ge(sp_zero, 2)
            pool.wait_ge(ld_pixels, 16 * BATCH)
            cut(pool.tensor_copy, 1)
            cut(pool.tensor_copy, 2)
            pool.wait_ge(cut_ready[1], 1)
            pool.wait_ge(cut_ready[2], 1)

            def expand(g):
                pool.wait_ge(proj_ready, 4 if g < 4 else 8)
                if g >= 2:
                    pool.wait_ge(s_done, g - 1)
                for m in range(KC):
                    for u in range(NP):
                        shape = [DC, HC, SEQ]
                        last = pool.tensor_tensor(k_exp[:, g % 2, m, u],
                                                  k_t[:, m, g, u * LANE:u * LANE + SEQ].unsqueeze(1).to_broadcast(shape),
                                                  beta_mask[:, m].unsqueeze(2).to_broadcast(shape), ALU.mult)
                last.then_inc(kexp_ready, 1)

            pool.wait_ge(bm_ready, 1)
            expand(0)
            expand(1)
            for g in range(NC):
                for w in range(4):
                    kind, u = divmod(w, NP)
                    pool.wait_ge(f_ready, 4 * g + w + 1)
                    if g >= 2 and w == 0:
                        pool.wait_ge(t_done, g - 1)
                    f, o, done = f_sb[:, w % 2], vu_t[:, g % 2, kind, :, u, :], 2 * (4 * g + w)
                    pool.tensor_tensor(f[:, :, 0:3], f[:, :, 0:3], f[:, :, 3:6], ALU.add).then_inc(pool_chain, 1)
                    pool.wait_ge(pool_chain, done + 1)
                    pool.tensor_tensor(o, f[:, :, 0], f[:, :, 1], ALU.add).then_inc(pool_chain, 1)
                    pool.wait_ge(pool_chain, done + 2)
                    pool.tensor_tensor(o, o, f[:, :, 2], ALU.add).then_inc(vu_ready, 1)
                if g + 2 < NC:
                    expand(g + 2)

            def gather(u):
                pool.indirect_dma_start(xg[:, u], None, xn_dram, bass.IndirectOffsetOnAxis(fetch[:, u:u + 1], 0)).then_inc(xg_ready[u], 16)

            pool.wait_ge(xn_stored, 16 * NC)
            pool.wait_ge(fetch_ready, 1)
            for u in range(2):
                pool.dma_start(o_sb[:, u], consts[:, 0:DIM]).then_inc(o_free[u], 16)
            gather(0)
            pool.wait_ge(fetch_ready, 2)
            gather(1)
            pool.wait_ge(fetch_ready, 3)
            pool.wait_ge(xt_done, 1)
            gather(0)
            pool.wait_ge(table_ready, 1)
            def hold():
                pool.sem_inc(pool_turns, 1)

            n = pool.value_load(table[0:1, TABLE:TABLE + 1], min_val=0, max_val=TILES)
            with pool.Fori(0, TILES // RING) as q:
                for half in range(2):
                    with pool.If(q * RING + 2 * half < n):
                        for j in (2 * half, 2 * half + 1):
                            t = q * RING + j
                            pool.wait_ge(fetch_ready, t + 4)
                            pool.wait_ge(xt_done, t + 2)
                            hold()
                            gather(ring_pos(j, 3, 2))
                            u = ring_pos(j, 0, 2)
                            r = ring_pos(j, 0, RING)
                            pool.wait_ge(o_ready, t + 3)
                            hold()
                            pool.indirect_dma_start(picks_dram, bass.IndirectOffsetOnAxis(store[:, r:r + 1], 0),
                                                    o_sb[:, u], None).then_inc(o_free[u], 16)
            for u in range(2):
                pool.wait_ge(xg_ready[u], 16)

        @block.vector
        def _(dve):
            count = [0]

            def link(ins):
                count[0] += 1
                ins.then_inc(dve_chain, 1)
                dve.wait_ge(dve_chain, count[0])

            def moments(g, ready):
                dve.wait_ge(ready, g + 1)
                link(dve.bn_stats(stats[:, g], h[:, g]))
                dve.bn_aggr(mv[:, g], stats[:, g]).then_inc(var_ready, 1)

            def normalise(g, norm):
                if norm < 2:
                    dve.wait_ge(std_ready, norm * NC + g + 1)
                    link(dve.reciprocal(rstd[:, g:g + 1], std[:, g:g + 1]))
                return dve.tensor_scalar(hn[:, g], h[:, g], mv[:, g, 0:1], rstd[:, g:g + 1], ALU.subtract, ALU.mult)

            dve.memset(wqkv_sb[DC:DC + 1, 0, :], 0.0).then_inc(rep_ready, 1)
            dve.wait_ge(rep_ready, 1)
            dve.wait_ge(ld_qkv, 32)
            for k in range(KC):
                shape = [DC + 1, 2, HC, HEAD_DIM]
                dve.tensor_copy(wkv_rep[:, k], wqkv_sb[:, k, DIM:].rearrange("p (v d) -> p v d", v=2).unsqueeze(2)
                                .to_broadcast(shape)).then_inc(rep_ready, 1)
            dve.wait_ge(ld_const, 16)
            dve.wait_ge(pos_proj, 1)
            dve.tensor_copy(pos_qt[:], ps[0:DC, 0, 0:KC * SEQ].rearrange("p (k s) -> p k s", k=KC)).then_inc(pos_in, 1)
            shape = [DC, HC, SEQ]
            dve.tensor_tensor(pos_kexp[:], ps[0:DC, 0, 2 * SEQ:3 * SEQ].unsqueeze(1).to_broadcast(shape),
                              headmask.unsqueeze(2).to_broadcast(shape), ALU.mult).then_inc(pos_in, 1)
            dve.tensor_copy(pos_v[:], ps[0:SEQ, 1, 0:DC]).then_inc(pos_in, 1)
            dve.wait_ge(pos_s, 1)
            shape = [SEQ, HC, SEQ]
            for m in range(KC):
                last = dve.tensor_tensor(pos_e[:, m * HC:(m + 1) * HC], ps[0:SEQ, 2 + m, 0:HC * SEQ].rearrange("p (h s) -> p h s", h=HC),
                                         c("causal", SEQ).unsqueeze(1).to_broadcast(shape), ALU.add)
                link(last)
            shape = [SEQ, HEADS, SEQ]
            link(dve.tensor_reduce(pos_max[:, 0], pos_e[:], X, ALU.max))
            dve.tensor_tensor(pos_e[:], pos_e[:], pos_max[:, 0].unsqueeze(2).to_broadcast(shape), ALU.subtract).then_inc(pos_sub, 1)
            dve.wait_ge(pos_exp, 1)
            link(dve.tensor_reduce(pos_max[:, 1], pos_e[:], X, ALU.add))
            link(dve.reciprocal(pos_max[:, 0], pos_max[:, 1]))
            dve.tensor_tensor(pos_e[:], pos_e[:], pos_max[:, 0].unsqueeze(2).to_broadcast(shape), ALU.mult).then_inc(pos_norm, 1)
            dve.wait_ge(pos_tr, 1)
            dve.tensor_copy(pos_et[:], ps[0:SEQ, 0:KC, 0:HC * SEQ]).then_inc(pos_et_ready, 1)
            dve.wait_ge(pos_f_done, 1)
            for m in range(KC):
                link(dve.tensor_tensor(pos_f[:, m], ps[0:DC, 2 + m, 0:HC * SEQ].rearrange("p (h s) -> p h s", h=HC),
                                       headmask.unsqueeze(2).to_broadcast([DC, HC, SEQ]), ALU.mult))
            for m in range(KC):
                link(dve.tensor_reduce(pos_ot[:, m], pos_f[:, m].rearrange("p h s -> p s h"), X, ALU.add))
            dve.tensor_copy(pos_ot2[:], pos_ot[:].unsqueeze(2).to_broadcast([DC, KC, NP, SEQ])).then_inc(pos_o_ready, 1)
            dve.wait_ge(base_done, 1)
            dve.tensor_copy(base[:], ps[0:TC, 0, 0:DIM]).then_inc(base_ready, 1)
            dve.wait_ge(base_ready, 1)
            for g in range(NC):
                dve.wait_ge(tok_done, g + 1)
                dve.tensor_tensor(h[:, g], ps[0:TC, 4 + g % 4, 0:DIM], base[:], ALU.add).then_inc(h_ready, 1)
                moments(g, h_ready)
                if g >= 1:
                    normalise(g - 1, 0).then_inc(hn_ready, 1)
            normalise(NC - 1, 0).then_inc(hn_ready, 1)
            dve.wait_ge(ld_ln, 32)
            for hf in range(2):
                dve.wait_ge(hnt_done, 4 * hf + 4)
                for k in range(KC):
                    dve.tensor_scalar(hn_t[:, k, hf * HALF:(hf + 1) * HALF], ps[0:DC, k + 2 * hf, 0:HALF],
                                      ln_gb[:, 0, k:k + 1], ln_gb[:, 1, k:k + 1], ALU.mult, ALU.add).then_inc(hnt_ready, 1)
            for n in range(2 * MC):
                hf, m = divmod(n, MC)
                dve.wait_ge(silu_ready, n + 1)
                dve.wait_ge(up_done, 2 * n + 2)
                dve.tensor_tensor(u_t[:, m, hf * HALF:(hf + 1) * HALF], silu_sb[:, n % 2],
                                  ps[:, 5 + 2 * (n % 2), 0:HALF], ALU.mult).then_inc(u_ready, 1)
            for g in range(NC):
                dve.wait_ge(down_done, g + 1)
                dve.tensor_tensor(h[:, g], h[:, g], ps[0:TC, g % 4, 0:DIM], ALU.add).then_inc(h2_ready, 1)
                moments(g, h2_ready)
                if g >= 1:
                    normalise(g - 1, 1).then_inc(hn2_ready, 1)
            normalise(NC - 1, 1).then_inc(hn2_ready, 1)
            dve.wait_ge(sp_zero, 1)
            for g in range(NC):
                dve.wait_ge(sp_done, g + 1)
                for k in range(KC):
                    last = dve.tensor_copy(spread_t[:, k, g].rearrange("p (a s) -> p a s", a=NP)[:, :, 0:SEQ],
                                           ps[0:DC, 4 + g % 4, k * TC:(k + 1) * TC].rearrange("p (a s) -> p a s", a=NP))
                last.then_inc(sp_ready, 1)
            dve.wait_ge(ld_beta, 16)
            dve.tensor_tensor(beta_mask[:], beta_bc[:].rearrange("p (k h) -> p k h", k=KC),
                              headmask.unsqueeze(1).to_broadcast([DC, KC, HC]), ALU.mult).then_inc(bm_ready, 1)

            def shift(g):
                dve.wait_ge(s_done, g + 1)
                if g >= 2:
                    dve.wait_ge(f_done, 4 * g - 4)
                s = ps[0:SPAN, 0:KC, 0:HC * SEQ].rearrange("p k (h s) -> p k h s", h=HC)
                mx = e_max[:].rearrange("p (k h) -> p k h", k=KC)
                link(dve.tensor_reduce(mx, s, X, ALU.max))
                for m in range(KC):
                    last = dve.tensor_tensor(e_sb[:, g % 2, m], s[:, m], mx[:, m].unsqueeze(2).to_broadcast([SPAN, HC, SEQ]), ALU.subtract)
                last.then_inc(sub_ready, 1)

            shift(0)
            for g in range(NC):
                if g + 1 < NC:
                    shift(g + 1)
                dve.wait_ge(exp_ready, g + 1)
                dve.wait_ge(sub_ready, min(g + 2, NC))
                link(dve.tensor_reduce(e_max[:], e_sb[:, g % 2].rearrange("p k h s -> p (k h) s"), X, ALU.add))
                link(dve.reciprocal(e_rz[:, g % 2], e_max[:]))
                e_flat = e_sb[:, g % 2].rearrange("p k h s -> p (k h) s")
                dve.tensor_tensor(e_flat, e_flat, e_rz[:, g % 2].unsqueeze(2).to_broadcast([SPAN, HEADS, SEQ]),
                                  ALU.mult).then_inc(norm_ready, 1)
                for w in range(4):
                    n = 4 * g + w
                    dve.wait_ge(f_done, n + 1)
                    if n >= 2:
                        dve.wait_ge(vu_ready, n - 1)
                    for m in range(KC):
                        last = dve.tensor_tensor(f_sb[:, n % 2, m], ps[0:DC, 4 + 2 * (n % 2) + m, 0:HC * SEQ].rearrange("p (h s) -> p h s", h=HC),
                                                 headmask.unsqueeze(2).to_broadcast([DC, HC, SEQ]), ALU.mult)
                    last.then_inc(f_ready, 1)
                dve.wait_ge(t_done, g + 1)
                dve.tensor_tensor(h[:, g], h[:, g], ps[0:TC, 3, 0:DIM], ALU.add).then_inc(h3_ready, 1)
                moments(g, h3_ready)
            dve.wait_ge(std_ready, 2 * NC + 1)
            link(dve.reciprocal(rstd[:], std[:]))
            for g in range(NC):
                normalise(g, 2).then_inc(xn_ready, 1)

            for k, v in ((earlier_bf, "earlier"), (ones_bf, "ones")):
                link(dve.tensor_copy(k[:], c(v, TC)[:, 0:TC]))
            link(dve.memset(zeros[:], 0.0))
            link(dve.memset(list_src[:], 0.0))
            link(dve.tensor_copy(list_src[:, :, :, 0:3], c("token", TC).rearrange("p (c w) -> p c w", w=3).unsqueeze(1)
                                 .to_broadcast([TC, ALL_E, NC, 3])))
            RW = GROUPS + ALL_E
            dve.wait_ge(ld_router, 80)
            dve.wait_ge(logit_done, 1)
            raw = ps[0:TC, 0, 0:NC * RW].rearrange("p (c w) -> p c w", w=RW)
            link(dve.tensor_tensor(logit_g[:], raw[:, :, 0:GROUPS], rb_sb[:, 0:GROUPS].unsqueeze(1).to_broadcast([TC, NC, GROUPS]), ALU.add))
            link(dve.tensor_tensor(logit_e[:].rearrange("p c g e -> p c (g e)"), raw[:, :, GROUPS:],
                                   rb_sb[:, GROUPS:].unsqueeze(1).to_broadcast([TC, NC, ALL_E]), ALU.add))
            link(dve.tensor_reduce(red_g[:], logit_g[:], X, ALU.max))
            link(dve.tensor_reduce(red_e[:], logit_e[:], X, ALU.max))
            dve.tensor_tensor(gate_g[:], logit_g[:], red_g[:].unsqueeze(2).to_broadcast([TC, NC, GROUPS]), ALU.subtract).then_inc(logit_ready, 1)
            dve.tensor_tensor(gate_e[:], logit_e[:], red_e[:].unsqueeze(3).to_broadcast([TC, NC, GROUPS, EXPERTS]), ALU.subtract).then_inc(logit_ready, 1)

            def rank(values, n, sets, tie, out_):
                shape = [TC, sets, n, n]
                other, own = values.unsqueeze(2).to_broadcast(shape), values.unsqueeze(3).to_broadcast(shape)
                a = cmp_a[:].rearrange("p s i j -> p (s i j)")[:, 0:sets * n * n].rearrange("p (s i j) -> p s i j", i=n, j=n)
                b = cmp_b[:].rearrange("p s i j -> p (s i j)")[:, 0:sets * n * n].rearrange("p (s i j) -> p s i j", i=n, j=n)
                link(dve.tensor_tensor(a, other, own, ALU.is_equal))
                link(dve.tensor_tensor(a, a, tie.rearrange("p (i j) -> p i j", i=n).unsqueeze(1).to_broadcast(shape), ALU.mult))
                link(dve.tensor_tensor(b, other, own, ALU.is_gt))
                link(dve.tensor_tensor(a, a, b, ALU.add))
                link(dve.tensor_reduce(out_, a, X, ALU.add))

            rank(logit_g[:], GROUPS, NC, c("tie_g", TC), rank_g[:])
            rank(logit_e[:].rearrange("p c g e -> p (c g) e"), EXPERTS, NC * GROUPS, c("tie_e", TC),
                 rank_e[:].rearrange("p c g e -> p (c g) e"))
            link(dve.tensor_scalar(sel_g[:], rank_g[:], float(TOP_G), None, ALU.is_lt))
            wide = [TC, NC, GROUPS, EXPERTS]
            rank_flat = rank_e[:].rearrange("p c g e -> p (c g) e")
            link(dve.scalar_tensor_tensor(out=sel[:].rearrange("p c g e -> p (c g) e"), in0=rank_flat, scalar=float(TOP_E),
                                          in1=sel_g[:].rearrange("p c g -> p (c g)").unsqueeze(2).to_broadcast([TC, NC * GROUPS, EXPERTS]),
                                          op0=ALU.is_lt, op1=ALU.mult))
            dve.tensor_copy(sel_bf[:], sel[:].rearrange("p c g e -> p c (g e)")).then_inc(sel_ready, 1)
            dve.wait_ge(gexp_ready, 2)
            link(dve.tensor_tensor(gate_g[:], gate_g[:], sel_g[:], ALU.mult))
            link(dve.scalar_tensor_tensor(out=gate_e[:].rearrange("p c g e -> p (c g e)"), in0=rank_e[:].rearrange("p c g e -> p (c g e)"),
                                          scalar=float(TOP_E), in1=gate_e[:].rearrange("p c g e -> p (c g e)"), op0=ALU.is_lt, op1=ALU.mult))
            link(dve.tensor_reduce(red_g[:], gate_g[:], X, ALU.add))
            link(dve.tensor_reduce(red_e[:], gate_e[:], X, ALU.add))
            link(dve.reciprocal(red_g[:], red_g[:]))
            link(dve.reciprocal(red_e[:], red_e[:]))
            link(dve.tensor_tensor(gate_g[:], gate_g[:], red_g[:].unsqueeze(2).to_broadcast([TC, NC, GROUPS]), ALU.mult))
            link(dve.tensor_tensor(gate_e[:], gate_e[:], red_e[:].unsqueeze(3).to_broadcast(wide), ALU.mult))
            for v in (gate_g[:].rearrange("p c g -> p (c g)"), gate_e[:].rearrange("p c g e -> p (c g e)")):
                link(dve.scalar_tensor_tensor(out=v, in0=v, scalar=GATE_EPS, in1=v, op0=ALU.is_ge, op1=ALU.mult))
            link(dve.tensor_tensor(comb[:], gate_e[:], gate_g[:].unsqueeze(3).to_broadcast(wide), ALU.mult))
            comb_v = comb[:].rearrange("p c g e -> p c (g e)")
            rest = gate_tmp[:].rearrange("p c g e -> p c (g e)")
            part = [list_src[:, :, :, w].rearrange("p e c -> p c e") for w in range(LIST_W)]
            link(dve.tensor_copy(part[4], comb_v))
            link(dve.tensor_tensor(rest, comb_v, part[4], ALU.subtract))
            link(dve.tensor_copy(part[5], rest))
            link(dve.tensor_tensor(rest, rest, part[5], ALU.subtract))
            dve.tensor_copy(part[6], rest).then_inc(comb_ready, 1)
            sel_v = sel[:].rearrange("p c g e -> p c (g e)")
            flat = "p c e -> p (c e)"
            link(dve.tensor_tensor_scan(order[:].rearrange(flat), zeros[:], sel_v.rearrange(flat), 0.0, ALU.add, ALU.add))
            link(dve.tensor_tensor(order[:], order[:], sel_v, ALU.subtract))
            link(dve.tensor_tensor(part[3], order[:], c("picked", TC).unsqueeze(2).to_broadcast([TC, NC, ALL_E]), ALU.subtract))
            dve.wait_ge(rank_done, 1)
            shape = [TC, ALL_E, MAX_STEPS]
            link(dve.tensor_tensor(tile_cmp[:], ps[0:TC, 1, NC * ALL_E:(NC + 1) * ALL_E].unsqueeze(2).to_broadcast(shape),
                                   c("steps", TC).unsqueeze(1).to_broadcast(shape), ALU.is_gt))
            link(dve.tensor_reduce(tiles_of[:], tile_cmp[:], X, ALU.add))
            link(dve.tensor_tensor_scan(tiles_end[:], zeros[:, 0:ALL_E], tiles_of[:], 0.0, ALU.add, ALU.add))
            link(dve.tensor_scalar(owner_cmp[:], tiles_end[0:TABLE], c("tile", TABLE), None, ALU.is_le))
            link(dve.tensor_reduce(owner[:], owner_cmp[:], X, ALU.add))
            dve.tensor_scalar(owner[:], owner[:], float(ALL_E - 1), None, ALU.min).then_inc(owner_ready, 1)
            link(dve.tensor_tensor(first_slot[:], tiles_end[:], tiles_of[:], ALU.subtract))
            link(dve.tensor_scalar(first_slot[:], first_slot[:], float(SLOTS), None, ALU.mult))
            link(dve.scalar_tensor_tensor(out=slot_tmp[:], in0=ps[0:TC, 1, 0:NC * ALL_E].rearrange("p (c e) -> p c e", e=ALL_E), scalar=1.0,
                                          in1=first_slot[:].unsqueeze(1).to_broadcast([TC, NC, ALL_E]), op0=ALU.add, op1=ALU.add))
            link(dve.tensor_tensor(slot_tmp[:], slot_tmp[:], sel_v, ALU.mult))
            link(dve.tensor_scalar(slot_of[:].rearrange("p e c -> p c e"), slot_tmp[:], -1.0, None, ALU.add))
            dve.wait_ge(owner_done, 1)
            link(dve.tensor_copy(table[0:1, 0:TABLE], ps[0:1, 2, 0:TABLE]))
            dve.tensor_copy(table[0:1, TABLE:TABLE + 1], tiles_end[0:1, ALL_E - 1:ALL_E]).then_inc(table_ready, 1)
            dve.wait_ge(table_ready, 1)

            def wait_small(base_count, ins, k):
                ins.then_inc(small_chain, 1)
                dve.wait_ge(small_chain, base_count + k)

            def make_place(tile_no, u, done):
                e = dve.value_load(table[0:1, bass.ds(tile_no, 1)], min_val=0, max_val=ALL_E - 1)
                a = AT["first"][0]
                wait_small(done, dve.tensor_scalar(slot_rel[:], slot_of[:, bass.ds(e, 1)].rearrange("p a c -> p (a c)"),
                                                   cst[0:TC, bass.ds(tile_no + a, 1)], None, ALU.subtract), 1)
                wait_small(done, dve.tensor_copy(list_col[:, u].rearrange("p c w -> p (c w)"),
                                                 list_src[:, bass.ds(e, 1)].rearrange("p a c w -> p (a c w)")), 2)
                shape = [TC, NC, SLOTS]
                dve.tensor_tensor(place[:, u], slot_rel[:].unsqueeze(2).to_broadcast(shape),
                                  c("slot", TC).unsqueeze(1).to_broadcast(shape), ALU.is_equal).then_inc(place_ready, 1)

            def read_list(u, done):
                l = list_sb[:, u]
                wait_small(done, dve.tensor_copy(l, ps[:, 4 + u, 0:LIST_W]), 1)
                wait_small(done, dve.scalar_tensor_tensor(out=fetch_f[:, u:u + 1], in0=l[:, 1:2], scalar=float(TC), in1=l[:, 0:1],
                                                          op0=ALU.mult, op1=ALU.add), 2)
                dve.tensor_copy(fetch[:, u:u + 1], fetch_f[:, u:u + 1]).then_inc(fetch_ready, 1)

            def read_meta(u, r, done):
                l = list_sb[:, u]
                spare = c("spare")[:, u:u + 1]
                wait_small(done, dve.scalar_tensor_tensor(out=store_f[:, u, 0:1], in0=l[:, 3:4], scalar=float(TOKENS), in1=fetch_f[:, u:u + 1],
                                                          op0=ALU.mult, op1=ALU.add), 1)
                wait_small(done, dve.scalar_tensor_tensor(out=store_f[:, u, 1:2], in0=l[:, 2:3], scalar=spare, in1=store_f[:, u, 0:1],
                                                          op0=ALU.mult, op1=ALU.subtract), 2)
                wait_small(done, dve.tensor_scalar(store[:, r:r + 1], store_f[:, u, 1:2], -1.0, spare, ALU.mult, ALU.add), 3)
                dve.scalar_tensor_tensor(out=gate[:, r:r + 1], in0=l[:, 6:7], scalar=l[:, 5:6], in1=l[:, 4:5],
                                         op0=ALU.add, op1=ALU.add).then_inc(meta_ready, 1)

            def copy_tokens(u):
                dve.tensor_copy(xt[0:DC, u], ps[0:DC, 4 + u, 0:KC * SLOTS].rearrange("p (k s) -> p k s", k=KC)).then_inc(xt_ready, 1)

            SMALL = 7
            make_place(0, 0, 0)
            dve.wait_ge(sp_zero, 2)
            for j in range(3):
                done = 2 + SMALL * j
                dve.wait_ge(list_done, j + 1)
                read_list(j % 2, done)
                if j >= 1:
                    dve.wait_ge(xt_done, j)
                    copy_tokens((j - 1) % 2)
                make_place(j + 1, (j + 1) % 2, done + 2)
                read_meta(j % 2, j, done + 4)
            n = dve.value_load(table[0:1, TABLE:TABLE + 1], min_val=0, max_val=TILES)
            with dve.Fori(0, TILES // RING) as q:
                for half in range(2):
                    with dve.If(q * RING + 2 * half < n):
                        for j in (2 * half, 2 * half + 1):
                            t = q * RING + j
                            done = q * (RING * SMALL) + (2 + SMALL * 3 + SMALL * j)
                            dve.wait_ge(list_done, t + 4)
                            read_list(ring_pos(j, 3, 2), done)
                            dve.wait_ge(xt_done, t + 3)
                            copy_tokens(ring_pos(j, 2, 2))
                            make_place(t + 4, ring_pos(j, 4, 2), done + 2)
                            dve.wait_ge(o_ready, t + 2)
                            dve.wait_ge(o_free[ring_pos(j, 1, 2)], q * 32 + 16 * ((j + 1) // 2 + 1))
                            read_meta(ring_pos(j, 3, 2), ring_pos(j, 3, RING), done + 4)

            dve.memset(zeros[:, 0:1], 0.0).then_inc(tiles_over, 1)

            dve.wait_ge(combt_done, 1)
            for a in range(2):
                dve.tensor_copy(comb_t[:, a * HALF:(a + 1) * HALF], ps[0:ALL_E, 4 + a, 0:HALF]).then_inc(combt_ready, 1)
            for g in range(NC):
                dve.wait_ge(b2_done, g + 1)
                dve.tensor_tensor(h[:, g], h[:, g], ps[0:TC, g % 4, 0:DIM], ALU.add).then_inc(total_ready, 1)
            dve.wait_ge(total_ready, NC)
            dve.wait_ge(picks_ready, 16 * NC)
            for g in range(NC):
                link(dve.tensor_reduce(total[:, g], picks[:, g].rearrange("p k d -> p d k"), X, ALU.add))
                dve.tensor_tensor(total[:, g], total[:, g], h[:, g], ALU.add).then_inc(out_ready, 1)

_INS = ["x", "L0_tok_patch_w", "L0_tok_patch_b", "L0_tok_ln_g", "L0_tok_ln_b", "L0_tok_w1", "L0_tok_w2", "L0_tok_w3",
        "L0_tok_wqkv", "L0_tok_bqkv", "L0_tok_wo", "L0_tok_bo", "L0_attn_Wq", "L0_attn_Wk", "L0_attn_betas",
        "L0_ffn_Wg", "L0_ffn_bg", "L0_ffn_We", "L0_ffn_be", "L0_ffn_W1", "L0_ffn_b1", "L0_ffn_W2", "L0_ffn_b2"]

def kernel(**inputs):
    import numpy as _np
    import concourse.bacc as _bacc
    from concourse import mybir as _mybir
    from concourse.bass_utils import run_bass_kernel_spmd as _run

    nc = _bacc.Bacc("TRN2", target_bir_lowering=False, num_devices=1)
    arrays, args = {}, []
    for name in _INS:
        a = _np.ascontiguousarray(inputs[name])
        arrays[f"in_{name}_dram"] = a
        args.append(nc.dram_tensor(f"in_{name}_dram", a.shape, _mybir.dt.from_np(a.dtype), kind="ExternalInput").ap())
    arrays["in_constants_dram"] = constants()
    args.append(nc.dram_tensor("in_constants_dram", (128, CONST_W), _mybir.dt.float32, kind="ExternalInput").ap())
    args.append(nc.dram_tensor("out_0_dram", (BATCH, SEQ, DIM), _mybir.dt.float32, kind="ExternalOutput").ap())
    vit_moe_program(nc, *args)
    r = _run(nc, [arrays], core_ids=[0])
    return r.results[0]["out_0_dram"]
```

```python
import numpy as np
from contextlib import ExitStack

import concourse.bass as bass
from concourse import mybir

BATCH, CHANNELS, IMG, PATCH = 16, 3, 112, 16
SIDE = IMG // PATCH
SEQ = SIDE * SIDE
TOKENS = BATCH * SEQ
DIM, HEADS = 192, 12
HEAD_DIM = DIM // HEADS
HIDDEN = 4 * DIM
GROUPS, EXPERTS, TOP_G, TOP_E = 4, 8, 2, 4
ALL_E = GROUPS * EXPERTS
PICKS = TOP_G * TOP_E
LN_EPS, GATE_EPS = 1e-5, 1e-6

KC = 2
DC = DIM // KC
HC = HEADS // KC
NP = 2
TC = NP * SEQ
NC = TOKENS // TC
LANE = 64
ROWS_FULL = 128
SPAN = LANE + SEQ
MC = HIDDEN // 128
HALF = TOKENS // 2
ROWS = BATCH * SIDE
QC = CHANNELS * 2

SLOTS = 128
TILES = (TOKENS * PICKS - ALL_E) // SLOTS + ALL_E
RING = 4
TABLE = TILES + RING
MAX_STEPS = -(-TOKENS // SLOTS)
LIST_W = 8
NAT_FIRST = 5
assert TILES % RING == 0

FIELDS = dict(ident=128, sin=KC * SEQ, earlier=TC, headmask=HC, causal=SEQ, slot=SLOTS,
              token=NC * 3, tie_e=EXPERTS * EXPERTS, tie_g=GROUPS * GROUPS, steps=MAX_STEPS,
              tile=1, spare=2, picked=NC, first=TABLE, eps=1, ones=128)
AT, _at = {}, 0
for _name, _width in FIELDS.items():
    AT[_name] = (_at, _at + _width)
    _at += _width
CONST_W = _at

def constants():
    c = np.zeros((128, CONST_W), np.float32)

    def put(name, value):
        value = np.asarray(value, np.float32)
        value = value.reshape(value.shape[0], -1)
        a, _ = AT[name]
        c[:value.shape[0], a:a + value.shape[1]] = value

    put("ident", np.eye(128))
    scales = np.linspace(1.0, 5.0, DIM // 4)
    seq = np.linspace(-1.0, 1.0, SIDE)[:, None] * scales[None, :] * np.pi
    a = np.broadcast_to(seq[:, None, :], (SIDE, SIDE, DIM // 4))
    b = np.broadcast_to(seq[None, :, :], (SIDE, SIDE, DIM // 4))
    table = np.repeat(np.concatenate([np.sin(a), np.sin(b)], -1).reshape(SEQ, DIM // 2), 2, axis=-1)
    sin = np.zeros((DC + 1, KC, SEQ))
    sin[:DC] = table.T.reshape(KC, DC, SEQ).transpose(1, 0, 2)
    sin[DC, KC - 1] = 1.0
    put("sin", sin)
    t = np.arange(TC)
    put("earlier", t[:, None] < t[None, :])
    put("headmask", np.arange(DC)[:, None] // HEAD_DIM == np.arange(HC)[None, :])
    s = np.arange(SEQ)
    put("causal", np.where(s[:, None] >= s[None, :], 0.0, -1e30))
    put("slot", np.broadcast_to(np.arange(SLOTS), (128, SLOTS)))
    token = np.zeros((TC, NC, 3))
    token[:, :, 0] = t[:, None]
    token[:, :, 1] = np.arange(NC)[None, :]
    token[:, :, 2] = 1.0
    put("token", token)
    e, g = np.arange(EXPERTS), np.arange(GROUPS)
    put("tie_e", np.broadcast_to((e[None, :] < e[:, None]).ravel(), (128, EXPERTS ** 2)))
    put("tie_g", np.broadcast_to((g[None, :] < g[:, None]).ravel(), (128, GROUPS ** 2)))
    put("steps", np.broadcast_to(SLOTS * np.arange(MAX_STEPS), (128, MAX_STEPS)))
    put("tile", np.arange(128)[:, None])
    put("spare", PICKS * TOKENS + np.arange(128)[:, None] + SLOTS * np.arange(2)[None, :])
    put("picked", np.broadcast_to(PICKS * np.arange(NC), (128, NC)))
    put("first", np.broadcast_to(SLOTS * np.arange(TABLE), (128, TABLE)))
    put("eps", np.full((128, 1), LN_EPS))
    put("ones", np.ones((128, 128)))
    return c

def vit_moe_program(nc, x, patch_w, patch_b, ln_g, ln_b, w1, w2, w3, wqkv, bqkv, wo, bo,
                    attn_wq, attn_wk, betas, wg, bg, we, be, ew1, eb1, ew2, eb2, consts, out):
    F32, BF16, I32 = mybir.dt.float32, mybir.dt.bfloat16, mybir.dt.int32
    ALU, ACT, X = mybir.AluOpType, mybir.ActivationFunctionType, mybir.AxisListType.X

    with ExitStack() as ctx:
        def sb(name, shape, dt=F32):
            return ctx.enter_context(nc.sbuf_tensor(name, shape, dt))

        def sem(name):
            return ctx.enter_context(nc.semaphore(name))

        early = ExitStack()

        def sb_early(name, shape, dt=F32):
            return early.enter_context(nc.sbuf_tensor(name, shape, dt))

        front = ExitStack()

        def sb_front(name, shape, dt=F32):
            return front.enter_context(nc.sbuf_tensor(name, shape, dt))

        xn_dram = nc.dram_tensor("xn_dram", [TOKENS, DIM], F32, kind="Internal").ap()
        picks_dram = nc.dram_tensor("picks_dram", [PICKS * TOKENS + 2 * SLOTS, DIM], F32, kind="Internal").ap()

        cst = sb("cst", [128, CONST_W])
        wqk_sb = sb("wqk_sb", [DC, 2, KC, DIM])
        wqk_t = sb("wqk_t", [DC, 2, KC, DIM])
        beta_bc = sb("beta_bc", [DC, HEADS])
        beta_mask = sb("beta_mask", [DC, KC, HC])
        wr_sb = sb("wr_sb", [DC, KC, GROUPS + ALL_E])
        rb_sb = sb("rb_sb", [TC, GROUPS + ALL_E])
        b2_sb = sb("b2_sb", [ALL_E, DIM])
        h = sb("h", [TC, NC, DIM])
        hn = sb("hn", [TC, NC, DIM])
        xt = sb("xt", [DC + 1, 2, KC, SLOTS])
        stats = sb("stats", [TC, NC, 6])
        mv = sb("mv", [TC, NC, 2])
        std = sb("std", [TC, NC])
        rstd = sb("rstd", [TC, NC])
        hn_t = sb("hn_t", [DC, KC, TOKENS])
        patch_w_sb = sb_early("patch_w_sb", [128, CHANNELS, 2, DIM])
        w1_sb = sb_early("w1_sb", [DC, KC, HIDDEN])
        w3_sb = sb_early("w3_sb", [DC, KC, HIDDEN])
        w2_sb = sb_early("w2_sb", [128, MC, DIM])
        ln_gb = sb_early("ln_gb", [DC, 2, KC])
        base = sb_early("base", [TC, DIM])
        patch_t = sb_early("patch_t", [128, QC, TOKENS])
        silu_sb = sb_early("silu_sb", [128, 2, HALF])
        u_t = sb_early("u_t", [128, MC, TOKENS])
        spread_t = sb_early("spread_t", [DC, KC, NC, 128])
        q_t = sb_early("q_t", [ROWS_FULL, KC, NC, 128])
        k_t = sb_early("k_t", [DC, KC, NC, 128])
        pixels = sb_front("pixels", [ROWS, CHANNELS, PATCH * IMG])
        patches = sb_front("patches", [ROWS, CHANNELS, SIDE, PATCH, PATCH])
        wqkv_sb = sb_front("wqkv_sb", [DC + 1, KC, DIM + 2 * HEAD_DIM])
        wkv_rep = sb_front("wkv_rep", [DC + 1, KC, 2, HC, HEAD_DIM])
        wo_sb = sb_front("wo_sb", [DC, KC, DIM])
        row_bias = sb_front("row_bias", [2, DIM])
        pos_qt = sb_front("pos_qt", [DC, KC, SEQ])
        pos_kexp = sb_front("pos_kexp", [DC, HC, SEQ])
        pos_v = sb_front("pos_v", [SEQ, DC])
        pos_e = sb_front("pos_e", [SEQ, HEADS, SEQ])
        pos_max = sb_front("pos_max", [SEQ, 2, HEADS])
        pos_et = sb_front("pos_et", [SEQ, KC, HC * SEQ])
        pos_f = sb_front("pos_f", [DC, KC, HC, SEQ])
        pos_ot = sb_front("pos_ot", [DC, KC, SEQ])
        pos_ot2 = sb_front("pos_ot2", [DC, KC, NP, SEQ])
        front.close()
        q_n = sb_early("q_n", [SPAN, NC, NP, DIM])
        k_n = sb_early("k_n", [ROWS_FULL, NC, NP, DIM])
        k_exp = sb_early("k_exp", [ROWS_FULL, 2, KC, NP, HC, SEQ])
        e_sb = sb_early("e_sb", [SPAN, 2, KC, HC, SEQ])
        e_max = sb_early("e_max", [SPAN, HEADS])
        e_rz = sb_early("e_rz", [SPAN, 2, HEADS])
        e_t = sb_early("e_t", [ROWS_FULL, 3, 4, SPAN])
        vu_t = sb_early("vu_t", [DC, 2, 2, KC, NP, SEQ])
        early.close()
        logit_g = sb("logit_g", [TC, NC, GROUPS])
        logit_e = sb("logit_e", [TC, NC, GROUPS, EXPERTS])
        cmp_a = sb("cmp_a", [TC, NC * GROUPS, EXPERTS, EXPERTS])
        cmp_b = sb("cmp_b", [TC, NC * GROUPS, EXPERTS, EXPERTS])
        sel_g = sb("sel_g", [TC, NC, GROUPS])
        rank_e = sb("rank_e", [TC, NC, GROUPS, EXPERTS])
        rank_g = sb("rank_g", [TC, NC, GROUPS])
        red_e = sb("red_e", [TC, NC, GROUPS])
        red_g = sb("red_g", [TC, NC])
        gate_e = sb("gate_e", [TC, NC, GROUPS, EXPERTS])
        gate_g = sb("gate_g", [TC, NC, GROUPS])
        gate_tmp = sb("gate_tmp", [TC, NC, GROUPS, EXPERTS])
        sel = sb("sel", [TC, NC, GROUPS, EXPERTS])
        sel_bf = sb("sel_bf", [TC, NC, ALL_E], BF16)
        comb = sb("comb", [TC, NC, GROUPS, EXPERTS])
        comb_t = sb("comb_t", [ALL_E, TOKENS])
        zeros = sb("zeros", [TC, NC * ALL_E])
        order = sb("order", [TC, NC, ALL_E])
        earlier_bf = sb("earlier_bf", [TC, TC], BF16)
        ones_bf = sb("ones_bf", [TC, TC], BF16)
        tile_cmp = sb("tile_cmp", [TC, ALL_E, MAX_STEPS])
        tiles_of = sb("tiles_of", [TC, ALL_E])
        tiles_end = sb("tiles_end", [TC, ALL_E])
        first_slot = sb("first_slot", [TC, ALL_E])
        slot_of = sb("slot_of", [TC, ALL_E, NC])
        slot_tmp = sb("slot_tmp", [TC, NC, ALL_E])
        list_src = sb("list_src", [TC, ALL_E, NC, LIST_W], BF16)
        owner_cmp = sb("owner_cmp", [TABLE, ALL_E])
        owner = sb("owner", [TABLE, 1])
        table = sb("table", [1, TABLE + 1], I32)
        slot_rel = sb("slot_rel", [TC, NC])
        place = sb("place", [TC, 2, NC, SLOTS], BF16)
        list_col = sb("list_col", [TC, 2, NC, LIST_W], BF16)
        list_sb = sb("list_sb", [SLOTS, 2, LIST_W])
        fetch_f = sb("fetch_f", [SLOTS, 2])
        fetch = sb("fetch", [SLOTS, 2], I32)
        store_f = sb("store_f", [SLOTS, 2, 2])
        store = sb("store", [SLOTS, RING], I32)
        gate = sb("gate", [SLOTS, RING])
        xg = sb("xg", [SLOTS, 2, DIM])
        ew1_sb = sb("ew1_sb", [DC + 1, 2, KC, HIDDEN])
        ew2_sb = sb("ew2_sb", [128, 2, MC, DIM])
        ht = sb("ht", [128, 2, MC, SLOTS])
        o_sb = sb("o_sb", [SLOTS, 2, DIM])
        picks = sb("picks", [TC, NC, PICKS, DIM])
        total = sb("total", [TC, NC, DIM])

        ps = ctx.enter_context(nc.psum_tensor("ps", [128, 8, 512], F32))

        def c(name, parts=128):
            a, b = AT[name]
            return cst[0:parts, a:b]

        ident = c("ident")
        headmask = c("headmask", DC)

        ld_const, ld_qkv, ld_pixels, ld_patch_w, ld_wo = (sem(n) for n in (
            "ld_const", "ld_qkv", "ld_pixels", "ld_patch_w", "ld_wo"))
        ld_ln, ld_w13, ld_w2, ld_wqk, ld_beta, ld_router, ld_b2 = (sem(n) for n in (
            "ld_ln", "ld_w13", "ld_w2", "ld_wqk", "ld_beta", "ld_router", "ld_b2"))
        var_ready, std_ready = sem("var_ready"), sem("std_ready")
        dve_chain, small_chain = sem("dve_chain"), sem("small_chain")
        rep_ready, pos_proj, pos_in, pos_s, pos_sub, pos_exp, pos_norm = (sem(n) for n in (
            "rep_ready", "pos_proj", "pos_in", "pos_s", "pos_sub", "pos_exp", "pos_norm"))
        pos_tr, pos_et_ready, pos_f_done, pos_o_ready, base_done, base_ready = (sem(n) for n in (
            "pos_tr", "pos_et_ready", "pos_f_done", "pos_o_ready", "base_done", "base_ready"))
        cut_ready = [sem(f"cut_ready{ch}") for ch in range(CHANNELS)]
        px_done, px_ready, tok_done, h_ready, hn_ready, hnt_done, hnt_ready = (sem(n) for n in (
            "px_done", "px_ready", "tok_done", "h_ready", "hn_ready", "hnt_done", "hnt_ready"))
        up_done, silu_ready, u_ready, down_done, h2_ready = (sem(n) for n in (
            "up_done", "silu_ready", "u_ready", "down_done", "h2_ready"))
        wt_done, wt_ready, hn2_ready, sp_done, sp_ready, sp_zero, proj_done = (sem(n) for n in (
            "wt_done", "wt_ready", "hn2_ready", "sp_done", "sp_ready", "sp_zero", "proj_done"))
        pad_zero = sem("pad_zero")
        nat_done, bm_ready, kexp_ready, s_done, sub_ready, exp_ready, norm_ready = (sem(n) for n in (
            "nat_done", "bm_ready", "kexp_ready", "s_done", "sub_ready", "exp_ready", "norm_ready"))
        et_done, et_ready, f_done, even_ready, vu_ready, t_done, h3_ready = (sem(n) for n in (
            "et_done", "et_ready", "f_done", "even_ready", "vu_ready", "t_done", "h3_ready"))
        qk_ready = [sem("q_ready"), sem("k_ready")]
        nat_ready = [sem("q_n_ready"), sem("k_n_ready")]
        xn_ready, xn_stored, xnt_done, xnt_ready, logit_done, logit_ready, gexp_ready = (sem(n) for n in (
            "xn_ready", "xn_stored", "xnt_done", "xnt_ready", "logit_done", "logit_ready", "gexp_ready"))
        sel_ready, rank_done, comb_ready, combt_done, combt_ready, owner_ready, owner_done, table_ready = (
            sem(n) for n in ("sel_ready", "rank_done", "comb_ready", "combt_done", "combt_ready",
                             "owner_ready", "owner_done", "table_ready"))
        place_ready, list_done, fetch_ready, meta_ready, xt_done, xt_ready = (sem(n) for n in (
            "place_ready", "list_done", "fetch_ready", "meta_ready", "xt_done", "xt_ready"))
        xg_ready = [sem(f"xg_ready{u}") for u in range(2)]
        ew1_ready = [sem(f"ew1_ready{u}") for u in range(2)]
        ew2_ready = [sem(f"ew2_ready{u}") for u in range(2)]
        o_free = [sem(f"o_free{u}") for u in range(2)]
        tiles_over, pool_turns = sem("tiles_over"), sem("pool_turns")
        mm1_done, ht_ready, mm2_done, o_ready = (sem(n) for n in ("mm1_done", "ht_ready", "mm2_done", "o_ready"))
        b2_done, total_ready, picks_ready, out_ready, stored = (sem(n) for n in (
            "b2_done", "total_ready", "picks_ready", "out_ready", "stored"))

        def cut(copy, ch):
            return copy(patches[:, ch].rearrange("p j r w -> p r j w"),
                        pixels[:, ch].rearrange("p (r j w) -> p r j w", r=PATCH, w=PATCH)).then_inc(cut_ready[ch], 1)

        def ring_pos(j, off, n):
            return (j + off) % n

        block = ctx.enter_context(nc.Block())

        @block.sync
        def _(sp):
            sp.dma_start(cst[:], consts).then_inc(ld_const, 16)
            sp.dma_start(wqkv_sb[0:DC], wqkv.rearrange("(k p) n -> p k n", p=DC)).then_inc(ld_qkv, 16)
            sp.dma_start(wqkv_sb[DC:DC + 1, KC - 1, :], bqkv.rearrange("(a n) -> a n", a=1)).then_inc(ld_qkv, 16)
            for b in range(BATCH):
                sp.dma_start(pixels[b * SIDE:(b + 1) * SIDE],
                             x[b].rearrange("c (i r) w -> i c (r w)", r=PATCH)).then_inc(ld_pixels, 16)
            sp.dma_start(wo_sb[:], wo.rearrange("(k p) n -> p k n", p=DC)).then_inc(ld_wo, 16)
            sp.dma_start(row_bias[0:1], bo.rearrange("(a n) -> a n", a=1)).then_inc(ld_wo, 16)
            sp.dma_start(row_bias[1:2], patch_b.rearrange("(a n) -> a n", a=1)).then_inc(ld_wo, 16)
            patch_view = patch_w.rearrange("(f p c) n -> c f p n", f=2, c=CHANNELS)
            for ch in range(CHANNELS):
                sp.dma_start(patch_w_sb[:, ch], patch_view[ch].rearrange("f p n -> p f n")).then_inc(ld_patch_w, 16)
            sp.dma_start(ln_gb[:, 0, :], ln_g.rearrange("(k p) -> p k", p=DC), allow_slow_non_contiguous=True).then_inc(ld_ln, 16)
            sp.dma_start(ln_gb[:, 1, :], ln_b.rearrange("(k p) -> p k", p=DC), allow_slow_non_contiguous=True).then_inc(ld_ln, 16)
            sp.dma_start(w1_sb[:], w1.rearrange("(k p) n -> p k n", p=DC)).then_inc(ld_w13, 16)
            sp.dma_start(w3_sb[:], w3.rearrange("(k p) n -> p k n", p=DC)).then_inc(ld_w13, 16)
            sp.dma_start(wqk_sb[:, 0], attn_wq.rearrange("(k p) n -> p k n", p=DC)).then_inc(ld_wqk, 16)
            sp.dma_start(wqk_sb[:, 1], attn_wk.rearrange("(k p) n -> p k n", p=DC)).then_inc(ld_wqk, 16)
            sp.dma_start(w2_sb[:], w2.rearrange("(k p) n -> p k n", p=128)).then_inc(ld_w2, 16)
            sp.dma_start(beta_bc[:], betas.partition_broadcast(DC)).then_inc(ld_beta, 16)
            sp.dma_start(wr_sb[:, :, 0:GROUPS], wg.rearrange("(k p) n -> p k n", p=DC)).then_inc(ld_router, 16)
            for k in range(KC):
                sp.dma_start(wr_sb[:, k, GROUPS:].rearrange("p (g e) -> p g e", g=GROUPS),
                             we[:, k * DC:(k + 1) * DC, :].rearrange("g p e -> p g e")).then_inc(ld_router, 16)
            sp.dma_start(rb_sb[:, 0:GROUPS], bg.partition_broadcast(TC)).then_inc(ld_router, 16)
            sp.dma_start(rb_sb[:, GROUPS:], be.rearrange("g e -> (g e)").partition_broadcast(TC)).then_inc(ld_router, 16)
            sp.dma_start(b2_sb[:], eb2.rearrange("g e n -> (g e) n")).then_inc(ld_b2, 16)

            for g in range(NC):
                sp.wait_ge(xn_ready, g + 1)
                sp.dma_start(xn_dram[g * TC:(g + 1) * TC, :], hn[:, g, :]).then_inc(xn_stored, 16)

            ew1_v = ew1.rearrange("g e (k p) m -> (g e) p k m", p=DC)
            eb1_v = eb1.rearrange("g e m -> (g e) m")
            ew2_v = ew2.rearrange("g e (k p) n -> (g e) p k n", p=128)

            def load_w1(tile, u, *wait):
                e = sp.value_load(table[0:1, bass.ds(tile, 1)], min_val=0, max_val=ALL_E - 1)
                if wait:
                    sp.wait_ge(*wait)
                sp.dma_start(ew1_sb[0:DC, u], ew1_v[bass.ds(e, 1)].rearrange("a p k m -> p (a k) m")).then_inc(ew1_ready[u], 16)
                sp.dma_start(ew1_sb[DC:DC + 1, u, KC - 1, :], eb1_v[bass.ds(e, 1), :]).then_inc(ew1_ready[u], 16)

            def load_w2(tile, u, *wait):
                e = sp.value_load(table[0:1, bass.ds(tile, 1)], min_val=0, max_val=ALL_E - 1)
                if wait:
                    sp.wait_ge(*wait)
                sp.dma_start(ew2_sb[:, u], ew2_v[bass.ds(e, 1)].rearrange("a p k n -> p (a k) n")).then_inc(ew2_ready[u], 16)

            sp.wait_ge(table_ready, 1)
            load_w1(0, 0)
            load_w1(1, 1)
            load_w2(0, 0)
            load_w2(1, 1)
            sp.wait_ge(mm1_done, 2)
            load_w1(2, 0)
            n = sp.value_load(table[0:1, TABLE:TABLE + 1], min_val=0, max_val=TILES)
            after_even, after_others, after_ew2 = (sp.alloc_register(a) for a in ("after_even", "after_others", "after_ew2"))
            sp.reg_alu(after_ew2, n + 1, 1, ALU.logical_shift_right)
            sp.reg_alu(after_ew2, after_ew2, 16, ALU.mult)
            sp.reg_alu(after_ew2, after_ew2, 16, ALU.add)
            sp.reg_alu(after_others, after_ew2, after_ew2, ALU.add)
            sp.reg_alu(after_even, after_others, 32, ALU.add)
            with sp.Fori(0, TILES // RING) as q:
                for half in range(2):
                    with sp.If(q * RING + 2 * half < n):
                        for j in (2 * half, 2 * half + 1):
                            t = q * RING + j
                            load_w1(t + 3, ring_pos(j, 3, 2), mm1_done, t * 2 + 4)
                            load_w2(t + 2, ring_pos(j, 2, 2), mm2_done, t + 1)
            sp.wait_ge(ew1_ready[0], after_even)
            sp.wait_ge(ew1_ready[1], after_others)
            for u in range(2):
                sp.wait_ge(ew2_ready[u], after_ew2)
                sp.wait_ge(o_free[u], after_ew2)
            for g in range(NC):
                sp.dma_start(picks[:, g], picks_dram[0:PICKS * TOKENS, :].rearrange(
                    "(k t) d -> t k d", k=PICKS)[g * TC:(g + 1) * TC]).then_inc(picks_ready, 16)
            out_v = out.rearrange("b s d -> (b s) d")
            for g in range(NC):
                sp.wait_ge(out_ready, g + 1)
                sp.dma_start(out_v[g * TC:(g + 1) * TC, :], total[:, g, :]).then_inc(stored, 16)
            sp.wait_ge(stored, 16 * NC)

        @block.tensor
        def _(pe):
            def mm(o, lhs, rhs, start=True, stop=True):
                return pe.matmul(o, lhs, rhs, start=start, stop=stop)

            pe.wait_ge(ld_const, 16)
            pe.wait_ge(ld_qkv, 32)
            pe.wait_ge(rep_ready, 3)
            sin = c("sin", DC + 1).rearrange("p (k s) -> p k s", k=KC)
            for m in range(KC):
                for k in range(KC):
                    mm(ps[0:DC, 0, m * SEQ:(m + 1) * SEQ], wqkv_sb[:, k, m * DC:(m + 1) * DC], sin[:, k], k == 0, k == 1)
            for k in range(KC):
                mm(ps[0:DC, 0, 2 * SEQ:3 * SEQ], wkv_rep[:, k, 0].rearrange("p h d -> p (h d)"), sin[:, k], k == 0, k == 1)
            for k in range(KC):
                last = mm(ps[0:SEQ, 1, 0:DC], sin[:, k], wkv_rep[:, k, 1].rearrange("p h d -> p (h d)"), k == 0, k == 1)
            last.then_inc(pos_proj, 1)
            pe.wait_ge(pos_in, 3)
            for m in range(KC):
                last = mm(ps[0:SEQ, 2 + m, 0:HC * SEQ], pos_qt[:, m], pos_kexp[:].rearrange("p h s -> p (h s)"))
            last.then_inc(pos_s, 1)

            def pixel_unit(n):
                q, r = divmod(n, 2)
                ch, f = divmod(q, 2)
                pe.wait_ge(cut_ready[ch], 1)
                if n >= 4:
                    pe.wait_ge(px_ready, n - 3)
                js = range(0, 4) if r == 0 else range(4, SIDE)
                for a, jj in enumerate(js):
                    last = pe.transpose(ps[:, 4 + n % 4, a * ROWS:(a + 1) * ROWS],
                                        patches[:, ch, jj, f * 8:f * 8 + 8].rearrange("p r w -> p (r w)"), ident[0:ROWS, 0:ROWS])
                last.then_inc(px_done, 1)

            for n in range(6):
                pixel_unit(n)
            pe.wait_ge(pos_norm, 1)
            for hd in range(HEADS):
                m, a = divmod(hd, HC)
                last = pe.transpose(ps[0:SEQ, m, a * SEQ:(a + 1) * SEQ], pos_e[:, hd, :], ident[0:SEQ, 0:SEQ])
            last.then_inc(pos_tr, 1)
            for n in range(6, 9):
                pixel_unit(n)
            pe.wait_ge(pos_et_ready, 1)
            for m in range(KC):
                last = mm(ps[0:DC, 2 + m, 0:HC * SEQ], pos_v[:], pos_et[:, m])
            last.then_inc(pos_f_done, 1)
            for n in range(9, 12):
                pixel_unit(n)
            pe.wait_ge(pos_o_ready, 1)
            pe.wait_ge(ld_wqk, 32)
            for w in range(2):
                for m in range(KC):
                    for k in range(KC):
                        last = pe.transpose(ps[0:DC, 2 + w, (k * KC + m) * DC:(k * KC + m + 1) * DC],
                                            wqk_sb[:, w, m, k * DC:(k + 1) * DC], ident[0:DC, 0:DC])
            last.then_inc(wt_done, 1)
            pe.wait_ge(ld_wo, 48)
            for m in range(KC):
                mm(ps[0:TC, 0, 0:DIM], pos_ot2[:, m].rearrange("p a s -> p (a s)"), wo_sb[:, m], m == 0, False)
            mm(ps[0:TC, 0, 0:DIM], c("ones", 2)[:, 0:TC], row_bias[:], False, True).then_inc(base_done, 1)

            pe.wait_ge(ld_patch_w, 48)
            pe.wait_ge(px_ready, 12)

            def hn_turn(g):
                pe.wait_ge(hn_ready, g + 1)
                for k in range(KC):
                    last = pe.transpose(ps[0:DC, k + 2 * (g // 4), (g % 4) * TC:(g % 4 + 1) * TC],
                                        hn[:, g, k * DC:(k + 1) * DC], ident[0:TC, 0:TC])
                last.then_inc(hnt_done, 1)

            for g in range(NC):
                if g >= 4:
                    pe.wait_ge(h_ready, g - 3)
                for q in range(QC):
                    last = mm(ps[0:TC, 4 + g % 4, 0:DIM], patch_t[:, q, g * TC:(g + 1) * TC],
                              patch_w_sb[:, q // 2, q % 2, :], q == 0, q == QC - 1)
                last.then_inc(tok_done, 1)
                if g == 2:
                    pe.wait_ge(wt_ready, 2)
                    pe.wait_ge(base_ready, 1)
                if g >= 2:
                    hn_turn(g - 2)

            pe.wait_ge(ld_w13, 32)
            pe.wait_ge(h_ready, NC)
            for n in range(2 * MC):
                hf, m = divmod(n, MC)
                pe.wait_ge(hnt_ready, 2 * hf + 2)
                if n >= 2:
                    pe.wait_ge(u_ready, n - 1)
                for a, w in enumerate((w1_sb, w3_sb)):
                    for k in range(KC):
                        last = mm(ps[:, 4 + 2 * (n % 2) + a, 0:HALF], w[:, k, m * 128:(m + 1) * 128],
                                  hn_t[:, k, hf * HALF:(hf + 1) * HALF], k == 0, k == 1)
                    last.then_inc(up_done, 1)
                if n < 2:
                    hn_turn(NC - 2 + n)

            def spread(g):
                pe.wait_ge(hn2_ready, g + 1)
                if g >= 4:
                    pe.wait_ge(sp_ready, g - 3)
                for k in range(KC):
                    last = pe.transpose(ps[0:DC, 4 + g % 4, k * TC:(k + 1) * TC],
                                        hn[:, g, k * DC:(k + 1) * DC], ident[0:TC, 0:TC])
                last.then_inc(sp_done, 1)

            def project(hf):
                pe.wait_ge(sp_ready, 4 * hf + 4)
                for n in range(4):
                    w, m = divmod(n, 2)
                    if hf == 0:
                        pe.wait_ge(h2_ready, 5 + n)
                    else:
                        pe.wait_ge(qk_ready[w], m + 1)
                    for k in range(KC):
                        last = mm(ps[0:DC, n, 0:4 * SPAN], wqk_t[:, w, k, m * DC:(m + 1) * DC],
                                  spread_t[:, k, 4 * hf:4 * hf + 4, 0:SPAN], k == 0, k == 1)
                    last.then_inc(proj_done, 1)

            def natural(g):
                for w in range(2):
                    pe.wait_ge(qk_ready[w], 2 if g < 4 else 4)
                    if g >= 2:
                        pe.wait_ge(nat_ready[w], (g - 1) * (NP - w))
                for m in range(KC):
                    last = pe.transpose(ps[0:SPAN, 4 + 2 * (g % 2), m * DC:(m + 1) * DC], q_t[0:DC, m, g, 0:SPAN], ident[0:DC, 0:DC])
                for u in range(NP):
                    for m in range(KC):
                        last = pe.transpose(ps[0:SEQ, 5 + 2 * (g % 2), u * DIM + m * DC:u * DIM + (m + 1) * DC],
                                            k_t[:, m, g, u * LANE:u * LANE + SEQ], ident[0:DC, 0:DC])
                last.then_inc(nat_done, 1)

            pe.wait_ge(ld_w2, 16)
            pe.wait_ge(hnt_ready, 4)
            for g in range(NC):
                if g >= 4:
                    pe.wait_ge(h2_ready, g - 3)
                pe.wait_ge(u_ready, MC if g < 4 else 2 * MC)
                for m in range(MC):
                    last = mm(ps[0:TC, g % 4, 0:DIM], u_t[:, m, g * TC:(g + 1) * TC], w2_sb[:, m], m == 0, m == MC - 1)
                last.then_inc(down_done, 1)
                if g == 2:
                    pe.wait_ge(u_ready, 2 * MC)
                if g >= 2:
                    spread(g - 2)
            project(0)
            spread(NC - 2)
            spread(NC - 1)
            pe.wait_ge(sp_ready, NC)
            natural(0)
            project(1)
            for g in range(1, NAT_FIRST):
                natural(g)

            def scores(g):
                pe.wait_ge(kexp_ready, g + 1)
                if g >= 1:
                    pe.wait_ge(sub_ready, g)
                for m in range(KC):
                    for u in range(NP):
                        rows = LANE if u == 0 else SEQ
                        last = mm(ps[u * LANE:u * LANE + rows, m, 0:HC * SEQ], q_t[:, m, g, u * LANE:u * LANE + rows],
                                  k_exp[:, g % 2, m, u].rearrange("p h s -> p (h s)"))
                last.then_inc(s_done, 1)

            def flip(g, s):
                if s == 0:
                    if g >= 1:
                        pe.wait_ge(et_ready, 3 * g)
                elif s == 1:
                    if g >= 2:
                        pe.wait_ge(h3_ready, g - 1)
                else:
                    pe.wait_ge(et_ready, 3 * g + 1)
                for a in range(4):
                    m, hd = divmod(4 * s + a, HC)
                    last = pe.transpose(ps[0:SEQ, 2 + s % 2, a * SPAN:(a + 1) * SPAN], e_sb[:, g % 2, m, hd, :],
                                        ident[0:SPAN, 0:SPAN])
                last.then_inc(et_done, 1)

            def weighted(g, w):
                kind, u = divmod(w, NP)
                n = 4 * g + w
                if n >= 2:
                    pe.wait_ge(vu_ready, n - 1)
                if kind == 1:
                    pe.wait_ge(et_ready, 3 * g + 3)
                for m in range(KC):
                    bank = 4 + 2 * (n % 2) + m
                    if kind == 0:
                        last = mm(ps[0:DC, bank, 0:HC * SEQ], q_n[:, g, u, m * DC:(m + 1) * DC],
                                  e_sb[:, g % 2, m].rearrange("p h s -> p (h s)"))
                    else:
                        rhs = e_t[:].rearrange("p s a q -> p (s a) q")[:, m * HC:(m + 1) * HC, u * LANE:u * LANE + SEQ]
                        last = mm(ps[0:DC, bank, 0:HC * SEQ], k_n[:, g, u, m * DC:(m + 1) * DC], rhs)
                last.then_inc(f_done, 1)

            def gradient(g):
                pe.wait_ge(vu_ready, 4 * g + 4)
                pe.wait_ge(et_ready, min(3 * g + 5, 3 * NC))
                for i, (kind, m) in enumerate(((0, 0), (0, 1), (1, 0), (1, 1))):
                    last = mm(ps[0:TC, 3, 0:DIM], vu_t[:, g % 2, kind, m].rearrange("p a s -> p (a s)"),
                              wqk_sb[:, 1 - kind, m], i == 0, i == 3)
                last.then_inc(t_done, 1)

            for w in range(2):
                pe.wait_ge(qk_ready[w], 4)
            pe.wait_ge(pad_zero, 5)
            scores(0)
            for g in range(NAT_FIRST, NC):
                natural(g)
            for w in range(2):
                pe.wait_ge(nat_ready[w], NC * (NP - w))
            for g in range(NC):
                if g + 1 < NC:
                    scores(g + 1)
                pe.wait_ge(norm_ready, g + 1)
                flip(g, 0)
                flip(g, 1)
                weighted(g, 0)
                flip(g, 2)
                weighted(g, 1)
                if g >= 1:
                    gradient(g - 1)
                weighted(g, 2)
                weighted(g, 3)
            gradient(NC - 1)

            pe.wait_ge(vu_ready, 4 * NC)
            for g in range(NC):
                pe.wait_ge(xn_ready, g + 1)
                if g >= 4:
                    pe.wait_ge(xnt_ready, g - 3)
                for k in range(KC):
                    last = pe.transpose(ps[0:DC, 4 + g % 4, k * TC:(k + 1) * TC],
                                        hn[:, g, k * DC:(k + 1) * DC], ident[0:TC, 0:TC])
                last.then_inc(xnt_done, 1)
            pe.wait_ge(ld_router, 80)
            RW = GROUPS + ALL_E
            for g in range(NC):
                pe.wait_ge(xnt_ready, g + 1)
                for k in range(KC):
                    last = mm(ps[0:TC, 0, g * RW:(g + 1) * RW], hn_t[:, k, g * TC:(g + 1) * TC], wr_sb[:, k], k == 0, k == 1)
            last.then_inc(logit_done, 1)
            pe.wait_ge(sel_ready, 1)
            for g in range(NC):
                for b in range(g + 1):
                    mm(ps[0:TC, 1, g * ALL_E:(g + 1) * ALL_E], (earlier_bf if b == g else ones_bf)[:], sel_bf[:, b], b == 0, b == g)
            for b in range(NC):
                last = mm(ps[0:TC, 1, NC * ALL_E:(NC + 1) * ALL_E], ones_bf[:], sel_bf[:, b], b == 0, b == NC - 1)
            last.then_inc(rank_done, 1)
            pe.wait_ge(owner_ready, 1)
            mm(ps[0:1, 2, 0:TABLE], owner[:], ident[0:TABLE, 0:TABLE]).then_inc(owner_done, 1)

            def make_list(tile_no, u):
                pe.wait_ge(place_ready, tile_no + 1)
                for b in range(NC):
                    last = mm(ps[:, 4 + u, 0:LIST_W], place[:, u, b], list_col[:, u, b], b == 0, b == NC - 1)
                last.then_inc(list_done, 1)

            def turn(u):
                for k in range(KC):
                    last = pe.transpose(ps[0:DC, 4 + u, k * SLOTS:(k + 1) * SLOTS], xg[:, u, k * DC:(k + 1) * DC], ident)
                last.then_inc(xt_done, 1)

            def up(u):
                for m in range(MC):
                    o = ps[:, 2 * u + m // 4, (m % 4) * SLOTS:(m % 4 + 1) * SLOTS]
                    mm(o, ew1_sb[0:DC, u, 0, m * 128:(m + 1) * 128], xt[0:DC, u, 0], True, False)
                    last = mm(o, ew1_sb[:, u, 1, m * 128:(m + 1) * 128], xt[:, u, 1], False, True)
                    if m in (3, MC - 1):
                        last.then_inc(mm1_done, 1)

            def down(u):
                for m in range(MC):
                    last = mm(ps[:, 6 + u, 0:DIM], ht[:, u, m], ew2_sb[:, u, m], m == 0, m == MC - 1)
                last.then_inc(mm2_done, 1)

            make_list(0, 0)
            make_list(1, 1)
            pe.wait_ge(fetch_ready, 1)
            pe.wait_ge(xg_ready[0], 16)
            turn(0)
            pe.wait_ge(xt_ready, 1)
            make_list(2, 0)
            pe.wait_ge(fetch_ready, 2)
            pe.wait_ge(xg_ready[1], 16)
            turn(1)
            pe.wait_ge(ew1_ready[0], 32)
            up(0)
            n = pe.value_load(table[0:1, TABLE:TABLE + 1], min_val=0, max_val=TILES)
            with pe.Fori(0, TILES // RING) as q:
                for half in range(2):
                    with pe.If(q * RING + 2 * half < n):
                        for j in (2 * half, 2 * half + 1):
                            t = q * RING + j
                            pe.wait_ge(xt_ready, t + 2)
                            make_list(t + 3, ring_pos(j, 3, 2))
                            pe.wait_ge(fetch_ready, t + 3)
                            pe.wait_ge(xg_ready[ring_pos(j, 2, 2)], q * 32 + 16 * ((j + 2) // 2 + 1))
                            turn(ring_pos(j, 2, 2))
                            u = ring_pos(j, 1, 2)
                            pe.wait_ge(ew1_ready[u], q * 64 + 32 * ((j + 1) // 2 + 1))
                            up(u)
                            u = ring_pos(j, 0, 2)
                            pe.wait_ge(ht_ready, t * 2 + 2)
                            pe.wait_ge(ew2_ready[u], q * 32 + 16 * (j // 2 + 1))
                            pe.wait_ge(o_ready, t + 1)
                            down(u)
            pe.wait_ge(comb_ready, 1)
            pe.wait_ge(tiles_over, 2)
            for g in range(NC):
                last = pe.transpose(ps[0:ALL_E, 4 + g // 4, (g % 4) * TC:(g % 4 + 1) * TC],
                                    comb[:, g].rearrange("p g e -> p (g e)"), ident[0:TC, 0:TC])
            last.then_inc(combt_done, 1)
            pe.wait_ge(combt_ready, 2)
            pe.wait_ge(ld_b2, 16)
            for g in range(NC):
                if g >= 4:
                    pe.wait_ge(total_ready, g - 3)
                mm(ps[0:TC, g % 4, 0:DIM], comb_t[:, g * TC:(g + 1) * TC], b2_sb[:]).then_inc(b2_done, 1)

        @block.scalar
        def _(act):
            act.sem_inc(o_ready, 2)
            act.wait_ge(ld_pixels, 16 * BATCH)
            cut(act.copy, 0)
            act.wait_ge(pos_sub, 1)
            act.activation(pos_e[:], pos_e[:], ACT.Exp, scale=HEAD_DIM ** -0.5).then_inc(pos_exp, 1)
            for n in range(12):
                q, r = divmod(n, 2)
                j0, j1 = (0, 4) if r == 0 else (4, SIDE)
                act.wait_ge(px_done, n + 1)
                act.copy(patch_t[:, q].rearrange("p (b j) -> p j b", j=SIDE)[:, j0:j1],
                         ps[:, 4 + n % 4, 0:(j1 - j0) * ROWS].rearrange("p (j b) -> p j b", b=ROWS)).then_inc(px_ready, 1)
            def deviation(g, norm):
                act.wait_ge(var_ready, norm * NC + g + 1)
                act.activation(std[:, g:g + 1], mv[:, g, 1:2], ACT.Sqrt, bias=c("eps", TC)).then_inc(std_ready, 1)

            act.wait_ge(wt_done, 1)
            for w in range(2):
                act.copy(wqk_t[:, w].rearrange("p k n -> p (k n)"), ps[0:DC, 2 + w, 0:KC * DIM]).then_inc(wt_ready, 1)
            for g in range(NC):
                deviation(g, 0)

            for n in range(2 * MC):
                act.wait_ge(up_done, 2 * n + 1)
                if n >= 2:
                    act.wait_ge(u_ready, n - 1)
                act.activation(silu_sb[:, n % 2], ps[:, 4 + 2 * (n % 2), 0:HALF], ACT.Silu).then_inc(silu_ready, 1)
            def spread(g):
                act.wait_ge(sp_done, g + 1)
                act.copy(spread_t[:, :, g].rearrange("p k (a s) -> p k a s", a=NP)[:, :, :, 0:SEQ],
                         ps[0:DC, 4 + g % 4, 0:KC * TC].rearrange("p (k a s) -> p k a s", k=KC, a=NP)).then_inc(sp_ready, 1)

            def project(hf):
                for m in range(KC):
                    act.wait_ge(proj_done, 4 * hf + m + 1)
                    act.copy(q_t[0:DC, m, 4 * hf:4 * hf + 4, 0:SPAN],
                             ps[0:DC, m, 0:4 * SPAN].rearrange("p (g s) -> p g s", g=4)).then_inc(qk_ready[0], 1)

            def natural(g):
                act.wait_ge(nat_done, g + 1)
                for u, rows in enumerate((slice(0, LANE), slice(LANE, SPAN))):
                    act.copy(q_n[rows, g, u], ps[rows, 4 + 2 * (g % 2), 0:DIM]).then_inc(nat_ready[0], 1)

            act.wait_ge(sp_zero, 1)
            act.wait_ge(pad_zero, 5)
            for g in range(NC):
                deviation(g, 1)
                if g >= 2:
                    spread(g - 2)
            project(0)
            spread(NC - 2)
            spread(NC - 1)
            natural(0)
            project(1)
            for g in range(1, NAT_FIRST):
                natural(g)

            def exp(g):
                act.wait_ge(sub_ready, g + 1)
                act.activation(e_sb[:, g % 2], e_sb[:, g % 2], ACT.Exp).then_inc(exp_ready, 1)

            def even_heads(g, w):
                kind, u = divmod(w, NP)
                n = 4 * g + w
                act.wait_ge(f_done, n + 1)
                if w == 0 and g >= 2:
                    act.wait_ge(t_done, g - 1)
                for b in range(HC // 2):
                    rows = slice(b * 32, b * 32 + 32)
                    act.activation(vu_t[rows, g % 2, kind, :, u, :],
                                   ps[rows, 4 + 2 * (n % 2):6 + 2 * (n % 2), 2 * b * SEQ:(2 * b + 1) * SEQ],
                                   ACT.Copy, scale=headmask[rows, 2 * b:2 * b + 1]).then_inc(even_ready, 1)

            def turned(g, s):
                act.wait_ge(et_done, 3 * g + s + 1)
                if g >= 1 and s == 0:
                    act.wait_ge(f_done, 4 * g)
                act.copy(e_t[0:SEQ, s].rearrange("p a q -> p (a q)"), ps[0:SEQ, 2 + s % 2, 0:4 * SPAN]).then_inc(et_ready, 1)

            exp(0)
            for g in range(NAT_FIRST, NC):
                natural(g)
            for g in range(NC):
                turned(g, 0)
                turned(g, 1)
                if g + 1 < NC:
                    exp(g + 1)
                even_heads(g, 0)
                turned(g, 2)
                even_heads(g, 1)
                even_heads(g, 2)
                even_heads(g, 3)

            act.wait_ge(var_ready, 3 * NC)
            act.activation(std[:], mv[:, :, 1], ACT.Sqrt, bias=c("eps", TC)).then_inc(std_ready, 1)
            for g in range(NC):
                act.wait_ge(xnt_done, g + 1)
                act.copy(hn_t[:, :, g * TC:(g + 1) * TC],
                         ps[0:DC, 4 + g % 4, 0:KC * TC].rearrange("p (k t) -> p k t", k=KC)).then_inc(xnt_ready, 1)
            act.wait_ge(logit_ready, 2)
            act.activation(gate_g[:], gate_g[:], ACT.Exp).then_inc(gexp_ready, 1)
            act.activation(gate_e[:], gate_e[:], ACT.Exp).then_inc(gexp_ready, 1)

            def gelu(tile2, u):
                act.wait_ge(mm1_done, tile2 + 1)
                act.activation(ht[:, u, 0:4].rearrange("p m s -> p (m s)"), ps[:, 2 * u, 0:4 * SLOTS], ACT.Gelu).then_inc(ht_ready, 1)
                act.wait_ge(mm1_done, tile2 + 2)
                act.activation(ht[:, u, 4:MC].rearrange("p m s -> p (m s)"), ps[:, 2 * u + 1, 0:(MC - 4) * SLOTS], ACT.Gelu).then_inc(ht_ready, 1)

            act.wait_ge(table_ready, 1)
            gelu(0, 0)
            n = act.value_load(table[0:1, TABLE:TABLE + 1], min_val=0, max_val=TILES)
            with act.Fori(0, TILES // RING) as q:
                for half in range(2):
                    with act.If(q * RING + 2 * half < n):
                        for j in (2 * half, 2 * half + 1):
                            t = q * RING + j
                            gelu(t * 2 + 2, ring_pos(j, 1, 2))
                            u = ring_pos(j, 0, 2)
                            act.wait_ge(mm2_done, t + 1)
                            act.wait_ge(meta_ready, t + 1)
                            act.wait_ge(o_free[u], q * 32 + 16 * (j // 2 + 1))
                            act.activation(o_sb[:, u], ps[:, 6 + u, 0:DIM], ACT.Copy,
                                           scale=gate[:, ring_pos(j, 0, RING):ring_pos(j, 0, RING) + 1]).then_inc(o_ready, 1)
            act.copy(std[:, 0:1], rstd[:, 0:1]).then_inc(tiles_over, 1)

        @block.gpsimd
        def _(pool):
            pool.memset(spread_t[:], 0.0).then_inc(sp_zero, 1)
            pool.memset(xt[DC:DC + 1], 1.0).then_inc(sp_zero, 1)

            pool.wait_ge(sp_zero, 2)
            pool.wait_ge(ld_pixels, 16 * BATCH)
            cut(pool.tensor_copy, 1)
            cut(pool.tensor_copy, 2)
            pool.wait_ge(cut_ready[1], 1)
            pool.wait_ge(cut_ready[2], 1)
            pool.wait_ge(px_done, 12)
            pool.wait_ge(base_done, 1)
            pool.memset(q_n[:], 0.0).then_inc(pad_zero, 1)
            pool.memset(k_n[:], 0.0).then_inc(pad_zero, 1)
            pool.memset(e_t[:], 0.0).then_inc(pad_zero, 1)
            pool.wait_ge(pad_zero, 3)
            pool.memset(q_t[DC:ROWS_FULL], 0.0).then_inc(pad_zero, 1)
            pool.memset(k_exp[DC:ROWS_FULL], 0.0).then_inc(pad_zero, 1)
            pool.wait_ge(pad_zero, 5)

            def expand(g):
                pool.wait_ge(qk_ready[1], 2 if g < 4 else 4)
                if g >= 2:
                    pool.wait_ge(s_done, g - 1)
                for m in range(KC):
                    for u in range(NP):
                        shape = [DC, HC, SEQ]
                        last = pool.tensor_tensor(k_exp[0:DC, g % 2, m, u],
                                                  k_t[:, m, g, u * LANE:u * LANE + SEQ].unsqueeze(1).to_broadcast(shape),
                                                  beta_mask[:, m].unsqueeze(2).to_broadcast(shape), ALU.mult)
                last.then_inc(kexp_ready, 1)

            pool.wait_ge(bm_ready, 1)
            expand(0)
            expand(1)
            for g in range(2, NC):
                expand(g)

            def gather(u):
                pool.indirect_dma_start(xg[:, u], None, xn_dram, bass.IndirectOffsetOnAxis(fetch[:, u:u + 1], 0)).then_inc(xg_ready[u], 16)

            pool.wait_ge(xn_stored, 16 * NC)
            pool.wait_ge(fetch_ready, 1)
            for u in range(2):
                pool.dma_start(o_sb[:, u], consts[:, 0:DIM]).then_inc(o_free[u], 16)
            gather(0)
            pool.wait_ge(fetch_ready, 2)
            gather(1)
            pool.wait_ge(fetch_ready, 3)
            pool.wait_ge(xt_done, 1)
            gather(0)
            pool.wait_ge(table_ready, 1)
            def hold():
                pool.sem_inc(pool_turns, 1)

            n = pool.value_load(table[0:1, TABLE:TABLE + 1], min_val=0, max_val=TILES)
            with pool.Fori(0, TILES // RING) as q:
                for half in range(2):
                    with pool.If(q * RING + 2 * half < n):
                        for j in (2 * half, 2 * half + 1):
                            t = q * RING + j
                            pool.wait_ge(fetch_ready, t + 4)
                            pool.wait_ge(xt_done, t + 2)
                            hold()
                            gather(ring_pos(j, 3, 2))
                            u = ring_pos(j, 0, 2)
                            r = ring_pos(j, 0, RING)
                            pool.wait_ge(o_ready, t + 3)
                            hold()
                            pool.indirect_dma_start(picks_dram, bass.IndirectOffsetOnAxis(store[:, r:r + 1], 0),
                                                    o_sb[:, u], None).then_inc(o_free[u], 16)
            for u in range(2):
                pool.wait_ge(xg_ready[u], 16)

        @block.vector
        def _(dve):
            count = [0]

            def link(ins):
                count[0] += 1
                ins.then_inc(dve_chain, 1)
                dve.wait_ge(dve_chain, count[0])

            def moments(g, ready):
                dve.wait_ge(ready, g + 1)
                link(dve.bn_stats(stats[:, g], h[:, g]))
                dve.bn_aggr(mv[:, g], stats[:, g]).then_inc(var_ready, 1)

            def normalise(g, norm):
                if norm < 2:
                    dve.wait_ge(std_ready, norm * NC + g + 1)
                    link(dve.reciprocal(rstd[:, g:g + 1], std[:, g:g + 1]))
                return dve.tensor_scalar(hn[:, g], h[:, g], mv[:, g, 0:1], rstd[:, g:g + 1], ALU.subtract, ALU.mult)

            dve.memset(wqkv_sb[DC:DC + 1, 0, :], 0.0).then_inc(rep_ready, 1)
            dve.wait_ge(rep_ready, 1)
            dve.wait_ge(ld_qkv, 32)
            for k in range(KC):
                shape = [DC + 1, 2, HC, HEAD_DIM]
                dve.tensor_copy(wkv_rep[:, k], wqkv_sb[:, k, DIM:].rearrange("p (v d) -> p v d", v=2).unsqueeze(2)
                                .to_broadcast(shape)).then_inc(rep_ready, 1)
            dve.wait_ge(ld_const, 16)
            dve.wait_ge(pos_proj, 1)
            dve.tensor_copy(pos_qt[:], ps[0:DC, 0, 0:KC * SEQ].rearrange("p (k s) -> p k s", k=KC)).then_inc(pos_in, 1)
            shape = [DC, HC, SEQ]
            dve.tensor_tensor(pos_kexp[:], ps[0:DC, 0, 2 * SEQ:3 * SEQ].unsqueeze(1).to_broadcast(shape),
                              headmask.unsqueeze(2).to_broadcast(shape), ALU.mult).then_inc(pos_in, 1)
            dve.tensor_copy(pos_v[:], ps[0:SEQ, 1, 0:DC]).then_inc(pos_in, 1)
            dve.wait_ge(pos_s, 1)
            shape = [SEQ, HC, SEQ]
            for m in range(KC):
                last = dve.tensor_tensor(pos_e[:, m * HC:(m + 1) * HC], ps[0:SEQ, 2 + m, 0:HC * SEQ].rearrange("p (h s) -> p h s", h=HC),
                                         c("causal", SEQ).unsqueeze(1).to_broadcast(shape), ALU.add)
                link(last)
            shape = [SEQ, HEADS, SEQ]
            link(dve.tensor_reduce(pos_max[:, 0], pos_e[:], X, ALU.max))
            dve.tensor_tensor(pos_e[:], pos_e[:], pos_max[:, 0].unsqueeze(2).to_broadcast(shape), ALU.subtract).then_inc(pos_sub, 1)
            dve.wait_ge(pos_exp, 1)
            link(dve.tensor_reduce(pos_max[:, 1], pos_e[:], X, ALU.add))
            link(dve.reciprocal(pos_max[:, 0], pos_max[:, 1]))
            dve.tensor_tensor(pos_e[:], pos_e[:], pos_max[:, 0].unsqueeze(2).to_broadcast(shape), ALU.mult).then_inc(pos_norm, 1)
            dve.wait_ge(pos_tr, 1)
            dve.tensor_copy(pos_et[:], ps[0:SEQ, 0:KC, 0:HC * SEQ]).then_inc(pos_et_ready, 1)
            dve.wait_ge(pos_f_done, 1)
            for m in range(KC):
                link(dve.tensor_tensor(pos_f[:, m], ps[0:DC, 2 + m, 0:HC * SEQ].rearrange("p (h s) -> p h s", h=HC),
                                       headmask.unsqueeze(2).to_broadcast([DC, HC, SEQ]), ALU.mult))
            for m in range(KC):
                link(dve.tensor_reduce(pos_ot[:, m], pos_f[:, m].rearrange("p h s -> p s h"), X, ALU.add))
            dve.tensor_copy(pos_ot2[:], pos_ot[:].unsqueeze(2).to_broadcast([DC, KC, NP, SEQ])).then_inc(pos_o_ready, 1)
            dve.wait_ge(base_done, 1)
            dve.tensor_copy(base[:], ps[0:TC, 0, 0:DIM]).then_inc(base_ready, 1)
            dve.wait_ge(base_ready, 1)
            def affine(hf):
                dve.wait_ge(ld_ln, 32)
                dve.wait_ge(hnt_done, 4 * hf + 4)
                for k in range(KC):
                    dve.tensor_scalar(hn_t[:, k, hf * HALF:(hf + 1) * HALF], ps[0:DC, k + 2 * hf, 0:HALF],
                                      ln_gb[:, 0, k:k + 1], ln_gb[:, 1, k:k + 1], ALU.mult, ALU.add).then_inc(hnt_ready, 1)

            for g in range(NC):
                dve.wait_ge(tok_done, g + 1)
                dve.tensor_tensor(h[:, g], ps[0:TC, 4 + g % 4, 0:DIM], base[:], ALU.add).then_inc(h_ready, 1)
                moments(g, h_ready)
                if g >= 1:
                    normalise(g - 1, 0).then_inc(hn_ready, 1)
                if g == NC - 2:
                    affine(0)
            normalise(NC - 1, 0).then_inc(hn_ready, 1)
            affine(1)

            for n in range(2 * MC):
                hf, m = divmod(n, MC)
                dve.wait_ge(silu_ready, n + 1)
                dve.wait_ge(up_done, 2 * n + 2)
                dve.tensor_tensor(u_t[:, m, hf * HALF:(hf + 1) * HALF], silu_sb[:, n % 2],
                                  ps[:, 5 + 2 * (n % 2), 0:HALF], ALU.mult).then_inc(u_ready, 1)
            for g in range(NC):
                dve.wait_ge(down_done, g + 1)
                dve.tensor_tensor(h[:, g], h[:, g], ps[0:TC, g % 4, 0:DIM], ALU.add).then_inc(h2_ready, 1)
                moments(g, h2_ready)
                if g >= 1:
                    normalise(g - 1, 1).then_inc(hn2_ready, 1)
            normalise(NC - 1, 1).then_inc(hn2_ready, 1)
            dve.wait_ge(ld_beta, 16)
            dve.tensor_tensor(beta_mask[:], beta_bc[:].rearrange("p (k h) -> p k h", k=KC),
                              headmask.unsqueeze(1).to_broadcast([DC, KC, HC]), ALU.mult).then_inc(bm_ready, 1)

            dve.wait_ge(pad_zero, 5)

            def project(hf):
                for m in range(KC):
                    dve.wait_ge(proj_done, 4 * hf + 2 + m + 1)
                    dve.tensor_copy(k_t[:, m, 4 * hf:4 * hf + 4, 0:SPAN],
                                    ps[0:DC, 2 + m, 0:4 * SPAN].rearrange("p (g s) -> p g s", g=4)).then_inc(qk_ready[1], 1)

            def natural(g):
                dve.wait_ge(nat_done, g + 1)
                dve.tensor_copy(k_n[0:SEQ, g].rearrange("p a n -> p (a n)"), ps[0:SEQ, 5 + 2 * (g % 2), 0:NP * DIM]).then_inc(nat_ready[1], 1)

            project(0)
            natural(0)
            project(1)
            for g in range(1, NAT_FIRST):
                natural(g)

            def shift(g):
                dve.wait_ge(s_done, g + 1)
                if g >= 2:
                    dve.wait_ge(f_done, 4 * g - 6)
                s = ps[0:SPAN, 0:KC, 0:HC * SEQ].rearrange("p k (h s) -> p k h s", h=HC)
                mx = e_max[:].rearrange("p (k h) -> p k h", k=KC)
                link(dve.tensor_reduce(mx, s, X, ALU.max))
                for m in range(KC):
                    last = dve.tensor_tensor(e_sb[:, g % 2, m], s[:, m], mx[:, m].unsqueeze(2).to_broadcast([SPAN, HC, SEQ]), ALU.subtract)
                last.then_inc(sub_ready, 1)

            def odd_heads(g, w):
                kind, u = divmod(w, NP)
                n = 4 * g + w
                for b in range(HC // 2):
                    dve.wait_ge(even_ready, (HC // 2) * n + b + 1)
                    rows = slice(b * 32, b * 32 + 32)
                    o = vu_t[rows, g % 2, kind, :, u, :]
                    last = dve.scalar_tensor_tensor(out=o, in0=ps[rows, 4 + 2 * (n % 2):6 + 2 * (n % 2), (2 * b + 1) * SEQ:(2 * b + 2) * SEQ],
                                                    scalar=headmask[rows, 2 * b + 1:2 * b + 2], in1=o, op0=ALU.mult, op1=ALU.add)
                last.then_inc(vu_ready, 1)

            def residual(g):
                dve.wait_ge(t_done, g + 1)
                dve.tensor_tensor(h[:, g], h[:, g], ps[0:TC, 3, 0:DIM], ALU.add).then_inc(h3_ready, 1)
                moments(g, h3_ready)

            def norm(g):
                dve.wait_ge(exp_ready, g + 1)
                dve.wait_ge(sub_ready, g + 1)
                e_flat = e_sb[:, g % 2].rearrange("p k h s -> p (k h) s")
                link(dve.tensor_reduce(e_max[:], e_flat, X, ALU.add))
                link(dve.reciprocal(e_rz[:, g % 2], e_max[:]))
                dve.tensor_tensor(e_flat, e_flat, e_rz[:, g % 2].unsqueeze(2).to_broadcast([SPAN, HEADS, SEQ]),
                                  ALU.mult).then_inc(norm_ready, 1)

            shift(0)
            for g in range(NAT_FIRST, NC):
                natural(g)
            norm(0)
            for g in range(NC):
                if g + 1 < NC:
                    shift(g + 1)
                odd_heads(g, 0)
                odd_heads(g, 1)
                if g + 1 < NC:
                    norm(g + 1)
                if g >= 1:
                    residual(g - 1)
                odd_heads(g, 2)
                odd_heads(g, 3)
            residual(NC - 1)

            dve.wait_ge(std_ready, 2 * NC + 1)
            link(dve.reciprocal(rstd[:], std[:]))
            for g in range(NC):
                normalise(g, 2).then_inc(xn_ready, 1)

            for k, v in ((earlier_bf, "earlier"), (ones_bf, "ones")):
                link(dve.tensor_copy(k[:], c(v, TC)[:, 0:TC]))
            link(dve.memset(zeros[:], 0.0))
            link(dve.memset(list_src[:], 0.0))
            link(dve.tensor_copy(list_src[:, :, :, 0:3], c("token", TC).rearrange("p (c w) -> p c w", w=3).unsqueeze(1)
                                 .to_broadcast([TC, ALL_E, NC, 3])))
            RW = GROUPS + ALL_E
            dve.wait_ge(ld_router, 80)
            dve.wait_ge(logit_done, 1)
            raw = ps[0:TC, 0, 0:NC * RW].rearrange("p (c w) -> p c w", w=RW)
            link(dve.tensor_tensor(logit_g[:], raw[:, :, 0:GROUPS], rb_sb[:, 0:GROUPS].unsqueeze(1).to_broadcast([TC, NC, GROUPS]), ALU.add))
            link(dve.tensor_tensor(logit_e[:].rearrange("p c g e -> p c (g e)"), raw[:, :, GROUPS:],
                                   rb_sb[:, GROUPS:].unsqueeze(1).to_broadcast([TC, NC, ALL_E]), ALU.add))
            link(dve.tensor_reduce(red_g[:], logit_g[:], X, ALU.max))
            link(dve.tensor_reduce(red_e[:], logit_e[:], X, ALU.max))
            dve.tensor_tensor(gate_g[:], logit_g[:], red_g[:].unsqueeze(2).to_broadcast([TC, NC, GROUPS]), ALU.subtract).then_inc(logit_ready, 1)
            dve.tensor_tensor(gate_e[:], logit_e[:], red_e[:].unsqueeze(3).to_broadcast([TC, NC, GROUPS, EXPERTS]), ALU.subtract).then_inc(logit_ready, 1)

            def rank(values, n, sets, tie, out_):
                shape = [TC, sets, n, n]
                other, own = values.unsqueeze(2).to_broadcast(shape), values.unsqueeze(3).to_broadcast(shape)
                a = cmp_a[:].rearrange("p s i j -> p (s i j)")[:, 0:sets * n * n].rearrange("p (s i j) -> p s i j", i=n, j=n)
                b = cmp_b[:].rearrange("p s i j -> p (s i j)")[:, 0:sets * n * n].rearrange("p (s i j) -> p s i j", i=n, j=n)
                link(dve.tensor_tensor(a, other, own, ALU.is_equal))
                link(dve.tensor_tensor(a, a, tie.rearrange("p (i j) -> p i j", i=n).unsqueeze(1).to_broadcast(shape), ALU.mult))
                link(dve.tensor_tensor(b, other, own, ALU.is_gt))
                link(dve.tensor_tensor(a, a, b, ALU.add))
                link(dve.tensor_reduce(out_, a, X, ALU.add))

            rank(logit_g[:], GROUPS, NC, c("tie_g", TC), rank_g[:])
            rank(logit_e[:].rearrange("p c g e -> p (c g) e"), EXPERTS, NC * GROUPS, c("tie_e", TC),
                 rank_e[:].rearrange("p c g e -> p (c g) e"))
            link(dve.tensor_scalar(sel_g[:], rank_g[:], float(TOP_G), None, ALU.is_lt))
            wide = [TC, NC, GROUPS, EXPERTS]
            rank_flat = rank_e[:].rearrange("p c g e -> p (c g) e")
            link(dve.scalar_tensor_tensor(out=sel[:].rearrange("p c g e -> p (c g) e"), in0=rank_flat, scalar=float(TOP_E),
                                          in1=sel_g[:].rearrange("p c g -> p (c g)").unsqueeze(2).to_broadcast([TC, NC * GROUPS, EXPERTS]),
                                          op0=ALU.is_lt, op1=ALU.mult))
            dve.tensor_copy(sel_bf[:], sel[:].rearrange("p c g e -> p c (g e)")).then_inc(sel_ready, 1)
            dve.wait_ge(gexp_ready, 2)
            link(dve.tensor_tensor(gate_g[:], gate_g[:], sel_g[:], ALU.mult))
            link(dve.scalar_tensor_tensor(out=gate_e[:].rearrange("p c g e -> p (c g e)"), in0=rank_e[:].rearrange("p c g e -> p (c g e)"),
                                          scalar=float(TOP_E), in1=gate_e[:].rearrange("p c g e -> p (c g e)"), op0=ALU.is_lt, op1=ALU.mult))
            link(dve.tensor_reduce(red_g[:], gate_g[:], X, ALU.add))
            link(dve.tensor_reduce(red_e[:], gate_e[:], X, ALU.add))
            link(dve.reciprocal(red_g[:], red_g[:]))
            link(dve.reciprocal(red_e[:], red_e[:]))
            link(dve.tensor_tensor(gate_g[:], gate_g[:], red_g[:].unsqueeze(2).to_broadcast([TC, NC, GROUPS]), ALU.mult))
            link(dve.tensor_tensor(gate_e[:], gate_e[:], red_e[:].unsqueeze(3).to_broadcast(wide), ALU.mult))
            for v in (gate_g[:].rearrange("p c g -> p (c g)"), gate_e[:].rearrange("p c g e -> p (c g e)")):
                link(dve.scalar_tensor_tensor(out=v, in0=v, scalar=GATE_EPS, in1=v, op0=ALU.is_ge, op1=ALU.mult))
            link(dve.tensor_tensor(comb[:], gate_e[:], gate_g[:].unsqueeze(3).to_broadcast(wide), ALU.mult))
            comb_v = comb[:].rearrange("p c g e -> p c (g e)")
            rest = gate_tmp[:].rearrange("p c g e -> p c (g e)")
            part = [list_src[:, :, :, w].rearrange("p e c -> p c e") for w in range(LIST_W)]
            link(dve.tensor_copy(part[4], comb_v))
            link(dve.tensor_tensor(rest, comb_v, part[4], ALU.subtract))
            link(dve.tensor_copy(part[5], rest))
            link(dve.tensor_tensor(rest, rest, part[5], ALU.subtract))
            dve.tensor_copy(part[6], rest).then_inc(comb_ready, 1)
            sel_v = sel[:].rearrange("p c g e -> p c (g e)")
            flat = "p c e -> p (c e)"
            link(dve.tensor_tensor_scan(order[:].rearrange(flat), zeros[:], sel_v.rearrange(flat), 0.0, ALU.add, ALU.add))
            link(dve.tensor_tensor(order[:], order[:], sel_v, ALU.subtract))
            link(dve.tensor_tensor(part[3], order[:], c("picked", TC).unsqueeze(2).to_broadcast([TC, NC, ALL_E]), ALU.subtract))
            dve.wait_ge(rank_done, 1)
            shape = [TC, ALL_E, MAX_STEPS]
            link(dve.tensor_tensor(tile_cmp[:], ps[0:TC, 1, NC * ALL_E:(NC + 1) * ALL_E].unsqueeze(2).to_broadcast(shape),
                                   c("steps", TC).unsqueeze(1).to_broadcast(shape), ALU.is_gt))
            link(dve.tensor_reduce(tiles_of[:], tile_cmp[:], X, ALU.add))
            link(dve.tensor_tensor_scan(tiles_end[:], zeros[:, 0:ALL_E], tiles_of[:], 0.0, ALU.add, ALU.add))
            link(dve.tensor_scalar(owner_cmp[:], tiles_end[0:TABLE], c("tile", TABLE), None, ALU.is_le))
            link(dve.tensor_reduce(owner[:], owner_cmp[:], X, ALU.add))
            dve.tensor_scalar(owner[:], owner[:], float(ALL_E - 1), None, ALU.min).then_inc(owner_ready, 1)
            link(dve.tensor_tensor(first_slot[:], tiles_end[:], tiles_of[:], ALU.subtract))
            link(dve.tensor_scalar(first_slot[:], first_slot[:], float(SLOTS), None, ALU.mult))
            link(dve.scalar_tensor_tensor(out=slot_tmp[:], in0=ps[0:TC, 1, 0:NC * ALL_E].rearrange("p (c e) -> p c e", e=ALL_E), scalar=1.0,
                                          in1=first_slot[:].unsqueeze(1).to_broadcast([TC, NC, ALL_E]), op0=ALU.add, op1=ALU.add))
            link(dve.tensor_tensor(slot_tmp[:], slot_tmp[:], sel_v, ALU.mult))
            link(dve.tensor_scalar(slot_of[:].rearrange("p e c -> p c e"), slot_tmp[:], -1.0, None, ALU.add))
            dve.wait_ge(owner_done, 1)
            link(dve.tensor_copy(table[0:1, 0:TABLE], ps[0:1, 2, 0:TABLE]))
            dve.tensor_copy(table[0:1, TABLE:TABLE + 1], tiles_end[0:1, ALL_E - 1:ALL_E]).then_inc(table_ready, 1)
            dve.wait_ge(table_ready, 1)

            def wait_small(base_count, ins, k):
                ins.then_inc(small_chain, 1)
                dve.wait_ge(small_chain, base_count + k)

            def make_place(tile_no, u, done):
                e = dve.value_load(table[0:1, bass.ds(tile_no, 1)], min_val=0, max_val=ALL_E - 1)
                a = AT["first"][0]
                wait_small(done, dve.tensor_scalar(slot_rel[:], slot_of[:, bass.ds(e, 1)].rearrange("p a c -> p (a c)"),
                                                   cst[0:TC, bass.ds(tile_no + a, 1)], None, ALU.subtract), 1)
                wait_small(done, dve.tensor_copy(list_col[:, u].rearrange("p c w -> p (c w)"),
                                                 list_src[:, bass.ds(e, 1)].rearrange("p a c w -> p (a c w)")), 2)
                shape = [TC, NC, SLOTS]
                dve.tensor_tensor(place[:, u], slot_rel[:].unsqueeze(2).to_broadcast(shape),
                                  c("slot", TC).unsqueeze(1).to_broadcast(shape), ALU.is_equal).then_inc(place_ready, 1)

            def read_list(u, done):
                l = list_sb[:, u]
                wait_small(done, dve.tensor_copy(l, ps[:, 4 + u, 0:LIST_W]), 1)
                wait_small(done, dve.scalar_tensor_tensor(out=fetch_f[:, u:u + 1], in0=l[:, 1:2], scalar=float(TC), in1=l[:, 0:1],
                                                          op0=ALU.mult, op1=ALU.add), 2)
                dve.tensor_copy(fetch[:, u:u + 1], fetch_f[:, u:u + 1]).then_inc(fetch_ready, 1)

            def read_meta(u, r, done):
                l = list_sb[:, u]
                spare = c("spare")[:, u:u + 1]
                wait_small(done, dve.scalar_tensor_tensor(out=store_f[:, u, 0:1], in0=l[:, 3:4], scalar=float(TOKENS), in1=fetch_f[:, u:u + 1],
                                                          op0=ALU.mult, op1=ALU.add), 1)
                wait_small(done, dve.scalar_tensor_tensor(out=store_f[:, u, 1:2], in0=l[:, 2:3], scalar=spare, in1=store_f[:, u, 0:1],
                                                          op0=ALU.mult, op1=ALU.subtract), 2)
                wait_small(done, dve.tensor_scalar(store[:, r:r + 1], store_f[:, u, 1:2], -1.0, spare, ALU.mult, ALU.add), 3)
                dve.scalar_tensor_tensor(out=gate[:, r:r + 1], in0=l[:, 6:7], scalar=l[:, 5:6], in1=l[:, 4:5],
                                         op0=ALU.add, op1=ALU.add).then_inc(meta_ready, 1)

            def copy_tokens(u):
                dve.tensor_copy(xt[0:DC, u], ps[0:DC, 4 + u, 0:KC * SLOTS].rearrange("p (k s) -> p k s", k=KC)).then_inc(xt_ready, 1)

            SMALL = 7
            make_place(0, 0, 0)
            dve.wait_ge(sp_zero, 2)
            for j in range(3):
                done = 2 + SMALL * j
                dve.wait_ge(list_done, j + 1)
                read_list(j % 2, done)
                if j >= 1:
                    dve.wait_ge(xt_done, j)
                    copy_tokens((j - 1) % 2)
                make_place(j + 1, (j + 1) % 2, done + 2)
                read_meta(j % 2, j, done + 4)
            n = dve.value_load(table[0:1, TABLE:TABLE + 1], min_val=0, max_val=TILES)
            with dve.Fori(0, TILES // RING) as q:
                for half in range(2):
                    with dve.If(q * RING + 2 * half < n):
                        for j in (2 * half, 2 * half + 1):
                            t = q * RING + j
                            done = q * (RING * SMALL) + (2 + SMALL * 3 + SMALL * j)
                            dve.wait_ge(list_done, t + 4)
                            read_list(ring_pos(j, 3, 2), done)
                            dve.wait_ge(xt_done, t + 3)
                            copy_tokens(ring_pos(j, 2, 2))
                            make_place(t + 4, ring_pos(j, 4, 2), done + 2)
                            dve.wait_ge(o_ready, t + 2)
                            dve.wait_ge(o_free[ring_pos(j, 1, 2)], q * 32 + 16 * ((j + 1) // 2 + 1))
                            read_meta(ring_pos(j, 3, 2), ring_pos(j, 3, RING), done + 4)

            dve.memset(zeros[:, 0:1], 0.0).then_inc(tiles_over, 1)

            dve.wait_ge(combt_done, 1)
            for a in range(2):
                dve.tensor_copy(comb_t[:, a * HALF:(a + 1) * HALF], ps[0:ALL_E, 4 + a, 0:HALF]).then_inc(combt_ready, 1)
            for g in range(NC):
                dve.wait_ge(b2_done, g + 1)
                dve.tensor_tensor(h[:, g], h[:, g], ps[0:TC, g % 4, 0:DIM], ALU.add).then_inc(total_ready, 1)
            dve.wait_ge(total_ready, NC)
            dve.wait_ge(picks_ready, 16 * NC)
            for g in range(NC):
                link(dve.tensor_reduce(total[:, g], picks[:, g].rearrange("p k d -> p d k"), X, ALU.add))
                dve.tensor_tensor(total[:, g], total[:, g], h[:, g], ALU.add).then_inc(out_ready, 1)

_INS = ["x", "L0_tok_patch_w", "L0_tok_patch_b", "L0_tok_ln_g", "L0_tok_ln_b", "L0_tok_w1", "L0_tok_w2", "L0_tok_w3",
        "L0_tok_wqkv", "L0_tok_bqkv", "L0_tok_wo", "L0_tok_bo", "L0_attn_Wq", "L0_attn_Wk", "L0_attn_betas",
        "L0_ffn_Wg", "L0_ffn_bg", "L0_ffn_We", "L0_ffn_be", "L0_ffn_W1", "L0_ffn_b1", "L0_ffn_W2", "L0_ffn_b2"]

def kernel(**inputs):
    import numpy as _np
    import concourse.bacc as _bacc
    from concourse import mybir as _mybir
    from concourse.bass_utils import run_bass_kernel_spmd as _run

    nc = _bacc.Bacc("TRN2", target_bir_lowering=False, num_devices=1)
    arrays, args = {}, []
    for name in _INS:
        a = _np.ascontiguousarray(inputs[name])
        arrays[f"in_{name}_dram"] = a
        args.append(nc.dram_tensor(f"in_{name}_dram", a.shape, _mybir.dt.from_np(a.dtype), kind="ExternalInput").ap())
    arrays["in_constants_dram"] = constants()
    args.append(nc.dram_tensor("in_constants_dram", (128, CONST_W), _mybir.dt.float32, kind="ExternalInput").ap())
    args.append(nc.dram_tensor("out_0_dram", (BATCH, SEQ, DIM), _mybir.dt.float32, kind="ExternalOutput").ap())
    vit_moe_program(nc, *args)
    r = _run(nc, [arrays], core_ids=[0])
    return r.results[0]["out_0_dram"]
```

```python
import numpy as np
from contextlib import ExitStack

import concourse.bass as bass
from concourse import mybir

BATCH, CHANNELS, IMG, PATCH = 16, 3, 112, 16
SIDE = IMG // PATCH
SEQ = SIDE * SIDE
TOKENS = BATCH * SEQ
DIM, HEADS = 192, 12
HEAD_DIM = DIM // HEADS
HIDDEN = 4 * DIM
GROUPS, EXPERTS, TOP_G, TOP_E = 4, 8, 2, 4
ALL_E = GROUPS * EXPERTS
PICKS = TOP_G * TOP_E
LN_EPS, GATE_EPS = 1e-5, 1e-6

KC = 2
DC = DIM // KC
HC = HEADS // KC
NP = 2
TC = NP * SEQ
NC = TOKENS // TC
LANE = 64
ROWS_FULL = 128
SPAN = LANE + SEQ
MC = HIDDEN // 128
HALF = TOKENS // 2
ROWS = BATCH * SIDE
QC = CHANNELS * 2

SLOTS = 128
TILES = (TOKENS * PICKS - ALL_E) // SLOTS + ALL_E
RING = 4
STEP = 8
TABLE = TILES + RING
MAX_STEPS = -(-TOKENS // SLOTS)
LIST_W = 8
RB = 2
NB = NC // RB
PE_SUMS = TOP_E - 1
OWN_SUMS = 6
RW = GROUPS + ALL_E
NAT_FIRST = 5
assert TILES % STEP == 0 and STEP % RING == 0

FIELDS = dict(ident=128, sin=KC * SEQ, earlier=TC, headmask=HC, causal=SEQ, slot=SLOTS,
              token=NC * 3, tie_e=EXPERTS * EXPERTS, tie_g=GROUPS * GROUPS, steps=MAX_STEPS, pairs=TILES // 2,
              tile=1, spare=2, restart=NC * ALL_E, first=TABLE, eps=1, ones=128)
AT, _at = {}, 0
for _name, _width in FIELDS.items():
    AT[_name] = (_at, _at + _width)
    _at += _width
CONST_W = _at

def constants():
    c = np.zeros((128, CONST_W), np.float32)

    def put(name, value):
        value = np.asarray(value, np.float32)
        value = value.reshape(value.shape[0], -1)
        a, _ = AT[name]
        c[:value.shape[0], a:a + value.shape[1]] = value

    put("ident", np.eye(128))
    scales = np.linspace(1.0, 5.0, DIM // 4)
    seq = np.linspace(-1.0, 1.0, SIDE)[:, None] * scales[None, :] * np.pi
    a = np.broadcast_to(seq[:, None, :], (SIDE, SIDE, DIM // 4))
    b = np.broadcast_to(seq[None, :, :], (SIDE, SIDE, DIM // 4))
    table = np.repeat(np.concatenate([np.sin(a), np.sin(b)], -1).reshape(SEQ, DIM // 2), 2, axis=-1)
    sin = np.zeros((DC + 1, KC, SEQ))
    sin[:DC] = table.T.reshape(KC, DC, SEQ).transpose(1, 0, 2)
    sin[DC, KC - 1] = 1.0
    put("sin", sin)
    t = np.arange(TC)
    put("earlier", t[:, None] < t[None, :])
    put("headmask", np.arange(DC)[:, None] // HEAD_DIM == np.arange(HC)[None, :])
    s = np.arange(SEQ)
    put("causal", np.where(s[:, None] >= s[None, :], 0.0, -1e30))
    put("slot", np.broadcast_to(np.arange(SLOTS), (128, SLOTS)))
    token = np.zeros((TC, NC, 3))
    token[:, :, 0] = t[:, None]
    token[:, :, 1] = np.arange(NC)[None, :]
    token[:, :, 2] = 1.0
    put("token", token)
    e, g = np.arange(EXPERTS), np.arange(GROUPS)
    put("tie_e", np.broadcast_to((e[None, :] < e[:, None]).ravel(), (128, EXPERTS ** 2)))
    put("tie_g", np.broadcast_to((g[None, :] < g[:, None]).ravel(), (128, GROUPS ** 2)))
    put("steps", np.broadcast_to(np.where(np.arange(MAX_STEPS), SLOTS * np.arange(MAX_STEPS), -1),
                                 (128, MAX_STEPS)))
    put("pairs", np.broadcast_to(2 * np.arange(1, TILES // 2 + 1), (128, TILES // 2)))
    put("tile", np.arange(128)[:, None])
    put("spare", PICKS * TOKENS + np.arange(128)[:, None] + SLOTS * np.arange(2)[None, :])
    put("restart", np.broadcast_to(np.where(np.arange(NC * ALL_E) % ALL_E == 0, -PICKS, 0) * (np.arange(NC * ALL_E) > 0), (128, NC * ALL_E)))
    put("first", np.broadcast_to(SLOTS * np.arange(TABLE), (128, TABLE)))
    put("eps", np.full((128, 1), LN_EPS))
    put("ones", np.ones((128, 128)))
    return c

def vit_moe_program(nc, x, patch_w, patch_b, ln_g, ln_b, w1, w2, w3, wqkv, bqkv, wo, bo,
                    attn_wq, attn_wk, betas, wg, bg, we, be, ew1, eb1, ew2, eb2, consts, out):
    F32, BF16, I32 = mybir.dt.float32, mybir.dt.bfloat16, mybir.dt.int32
    ALU, ACT, X = mybir.AluOpType, mybir.ActivationFunctionType, mybir.AxisListType.X

    with ExitStack() as ctx:
        def sb(name, shape, dt=F32):
            return ctx.enter_context(nc.sbuf_tensor(name, shape, dt))

        def sem(name):
            return ctx.enter_context(nc.semaphore(name))

        early = ExitStack()

        def sb_early(name, shape, dt=F32):
            return early.enter_context(nc.sbuf_tensor(name, shape, dt))

        front = ExitStack()

        def sb_front(name, shape, dt=F32):
            return front.enter_context(nc.sbuf_tensor(name, shape, dt))

        xn_dram = nc.dram_tensor("xn_dram", [TOKENS, DIM], F32, kind="Internal").ap()
        picks_dram = nc.dram_tensor("picks_dram", [PICKS * TOKENS + 2 * SLOTS, DIM], F32, kind="Internal").ap()

        cst = sb("cst", [128, CONST_W])
        wqk_sb = sb("wqk_sb", [DC, 2, KC, DIM])
        wqk_t = sb("wqk_t", [DC, 2, KC, DIM])
        beta_bc = sb("beta_bc", [DC, HEADS])
        beta_mask = sb("beta_mask", [DC, KC, HC])
        wr_sb = sb("wr_sb", [DC, KC, GROUPS + ALL_E])
        rb_sb = sb("rb_sb", [TC, GROUPS + ALL_E])
        b2_sb = sb("b2_sb", [ROWS_FULL, DIM])
        h = sb("h", [TC, NC, DIM])
        hn = sb("hn", [TC, NC, DIM])
        xt = sb("xt", [DC + 1, 2, KC, SLOTS])
        stats = sb("stats", [TC, NC, 6])
        mv = sb("mv", [TC, NC, 2])
        std = sb("std", [TC, NC])
        rstd = sb("rstd", [TC, NC])
        hn_t = sb("hn_t", [DC, KC, TOKENS])
        logit_g = sb("logit_g", [TC, NC, GROUPS])
        logit_e = sb("logit_e", [TC, NC, GROUPS, EXPERTS])
        cmp_p = [sb(f"cmp_p{i}", [TC, RB * GROUPS, EXPERTS, EXPERTS]) for i in range(2)]
        rank_e = sb("rank_e", [TC, NC, GROUPS, EXPERTS])
        list_src = sb("list_src", [TC, ALL_E, NC, LIST_W], BF16)
        earlier_bf = sb("earlier_bf", [TC, TC], BF16)
        ones_bf = sb("ones_bf", [TC, TC], BF16)
        ew1_even, ew2_even = sb("ew1_even", [DC + 1, KC, HIDDEN]), sb("ew2_even", [128, MC, DIM])
        patch_w_sb = sb_early("patch_w_sb", [128, CHANNELS, 2, DIM])
        w1_sb = sb_early("w1_sb", [DC, KC, HIDDEN])
        w3_sb = sb_early("w3_sb", [DC, KC, HIDDEN])
        w2_sb = sb_early("w2_sb", [128, MC, DIM])
        ln_gb = sb_early("ln_gb", [DC, 2, KC])
        base = sb_early("base", [TC, DIM])
        patch_t = sb_early("patch_t", [128, QC, TOKENS])
        spread_t = sb_early("spread_t", [DC, KC, NC, 128])
        pixels = sb_front("pixels", [ROWS, CHANNELS, PATCH * IMG])
        patches = sb_front("patches", [ROWS, CHANNELS, SIDE, PATCH, PATCH])
        wqkv_sb = sb_front("wqkv_sb", [DC + 1, KC, DIM + 2 * HEAD_DIM])
        wkv_rep = sb_front("wkv_rep", [DC + 1, KC, 2, HC, HEAD_DIM])
        wo_sb = sb_front("wo_sb", [DC, KC, DIM])
        row_bias = sb_front("row_bias", [2, DIM])
        pos_qt = sb_front("pos_qt", [DC, KC, SEQ])
        pos_kexp = sb_front("pos_kexp", [DC, HC, SEQ])
        pos_v = sb_front("pos_v", [SEQ, DC])
        pos_e = sb_front("pos_e", [SEQ, HEADS, SEQ])
        pos_max = sb_front("pos_max", [SEQ, 2, HEADS])
        pos_et = sb_front("pos_et", [SEQ, KC, HC * SEQ])
        pos_f = sb_front("pos_f", [DC, KC, HC, SEQ])
        pos_ot = sb_front("pos_ot", [DC, KC, SEQ])
        pos_ot2 = sb_front("pos_ot2", [DC, KC, NP, SEQ])
        front.close()
        silu_sb = sb_early("silu_sb", [128, 2, HALF])
        u_t = sb_early("u_t", [128, MC, TOKENS])
        q_t = sb_early("q_t", [ROWS_FULL, KC, NC, 128])
        k_t = sb_early("k_t", [DC, KC, NC, 128])
        q_n = sb_early("q_n", [SPAN, NC, NP, DIM])
        k_n = sb_early("k_n", [ROWS_FULL, NC, NP, DIM])
        k_exp = sb_early("k_exp", [ROWS_FULL, 2, KC, NP, HC, SEQ])
        e_sb = sb_early("e_sb", [SPAN, 2, KC, HC, SEQ])
        e_max = sb_early("e_max", [SPAN, HEADS])
        e_rz = sb_early("e_rz", [SPAN, 2, HEADS])
        e_t = sb_early("e_t", [ROWS_FULL, 3, 4, SPAN])
        vu_t = sb_early("vu_t", [DC, 2, 2, KC, NP, SEQ])
        early.close()
        idle = sb("idle", [1, 1])
        comb_t = sb("comb_t", [ROWS_FULL, TOKENS])
        gate_g = sb("gate_g", [TC, NC, GROUPS])
        gate_e = sb("gate_e", [TC, NC, GROUPS, EXPERTS])
        rank_g = sb("rank_g", [TC, NC, GROUPS])
        sel_g = sb("sel_g", [TC, NC, GROUPS])
        red_e = sb("red_e", [TC, NC, GROUPS])
        red_g = sb("red_g", [TC, NC])
        rest = sb("rest", [TC, NC, ALL_E])
        sel = sb("sel", [TC, 1 + NC * ALL_E])
        sel_bf = sb("sel_bf", [TC, NC * ALL_E], BF16)
        order = sb("order", [TC, NC * ALL_E])
        comb = sb("comb", [TC, NC, GROUPS, EXPERTS])
        cmp_g = [sb(f"cmp_g{i}", [TC, NC, GROUPS, GROUPS]) for i in range(2)]
        cmp_v = [sb(f"cmp_v{i}", [TC, RB * GROUPS, EXPERTS, EXPERTS]) for i in range(2)]
        tile_cmp = sb("tile_cmp", [TC, ALL_E, MAX_STEPS])
        tiles_of = sb("tiles_of", [TC, ALL_E])
        tiles_end = sb("tiles_end", [TC, ALL_E])
        first_slot = sb("first_slot", [TC, ALL_E])
        zeros = sb("zeros", [TC, ALL_E])
        slot_of = sb("slot_of", [TC, ALL_E, NC])
        slot_tmp = sb("slot_tmp", [TC, NC, ALL_E])
        pair_cmp, last_start = sb("pair_cmp", [1, TILES // 2]), sb("last_start", [1, 1])
        owner_cmp = sb("owner_cmp", [TABLE, ALL_E])
        owner = sb("owner", [TABLE, 1])
        table = sb("table", [1, TABLE + 2], I32)
        slot_rel = sb("slot_rel", [TC, NC])
        place = sb("place", [TC, 2, NC, SLOTS], BF16)
        list_col = sb("list_col", [TC, 2, NC, LIST_W], BF16)
        list_sb = sb("list_sb", [SLOTS, 2, LIST_W])
        fetch_f = sb("fetch_f", [SLOTS, 2])
        fetch = sb("fetch", [SLOTS, 2], I32)
        store_f = sb("store_f", [SLOTS, 2, 2])
        store = sb("store", [SLOTS, RING], I32)
        gate = sb("gate", [SLOTS, RING])
        xg = sb("xg", [SLOTS, 2, DIM])
        ew1_sb = [ew1_even, sb("ew1_odd", [DC + 1, KC, HIDDEN])]
        ew2_sb = [ew2_even, sb("ew2_odd", [128, MC, DIM])]
        ht = sb("ht", [128, 2, MC, SLOTS])
        o_sb = sb("o_sb", [SLOTS, 2, DIM])
        picks = sb("picks", [TC, NC, PICKS, DIM])
        total = sb("total", [TC, NC, DIM])

        ps = ctx.enter_context(nc.psum_tensor("ps", [128, 8, 512], F32))

        def c(name, parts=128):
            a, b = AT[name]
            return cst[0:parts, a:b]

        ident = c("ident")
        headmask = c("headmask", DC)

        ld_const, ld_qkv, ld_pixels, ld_patch_w, ld_wo = (sem(n) for n in (
            "ld_const", "ld_qkv", "ld_pixels", "ld_patch_w", "ld_wo"))
        ld_ln, ld_w13, ld_w2, ld_wqk, ld_beta, ld_router, ld_b2 = (sem(n) for n in (
            "ld_ln", "ld_w13", "ld_w2", "ld_wqk", "ld_beta", "ld_router", "ld_b2"))
        var_ready, std_ready = sem("var_ready"), sem("std_ready")
        dve_chain, small_chain, pool_chain = sem("dve_chain"), sem("small_chain"), sem("pool_chain")
        raw_read, cmp_ready, pool_ranked = (sem(n) for n in ("raw_read", "cmp_ready", "pool_ranked"))
        rep_ready, pos_proj, pos_in, pos_s, pos_sub, pos_exp, pos_norm = (sem(n) for n in (
            "rep_ready", "pos_proj", "pos_in", "pos_s", "pos_sub", "pos_exp", "pos_norm"))
        pos_tr, pos_et_ready, pos_f_done, pos_o_ready, base_done, base_ready = (sem(n) for n in (
            "pos_tr", "pos_et_ready", "pos_f_done", "pos_o_ready", "base_done", "base_ready"))
        cut_ready = [sem(f"cut_ready{ch}") for ch in range(CHANNELS)]
        px_done, px_ready, tok_done, h_ready, hn_ready, hnt_done, hnt_ready = (sem(n) for n in (
            "px_done", "px_ready", "tok_done", "h_ready", "hn_ready", "hnt_done", "hnt_ready"))
        up_done, silu_ready, u_ready, down_done, h2_ready = (sem(n) for n in (
            "up_done", "silu_ready", "u_ready", "down_done", "h2_ready"))
        wt_done, wt_ready, hn2_ready, sp_done, sp_ready, sp_zero, proj_done = (sem(n) for n in (
            "wt_done", "wt_ready", "hn2_ready", "sp_done", "sp_ready", "sp_zero", "proj_done"))
        pad_zero, b2_zero = sem("pad_zero"), sem("b2_zero")
        nat_done, bm_ready, kexp_ready, s_done, sub_ready, exp_ready, norm_ready = (sem(n) for n in (
            "nat_done", "bm_ready", "kexp_ready", "s_done", "sub_ready", "exp_ready", "norm_ready"))
        et_done, et_ready, f_done, even_ready, vu_ready, t_done, h3_ready = (sem(n) for n in (
            "et_done", "et_ready", "f_done", "even_ready", "vu_ready", "t_done", "h3_ready"))
        qk_ready = [sem("q_ready"), sem("k_ready")]
        nat_ready = [sem("q_n_ready"), sem("k_n_ready")]
        xn_ready, xn_stored, xnt_done, xnt_ready, logit_done, logit_ready, gexp_ready = (sem(n) for n in (
            "xn_ready", "xn_stored", "xnt_done", "xnt_ready", "logit_done", "logit_ready", "gexp_ready"))
        sel_ready, rank_done, comb_ready, combt_done, combt_ready, owner_ready, owner_done, table_ready = (
            sem(n) for n in ("sel_ready", "rank_done", "comb_ready", "combt_done", "combt_ready",
                             "owner_ready", "owner_done", "table_ready"))
        place_ready, list_done, fetch_ready, meta_ready, xt_done, xt_ready = (sem(n) for n in (
            "place_ready", "list_done", "fetch_ready", "meta_ready", "xt_done", "xt_ready"))
        xg_ready = [sem(f"xg_ready{u}") for u in range(2)]
        ew1_ready = [sem(f"ew1_ready{u}") for u in range(2)]
        ew2_ready = [sem(f"ew2_ready{u}") for u in range(2)]
        o_free = [sem(f"o_free{u}") for u in range(2)]
        first_place, first_list, list_read = sem("first_place"), sem("first_list"), sem("list_read")
        tiles_over, pool_turns = sem("tiles_over"), sem("pool_turns")
        mm1_done, ht_ready, mm2_done, o_ready = (sem(n) for n in ("mm1_done", "ht_ready", "mm2_done", "o_ready"))
        base_sum_done, picks_summed, pool_summed, out_ready, stored = (sem(n) for n in (
            "base_sum_done", "picks_summed", "pool_summed", "out_ready", "stored"))
        picks_ready = [sem(f"picks_ready{part}") for part in range(2)]

        def cut(copy, ch):
            return copy(patches[:, ch].rearrange("p j r w -> p r j w"),
                        pixels[:, ch].rearrange("p (r j w) -> p r j w", r=PATCH, w=PATCH)).then_inc(cut_ready[ch], 1)

        def ring_pos(j, off, n):
            return (j + off) % n

        block = ctx.enter_context(nc.Block())

        @block.sync
        def _(sp):
            sp.dma_start(cst[:], consts).then_inc(ld_const, 16)
            sp.dma_start(wqkv_sb[0:DC], wqkv.rearrange("(k p) n -> p k n", p=DC)).then_inc(ld_qkv, 16)
            sp.dma_start(wqkv_sb[DC:DC + 1, KC - 1, :], bqkv.rearrange("(a n) -> a n", a=1)).then_inc(ld_qkv, 16)
            for b in range(BATCH):
                sp.dma_start(pixels[b * SIDE:(b + 1) * SIDE],
                             x[b].rearrange("c (i r) w -> i c (r w)", r=PATCH)).then_inc(ld_pixels, 16)
            sp.dma_start(wo_sb[:], wo.rearrange("(k p) n -> p k n", p=DC)).then_inc(ld_wo, 16)
            sp.dma_start(row_bias[0:1], bo.rearrange("(a n) -> a n", a=1)).then_inc(ld_wo, 16)
            sp.dma_start(row_bias[1:2], patch_b.rearrange("(a n) -> a n", a=1)).then_inc(ld_wo, 16)
            patch_view = patch_w.rearrange("(f p c) n -> c f p n", f=2, c=CHANNELS)
            for ch in range(CHANNELS):
                sp.dma_start(patch_w_sb[:, ch], patch_view[ch].rearrange("f p n -> p f n")).then_inc(ld_patch_w, 16)
            sp.dma_start(ln_gb[:, 0, :], ln_g.rearrange("(k p) -> p k", p=DC), allow_slow_non_contiguous=True).then_inc(ld_ln, 16)
            sp.dma_start(ln_gb[:, 1, :], ln_b.rearrange("(k p) -> p k", p=DC), allow_slow_non_contiguous=True).then_inc(ld_ln, 16)
            sp.dma_start(w1_sb[:], w1.rearrange("(k p) n -> p k n", p=DC)).then_inc(ld_w13, 16)
            sp.dma_start(w3_sb[:], w3.rearrange("(k p) n -> p k n", p=DC)).then_inc(ld_w13, 16)
            sp.dma_start(wqk_sb[:, 0], attn_wq.rearrange("(k p) n -> p k n", p=DC)).then_inc(ld_wqk, 16)
            sp.dma_start(wqk_sb[:, 1], attn_wk.rearrange("(k p) n -> p k n", p=DC)).then_inc(ld_wqk, 16)
            sp.dma_start(w2_sb[:], w2.rearrange("(k p) n -> p k n", p=128)).then_inc(ld_w2, 16)
            sp.dma_start(beta_bc[:], betas.partition_broadcast(DC)).then_inc(ld_beta, 16)
            sp.dma_start(wr_sb[:, :, 0:GROUPS], wg.rearrange("(k p) n -> p k n", p=DC)).then_inc(ld_router, 16)
            for k in range(KC):
                sp.dma_start(wr_sb[:, k, GROUPS:].rearrange("p (g e) -> p g e", g=GROUPS),
                             we[:, k * DC:(k + 1) * DC, :].rearrange("g p e -> p g e")).then_inc(ld_router, 16)
            sp.dma_start(rb_sb[:, 0:GROUPS], bg.partition_broadcast(TC)).then_inc(ld_router, 16)
            sp.dma_start(rb_sb[:, GROUPS:], be.rearrange("g e -> (g e)").partition_broadcast(TC)).then_inc(ld_router, 16)
            sp.dma_start(b2_sb[0:ALL_E], eb2.rearrange("g e n -> (g e) n")).then_inc(ld_b2, 16)

            ew1_v = ew1.rearrange("g e (k p) m -> (g e) p k m", p=DC)
            eb1_v = eb1.rearrange("g e m -> (g e) m")
            ew2_v = ew2.rearrange("g e (k p) n -> (g e) p k n", p=128)

            sp.dma_start(ew1_sb[0][0:DC], ew1_v[0]).then_inc(ew1_ready[0], 16)
            sp.dma_start(ew1_sb[0][DC:DC + 1, KC - 1, :], eb1_v[0:1]).then_inc(ew1_ready[0], 16)
            sp.dma_start(ew2_sb[0][:], ew2_v[0]).then_inc(ew2_ready[0], 16)
            for g in range(NC):
                sp.wait_ge(xn_ready, g + 1)
                sp.dma_start(xn_dram[g * TC:(g + 1) * TC, :], hn[:, g, :]).then_inc(xn_stored, 16)

            def load_w1(tile, u, *wait):
                e = sp.value_load(table[0:1, bass.ds(tile, 1)], min_val=0, max_val=ALL_E - 1)
                if wait:
                    sp.wait_ge(*wait)
                sp.dma_start(ew1_sb[u][0:DC], ew1_v[bass.ds(e, 1)].rearrange("a p k m -> p (a k) m")).then_inc(ew1_ready[u], 16)
                sp.dma_start(ew1_sb[u][DC:DC + 1, KC - 1, :], eb1_v[bass.ds(e, 1), :]).then_inc(ew1_ready[u], 16)

            def load_w2(tile, u, *wait):
                e = sp.value_load(table[0:1, bass.ds(tile, 1)], min_val=0, max_val=ALL_E - 1)
                if wait:
                    sp.wait_ge(*wait)
                sp.dma_start(ew2_sb[u][:], ew2_v[bass.ds(e, 1)].rearrange("a p k n -> p (a k) n")).then_inc(ew2_ready[u], 16)

            picks_v = picks_dram[0:PICKS * TOKENS, :].rearrange("(k t) d -> t k d", k=PICKS)

            def load_picks(g, part):
                ks = slice(part * TOP_E, (part + 1) * TOP_E)
                sp.dma_start(picks[:, g, ks], picks_v[g * TC:(g + 1) * TC, ks]).then_inc(picks_ready[part], 16)

            sp.wait_ge(table_ready, 1)
            load_w1(1, 1)
            load_w2(1, 1)
            sp.wait_ge(mm1_done, 2)
            load_w1(2, 0)
            n = sp.value_load(table[0:1, TABLE:TABLE + 1], min_val=0, max_val=TILES)
            after_even, after_others, after_ew2 = (sp.alloc_register(a) for a in ("after_even", "after_others", "after_ew2"))
            last_pair = sp.value_load(table[0:1, TABLE + 1:TABLE + 2], min_val=0, max_val=TILES)
            sp.reg_alu(after_ew2, n + 1, 1, ALU.logical_shift_right)
            sp.reg_alu(after_ew2, after_ew2, 16, ALU.mult)
            sp.reg_alu(after_ew2, after_ew2, 16, ALU.add)
            sp.reg_alu(after_others, after_ew2, after_ew2, ALU.add)
            sp.reg_alu(after_even, after_others, 32, ALU.add)
            with sp.Fori(0, TILES // STEP) as q:
                with ExitStack() as reached:
                    for pair in range(STEP // 2):
                        reached.enter_context(sp.If(q * STEP + 2 * pair < n))
                        start = q * STEP + 2 * pair
                        with sp.If(start == last_pair):
                            for u in range(2):
                                sp.wait_ge(o_free[u], q * (8 * STEP) + 16 * pair)
                            for j in (2 * pair, 2 * pair + 1):
                                t, u1, u2 = q * STEP + j, ring_pos(j, 3, 2), ring_pos(j, 2, 2)
                                for g in range(NC // 2):
                                    load_picks((j % 2) * (NC // 2) + g, 0)
                                sp.wait_ge(mm1_done, t * 2 + 4)
                                sp.dma_start(ew1_sb[u1][0:1, 0, 0:DIM], ew2_v[0, 0:1, 0]).then_inc(ew1_ready[u1], 16)
                                sp.dma_start(ew1_sb[u1][0:1, 1, 0:DIM], ew2_v[0, 0:1, 0]).then_inc(ew1_ready[u1], 16)
                                sp.wait_ge(mm2_done, t + 1)
                                sp.dma_start(ew2_sb[u2][0:1, 0], ew2_v[0, 0:1, 0]).then_inc(ew2_ready[u2], 16)
                        with sp.If(start < last_pair):
                            for j in (2 * pair, 2 * pair + 1):
                                t = q * STEP + j
                                load_w1(t + 3, ring_pos(j, 3, 2), mm1_done, t * 2 + 4)
                                load_w2(t + 2, ring_pos(j, 2, 2), mm2_done, t + 1)
            sp.wait_ge(ew1_ready[0], after_even)
            sp.wait_ge(ew1_ready[1], after_others)
            for u in range(2):
                sp.wait_ge(ew2_ready[u], after_ew2)
                sp.wait_ge(o_free[u], after_ew2)
            for g in (*range(OWN_SUMS, NC), *range(OWN_SUMS)):
                load_picks(g, 1)
            out_v = out.rearrange("b s d -> (b s) d")
            for g in range(NC):
                sp.wait_ge(out_ready, g + 1)
                sp.dma_start(out_v[g * TC:(g + 1) * TC, :], total[:, g]).then_inc(stored, 16)
            sp.wait_ge(stored, 16 * NC)

        @block.tensor
        def _(pe):
            def mm(o, lhs, rhs, start=True, stop=True):
                return pe.matmul(o, lhs, rhs, start=start, stop=stop)

            pe.wait_ge(ld_const, 16)
            pe.wait_ge(ld_qkv, 32)
            pe.wait_ge(rep_ready, 3)
            sin = c("sin", DC + 1).rearrange("p (k s) -> p k s", k=KC)
            for m in range(KC):
                for k in range(KC):
                    mm(ps[0:DC, 0, m * SEQ:(m + 1) * SEQ], wqkv_sb[:, k, m * DC:(m + 1) * DC], sin[:, k], k == 0, k == 1)
            for k in range(KC):
                mm(ps[0:DC, 0, 2 * SEQ:3 * SEQ], wkv_rep[:, k, 0].rearrange("p h d -> p (h d)"), sin[:, k], k == 0, k == 1)
            for k in range(KC):
                last = mm(ps[0:SEQ, 1, 0:DC], sin[:, k], wkv_rep[:, k, 1].rearrange("p h d -> p (h d)"), k == 0, k == 1)
            last.then_inc(pos_proj, 1)
            pe.wait_ge(pos_in, 3)
            for m in range(KC):
                last = mm(ps[0:SEQ, 2 + m, 0:HC * SEQ], pos_qt[:, m], pos_kexp[:].rearrange("p h s -> p (h s)"))
            last.then_inc(pos_s, 1)

            def pixel_unit(n):
                q, r = divmod(n, 2)
                ch, f = divmod(q, 2)
                pe.wait_ge(cut_ready[ch], 1)
                if n >= 4:
                    pe.wait_ge(px_ready, n - 3)
                js = range(0, 4) if r == 0 else range(4, SIDE)
                for a, jj in enumerate(js):
                    last = pe.transpose(ps[:, 4 + n % 4, a * ROWS:(a + 1) * ROWS],
                                        patches[:, ch, jj, f * 8:f * 8 + 8].rearrange("p r w -> p (r w)"), ident[0:ROWS, 0:ROWS])
                last.then_inc(px_done, 1)

            for n in range(6):
                pixel_unit(n)
            pe.wait_ge(pos_norm, 1)
            for hd in range(HEADS):
                m, a = divmod(hd, HC)
                last = pe.transpose(ps[0:SEQ, m, a * SEQ:(a + 1) * SEQ], pos_e[:, hd, :], ident[0:SEQ, 0:SEQ])
            last.then_inc(pos_tr, 1)
            for n in range(6, 9):
                pixel_unit(n)
            pe.wait_ge(pos_et_ready, 1)
            for m in range(KC):
                last = mm(ps[0:DC, 2 + m, 0:HC * SEQ], pos_v[:], pos_et[:, m])
            last.then_inc(pos_f_done, 1)
            pe.wait_ge(ld_wqk, 32)
            for w in range(2):
                for m in range(KC):
                    for k in range(KC):
                        last = pe.transpose(ps[0:DC, w, (k * KC + m) * DC:(k * KC + m + 1) * DC],
                                            wqk_sb[:, w, m, k * DC:(k + 1) * DC], ident[0:DC, 0:DC])
            last.then_inc(wt_done, 1)
            for n in range(9, 12):
                pixel_unit(n)

            pe.wait_ge(ld_patch_w, 48)
            pe.wait_ge(px_ready, 12)

            def hn_turn(g):
                pe.wait_ge(hn_ready, g + 1)
                for k in range(KC):
                    last = pe.transpose(ps[0:DC, k + 2 * (g // 4), (g % 4) * TC:(g % 4 + 1) * TC],
                                        hn[:, g, k * DC:(k + 1) * DC], ident[0:TC, 0:TC])
                last.then_inc(hnt_done, 1)

            for g in range(NC):
                if g >= 4:
                    pe.wait_ge(h_ready, g - 3)
                for q in range(QC):
                    last = mm(ps[0:TC, 4 + g % 4, 0:DIM], patch_t[:, q, g * TC:(g + 1) * TC],
                              patch_w_sb[:, q // 2, q % 2, :], q == 0, q == QC - 1)
                last.then_inc(tok_done, 1)
                if g == 0:
                    pe.wait_ge(pos_o_ready, 1)
                    pe.wait_ge(ld_wo, 48)
                    for m in range(KC):
                        mm(ps[0:TC, 2, 0:DIM], pos_ot2[:, m].rearrange("p a s -> p (a s)"), wo_sb[:, m], m == 0, False)
                    mm(ps[0:TC, 2, 0:DIM], c("ones", 2)[:, 0:TC], row_bias[:], False, True).then_inc(base_done, 1)
                if g == 2:
                    pe.wait_ge(wt_ready, 2)
                    pe.wait_ge(base_ready, 1)
                if g >= 2:
                    hn_turn(g - 2)

            pe.wait_ge(ld_w13, 32)
            pe.wait_ge(h_ready, NC)
            for n in range(2 * MC):
                hf, m = divmod(n, MC)
                pe.wait_ge(hnt_ready, 2 * hf + 2)
                if n >= 2:
                    pe.wait_ge(u_ready, n - 1)
                for a, w in enumerate((w1_sb, w3_sb)):
                    for k in range(KC):
                        last = mm(ps[:, 4 + 2 * (n % 2) + a, 0:HALF], w[:, k, m * 128:(m + 1) * 128],
                                  hn_t[:, k, hf * HALF:(hf + 1) * HALF], k == 0, k == 1)
                    last.then_inc(up_done, 1)
                if n < 2:
                    hn_turn(NC - 2 + n)

            def spread(g):
                pe.wait_ge(hn2_ready, g + 1)
                if g >= 4:
                    pe.wait_ge(sp_ready, g - 3)
                for k in range(KC):
                    last = pe.transpose(ps[0:DC, 4 + g % 4, k * TC:(k + 1) * TC],
                                        hn[:, g, k * DC:(k + 1) * DC], ident[0:TC, 0:TC])
                last.then_inc(sp_done, 1)

            def project(hf):
                pe.wait_ge(sp_ready, 4 * hf + 4)
                for n in range(4):
                    w, m = divmod(n, 2)
                    if hf == 0:
                        pe.wait_ge(h2_ready, 5 + n)
                    else:
                        pe.wait_ge(qk_ready[w], m + 1)
                    for k in range(KC):
                        last = mm(ps[0:DC, n, 0:4 * SPAN], wqk_t[:, w, k, m * DC:(m + 1) * DC],
                                  spread_t[:, k, 4 * hf:4 * hf + 4, 0:SPAN], k == 0, k == 1)
                    last.then_inc(proj_done, 1)

            def natural(g):
                for w in range(2):
                    pe.wait_ge(qk_ready[w], 2 if g < 4 else 4)
                    if g >= 2:
                        pe.wait_ge(nat_ready[w], (g - 1) * (NP - w))
                for m in range(KC):
                    last = pe.transpose(ps[0:SPAN, 4 + 2 * (g % 2), m * DC:(m + 1) * DC], q_t[0:DC, m, g, 0:SPAN], ident[0:DC, 0:DC])
                for u in range(NP):
                    for m in range(KC):
                        last = pe.transpose(ps[0:SEQ, 5 + 2 * (g % 2), u * DIM + m * DC:u * DIM + (m + 1) * DC],
                                            k_t[:, m, g, u * LANE:u * LANE + SEQ], ident[0:DC, 0:DC])
                last.then_inc(nat_done, 1)

            pe.wait_ge(ld_w2, 16)
            pe.wait_ge(hnt_ready, 4)
            for g in range(NC):
                if g >= 4:
                    pe.wait_ge(h2_ready, g - 3)
                pe.wait_ge(u_ready, MC if g < 4 else 2 * MC)
                for m in range(MC):
                    last = mm(ps[0:TC, g % 4, 0:DIM], u_t[:, m, g * TC:(g + 1) * TC], w2_sb[:, m], m == 0, m == MC - 1)
                last.then_inc(down_done, 1)
                if g == 2:
                    pe.wait_ge(u_ready, 2 * MC)
                if g >= 2:
                    spread(g - 2)
            project(0)
            spread(NC - 2)
            spread(NC - 1)
            pe.wait_ge(sp_ready, NC)
            natural(0)
            project(1)
            for g in range(1, NAT_FIRST):
                natural(g)

            def scores(g):
                pe.wait_ge(kexp_ready, g + 1)
                if g >= 1:
                    pe.wait_ge(sub_ready, g)
                for m in range(KC):
                    for u in range(NP):
                        rows = LANE if u == 0 else SEQ
                        last = mm(ps[u * LANE:u * LANE + rows, m, 0:HC * SEQ], q_t[:, m, g, u * LANE:u * LANE + rows],
                                  k_exp[:, g % 2, m, u].rearrange("p h s -> p (h s)"))
                last.then_inc(s_done, 1)

            def flip(g, s):
                b = (g - RB - 2) // RB
                if b >= 0 and g == RB * b + RB + 2:
                    if s == 0:
                        pe.wait_ge(xnt_ready, b + 1)
                    elif s == 1:
                        pe.wait_ge(raw_read, 2 * b + 2)
                if s == 0:
                    if g >= 1:
                        pe.wait_ge(et_ready, 3 * g)
                elif s == 1:
                    if g >= 2:
                        pe.wait_ge(h3_ready, g - 1)
                else:
                    pe.wait_ge(et_ready, 3 * g + 1)
                for a in range(4):
                    m, hd = divmod(4 * s + a, HC)
                    last = pe.transpose(ps[0:SEQ, 2 + s % 2, a * SPAN:(a + 1) * SPAN], e_sb[:, g % 2, m, hd, :],
                                        ident[0:SPAN, 0:SPAN])
                last.then_inc(et_done, 1)

            def weighted(g, w):
                kind, u = divmod(w, NP)
                n = 4 * g + w
                if n >= 2:
                    pe.wait_ge(vu_ready, n - 1)
                if kind == 1:
                    pe.wait_ge(et_ready, 3 * g + 3)
                for m in range(KC):
                    bank = 4 + 2 * (n % 2) + m
                    if kind == 0:
                        last = mm(ps[0:DC, bank, 0:HC * SEQ], q_n[:, g, u, m * DC:(m + 1) * DC],
                                  e_sb[:, g % 2, m].rearrange("p h s -> p (h s)"))
                    else:
                        rhs = e_t[:].rearrange("p s a q -> p (s a) q")[:, m * HC:(m + 1) * HC, u * LANE:u * LANE + SEQ]
                        last = mm(ps[0:DC, bank, 0:HC * SEQ], k_n[:, g, u, m * DC:(m + 1) * DC], rhs)
                last.then_inc(f_done, 1)

            def gradient(g):
                if g == NC - 1:
                    pe.wait_ge(raw_read, 2 * (NB - 1))
                pe.wait_ge(vu_ready, 4 * g + 4)
                pe.wait_ge(et_ready, min(3 * g + 5, 3 * NC))
                for i, (kind, m) in enumerate(((0, 0), (0, 1), (1, 0), (1, 1))):
                    last = mm(ps[0:TC, 3, 0:DIM], vu_t[:, g % 2, kind, m].rearrange("p a s -> p (a s)"),
                              wqk_sb[:, 1 - kind, m], i == 0, i == 3)
                last.then_inc(t_done, 1)

            def routing_turn(b):
                g = RB * b + RB + 1
                pe.wait_ge(et_ready, min(3 * g + 3, 3 * NC))
                pe.wait_ge(xn_ready, RB * b + RB)
                for a in range(RB):
                    for k in range(KC):
                        last = pe.transpose(ps[0:DC, 2, (k * RB + a) * TC:(k * RB + a + 1) * TC],
                                            hn[:, RB * b + a, k * DC:(k + 1) * DC], ident[0:TC, 0:TC])
                last.then_inc(xnt_done, 1)

            def logits(b):
                g = RB * b + RB + 1
                pe.wait_ge(ld_router, 80)
                pe.wait_ge(h3_ready, min(g, NC))
                pe.wait_ge(xnt_ready, b + 1)
                for a in range(RB):
                    c0 = (RB * b + a) * TC
                    for k in range(KC):
                        last = mm(ps[0:TC, 3, a * RW:(a + 1) * RW], hn_t[:, k, c0:c0 + TC], wr_sb[:, k], k == 0, k == 1)
                last.then_inc(logit_done, 1)

            for w in range(2):
                pe.wait_ge(qk_ready[w], 4)
            pe.wait_ge(pad_zero, 5)
            scores(0)
            for g in range(NAT_FIRST, NC):
                natural(g)
            for w in range(2):
                pe.wait_ge(nat_ready[w], NC * (NP - w))
            for g in range(NC):
                if g + 1 < NC:
                    scores(g + 1)
                pe.wait_ge(norm_ready, g + 1)
                flip(g, 0)
                flip(g, 1)
                weighted(g, 0)
                flip(g, 2)
                weighted(g, 1)
                if g >= 1:
                    gradient(g - 1)
                weighted(g, 2)
                b = (g - RB - 1) // RB
                if b >= 0 and g == RB * b + RB + 1:
                    routing_turn(b)
                weighted(g, 3)
                if b >= 0 and g == RB * b + RB + 1:
                    logits(b)
            gradient(NC - 1)
            routing_turn(NB - 1)
            logits(NB - 1)

            pe.wait_ge(sel_ready, 1)
            pe.wait_ge(sub_ready, NC)
            mm(ps[0:TC, 1, 0:NC * ALL_E], earlier_bf[:], sel_bf[:], True, False)
            for b in range(NC):
                chunk = sel_bf[:, b * ALL_E:(b + 1) * ALL_E]
                if b + 1 < NC:
                    mm(ps[0:TC, 1, (b + 1) * ALL_E:NC * ALL_E].rearrange("p (c e) -> p c e", e=ALL_E), ones_bf[:],
                       chunk.unsqueeze(1).to_broadcast([TC, NC - 1 - b, ALL_E]), False, b == NC - 2)
            for b in range(NC):
                last = mm(ps[0:TC, 1, NC * ALL_E:(NC + 1) * ALL_E], ones_bf[:], sel_bf[:, b * ALL_E:(b + 1) * ALL_E], b == 0, b == NC - 1)
            last.then_inc(rank_done, 1)

            def make_list(tile_no, u):
                pe.wait_ge(place_ready, tile_no + 1)
                for b in range(NC):
                    last = mm(ps[:, 4 + u, 0:LIST_W], place[:, u, b], list_col[:, u, b], b == 0, b == NC - 1)
                last.then_inc(list_done, 1)

            def turn(u):
                for k in range(KC):
                    last = pe.transpose(ps[0:DC, 4 + u, k * SLOTS:(k + 1) * SLOTS], xg[:, u, k * DC:(k + 1) * DC], ident)
                last.then_inc(xt_done, 1)

            def up(u, ms=range(MC)):
                for m in ms:
                    o = ps[:, 2 * u + m // 4, (m % 4) * SLOTS:(m % 4 + 1) * SLOTS]
                    mm(o, ew1_sb[u][0:DC, 0, m * 128:(m + 1) * 128], xt[0:DC, u, 0], True, False)
                    last = mm(o, ew1_sb[u][:, 1, m * 128:(m + 1) * 128], xt[:, u, 1], False, True)
                    if m in (3, MC - 1):
                        last.then_inc(mm1_done, 1)

            def down(u):
                for m in range(MC):
                    last = mm(ps[:, 6 + u, 0:DIM], ht[:, u, m], ew2_sb[u][:, m], m == 0, m == MC - 1)
                last.then_inc(mm2_done, 1)

            pe.wait_ge(first_place, 1)
            for b in range(NC):
                last = mm(ps[:, 5, 0:LIST_W], place[:, 0, b], list_col[:, 0, b], b == 0, b == NC - 1)
            last.then_inc(first_list, 1)
            pe.wait_ge(owner_ready, 1)
            mm(ps[0:1, 2, 0:TABLE], owner[:], ident[0:TABLE, 0:TABLE]).then_inc(owner_done, 1)
            pe.wait_ge(xg_ready[0], 16)
            turn(0)
            pe.wait_ge(xt_ready, 1)
            pe.wait_ge(ew1_ready[0], 32)
            up(0, range(4))
            make_list(0, 0)
            pe.wait_ge(fetch_ready, 1)
            make_list(1, 1)
            up(0, range(4, MC))
            pe.wait_ge(list_read, 1)
            make_list(2, 0)
            pe.wait_ge(fetch_ready, 2)
            pe.wait_ge(xg_ready[1], 16)
            turn(1)
            n = pe.value_load(table[0:1, TABLE:TABLE + 1], min_val=0, max_val=TILES)
            with pe.Fori(0, TILES // STEP) as q:
                with ExitStack() as reached:
                    for pair in range(STEP // 2):
                        reached.enter_context(pe.If(q * STEP + 2 * pair < n))
                        for j in (2 * pair, 2 * pair + 1):
                            t = q * STEP + j
                            pe.wait_ge(xt_ready, t + 2)
                            u = ring_pos(j, 1, 2)
                            pe.wait_ge(ew1_ready[u], q * (16 * STEP) + 32 * ((j + 1) // 2 + 1))
                            up(u)
                            make_list(t + 3, ring_pos(j, 3, 2))
                            pe.wait_ge(fetch_ready, t + 3)
                            pe.wait_ge(xg_ready[ring_pos(j, 2, 2)], q * (8 * STEP) + 16 * ((j + 2) // 2 + 1))
                            turn(ring_pos(j, 2, 2))
                            u = ring_pos(j, 0, 2)
                            pe.wait_ge(ht_ready, t * 2 + 2)
                            pe.wait_ge(ew2_ready[u], q * (8 * STEP) + 16 * (j // 2 + 1))
                            pe.wait_ge(o_ready, t + 1)
                            down(u)
            pe.wait_ge(comb_ready, 1)
            pe.wait_ge(tiles_over, 2)
            for g in range(NC):
                last = pe.transpose(ps[0:ALL_E, 4 + g // 4, (g % 4) * TC:(g % 4 + 1) * TC],
                                    comb[:, g].rearrange("p g e -> p (g e)"), ident[0:TC, 0:TC])
            last.then_inc(combt_done, 1)

            def sum_of(g):
                return ps[0:TC, g // 2, (g % 2) * DIM:(g % 2 + 1) * DIM]

            for g in range(NC):
                mm(sum_of(g), ident[0:TC, 0:TC], h[:, g], True, False)
                if g == 0:
                    pe.wait_ge(combt_ready, 2)
                    pe.wait_ge(b2_zero, 4)
                    pe.wait_ge(ld_b2, 16)
                    pe.wait_ge(picks_ready[0], 16 * NC)
                mm(sum_of(g), comb_t[:, g * TC:(g + 1) * TC], b2_sb[:], False, False)
                for k in range(PE_SUMS):
                    last = mm(sum_of(g), ident[0:TC, 0:TC], picks[:, g, k], False, k == PE_SUMS - 1)
                if g % 2:
                    last.then_inc(base_sum_done, 1)

        @block.scalar
        def _(act):
            act.sem_inc(o_ready, 2)
            act.wait_ge(ld_pixels, 16 * BATCH)
            cut(act.copy, 0)
            cut(act.copy, 1)
            act.wait_ge(pos_sub, 1)
            act.activation(pos_e[:], pos_e[:], ACT.Exp, scale=HEAD_DIM ** -0.5).then_inc(pos_exp, 1)
            for n in range(12):
                q, r = divmod(n, 2)
                j0, j1 = (0, 4) if r == 0 else (4, SIDE)
                act.wait_ge(px_done, n + 1)
                act.copy(patch_t[:, q].rearrange("p (b j) -> p j b", j=SIDE)[:, j0:j1],
                         ps[:, 4 + n % 4, 0:(j1 - j0) * ROWS].rearrange("p (j b) -> p j b", b=ROWS)).then_inc(px_ready, 1)
            def deviation(g, norm):
                act.wait_ge(var_ready, norm * NC + g + 1)
                act.activation(std[:, g:g + 1], mv[:, g, 1:2], ACT.Sqrt, bias=c("eps", TC)).then_inc(std_ready, 1)

            act.wait_ge(wt_done, 1)
            for w in range(2):
                act.copy(wqk_t[:, w].rearrange("p k n -> p (k n)"), ps[0:DC, w, 0:KC * DIM]).then_inc(wt_ready, 1)
            for g in range(NC):
                deviation(g, 0)

            for n in range(2 * MC):
                act.wait_ge(up_done, 2 * n + 1)
                if n >= 2:
                    act.wait_ge(u_ready, n - 1)
                act.activation(silu_sb[:, n % 2], ps[:, 4 + 2 * (n % 2), 0:HALF], ACT.Silu).then_inc(silu_ready, 1)
            def spread(g):
                act.wait_ge(sp_done, g + 1)
                act.copy(spread_t[:, :, g].rearrange("p k (a s) -> p k a s", a=NP)[:, :, :, 0:SEQ],
                         ps[0:DC, 4 + g % 4, 0:KC * TC].rearrange("p (k a s) -> p k a s", k=KC, a=NP)).then_inc(sp_ready, 1)

            def project(hf):
                for m in range(KC):
                    act.wait_ge(proj_done, 4 * hf + m + 1)
                    act.copy(q_t[0:DC, m, 4 * hf:4 * hf + 4, 0:SPAN],
                             ps[0:DC, m, 0:4 * SPAN].rearrange("p (g s) -> p g s", g=4)).then_inc(qk_ready[0], 1)

            def natural(g):
                act.wait_ge(nat_done, g + 1)
                for u, rows in enumerate((slice(0, LANE), slice(LANE, SPAN))):
                    act.copy(q_n[rows, g, u], ps[rows, 4 + 2 * (g % 2), 0:DIM]).then_inc(nat_ready[0], 1)

            act.wait_ge(sp_zero, 1)
            act.wait_ge(pad_zero, 5)
            for g in range(NC):
                deviation(g, 1)
                if g >= 2:
                    spread(g - 2)
            project(0)
            spread(NC - 2)
            spread(NC - 1)
            natural(0)
            project(1)
            for g in range(1, NAT_FIRST):
                natural(g)

            def exp(g):
                act.wait_ge(sub_ready, g + 1)
                act.activation(e_sb[:, g % 2], e_sb[:, g % 2], ACT.Exp).then_inc(exp_ready, 1)

            def even_heads(g, w):
                kind, u = divmod(w, NP)
                n = 4 * g + w
                act.wait_ge(f_done, n + 1)
                if w == 0 and g >= 2:
                    act.wait_ge(t_done, g - 1)
                for b in range(HC // 2):
                    rows = slice(b * 32, b * 32 + 32)
                    act.activation(vu_t[rows, g % 2, kind, :, u, :],
                                   ps[rows, 4 + 2 * (n % 2):6 + 2 * (n % 2), 2 * b * SEQ:(2 * b + 1) * SEQ],
                                   ACT.Copy, scale=headmask[rows, 2 * b:2 * b + 1]).then_inc(even_ready, 1)

            def turned(g, s):
                act.wait_ge(et_done, 3 * g + s + 1)
                if g >= 1 and s == 0:
                    act.wait_ge(f_done, 4 * g)
                act.copy(e_t[0:SEQ, s].rearrange("p a q -> p (a q)"), ps[0:SEQ, 2 + s % 2, 0:4 * SPAN]).then_inc(et_ready, 1)

            def routing_std(b):
                act.wait_ge(var_ready, 2 * NC + RB * (b + 1))
                act.activation(std[:, RB * b:RB * (b + 1)], mv[:, RB * b:RB * (b + 1), 1], ACT.Sqrt, bias=c("eps", TC)).then_inc(std_ready, 1)

            def routing_turn(b):
                act.wait_ge(xnt_done, b + 1)
                act.copy(hn_t[:, :, RB * b * TC:RB * (b + 1) * TC],
                         ps[0:DC, 2, 0:KC * RB * TC].rearrange("p (k t) -> p k t", k=KC)).then_inc(xnt_ready, 1)

            def routing_exp():
                act.wait_ge(logit_ready, 2)
                act.activation(gate_g[:], gate_g[:], ACT.Exp).then_inc(gexp_ready, 1)
                act.activation(gate_e[:], gate_e[:], ACT.Exp).then_inc(gexp_ready, 1)
                act.activation(idle[:], cst[0:1, 0:1], ACT.Gelu)

            exp(0)
            for g in range(NAT_FIRST, NC):
                natural(g)
            for g in range(NC):
                turned(g, 0)
                turned(g, 1)
                if g + 1 < NC:
                    exp(g + 1)
                even_heads(g, 0)
                turned(g, 2)
                even_heads(g, 1)
                even_heads(g, 2)
                b = (g - RB - 1) // RB
                if b >= 0 and g == RB * b + RB + 1:
                    routing_turn(b)
                even_heads(g, 3)
                if g % RB == 0 and g >= RB:
                    routing_std(g // RB - 1)

            routing_std(NB - 1)
            routing_turn(NB - 1)
            routing_exp()

            def gelu(tile2, u):
                act.wait_ge(mm1_done, tile2 + 1)
                act.activation(ht[:, u, 0:4].rearrange("p m s -> p (m s)"), ps[:, 2 * u, 0:4 * SLOTS], ACT.Gelu).then_inc(ht_ready, 1)
                act.wait_ge(mm1_done, tile2 + 2)
                act.activation(ht[:, u, 4:MC].rearrange("p m s -> p (m s)"), ps[:, 2 * u + 1, 0:(MC - 4) * SLOTS], ACT.Gelu).then_inc(ht_ready, 1)

            act.wait_ge(table_ready, 1)
            gelu(0, 0)
            n = act.value_load(table[0:1, TABLE:TABLE + 1], min_val=0, max_val=TILES)
            with act.Fori(0, TILES // STEP) as q:
                with ExitStack() as reached:
                    for pair in range(STEP // 2):
                        reached.enter_context(act.If(q * STEP + 2 * pair < n))
                        for j in (2 * pair, 2 * pair + 1):
                            t = q * STEP + j
                            gelu(t * 2 + 2, ring_pos(j, 1, 2))
                            u = ring_pos(j, 0, 2)
                            act.wait_ge(mm2_done, t + 1)
                            act.wait_ge(meta_ready, t + 1)
                            act.wait_ge(o_free[u], q * (8 * STEP) + 16 * (j // 2 + 1))
                            act.activation(o_sb[:, u], ps[:, 6 + u, 0:DIM], ACT.Copy,
                                           scale=gate[:, ring_pos(j, 0, RING):ring_pos(j, 0, RING) + 1]).then_inc(o_ready, 1)
            act.copy(std[:, 0:1], rstd[:, 0:1]).then_inc(tiles_over, 1)
            act.wait_ge(combt_done, 1)
            for a in range(2):
                act.copy(comb_t[0:ALL_E, a * HALF:(a + 1) * HALF], ps[0:ALL_E, 4 + a, 0:HALF]).then_inc(combt_ready, 1)

        @block.gpsimd
        def _(pool):
            pool.memset(spread_t[:], 0.0).then_inc(sp_zero, 1)
            pool.memset(xt[DC:DC + 1], 1.0).then_inc(sp_zero, 1)

            pool.wait_ge(sp_zero, 2)
            for i, rows in enumerate((slice(32, 64), slice(64, 128))):
                pool.memset(b2_sb[rows], 0.0).then_inc(b2_zero, 1)
                pool.wait_ge(b2_zero, i + 1)
            pool.wait_ge(px_done, 12)
            pool.wait_ge(base_done, 1)
            pool.memset(q_n[:], 0.0).then_inc(pad_zero, 1)
            pool.memset(k_n[:], 0.0).then_inc(pad_zero, 1)
            pool.memset(e_t[:], 0.0).then_inc(pad_zero, 1)
            pool.wait_ge(pad_zero, 3)
            pool.memset(q_t[DC:ROWS_FULL], 0.0).then_inc(pad_zero, 1)
            pool.memset(k_exp[DC:ROWS_FULL], 0.0).then_inc(pad_zero, 1)
            pool.wait_ge(pad_zero, 5)

            def expand(g):
                pool.wait_ge(qk_ready[1], 2 if g < 4 else 4)
                if g >= 2:
                    pool.wait_ge(s_done, g - 1)
                for m in range(KC):
                    for u in range(NP):
                        shape = [DC, HC, SEQ]
                        last = pool.tensor_tensor(k_exp[0:DC, g % 2, m, u],
                                                  k_t[:, m, g, u * LANE:u * LANE + SEQ].unsqueeze(1).to_broadcast(shape),
                                                  beta_mask[:, m].unsqueeze(2).to_broadcast(shape), ALU.mult)
                last.then_inc(kexp_ready, 1)

            pool.wait_ge(bm_ready, 1)
            expand(0)
            expand(1)
            steps = [0]

            def follow(ins):
                steps[0] += 1
                ins.then_inc(pool_chain, 1)
                pool.wait_ge(pool_chain, steps[0])

            def pool_rank(b):
                equal, above = cmp_p[0][:], cmp_p[1][:]
                shape, n = [TC, RB * GROUPS, EXPERTS, EXPERTS], EXPERTS
                pool.wait_ge(cmp_ready, 2 * b + 2)
                follow(pool.tensor_tensor(equal, equal, c("tie_e", TC).rearrange("p (i j) -> p i j", i=n).unsqueeze(1).to_broadcast(shape), ALU.mult))
                follow(pool.tensor_tensor(equal, equal, above, ALU.add))
                while n > 2:
                    n //= 2
                    follow(pool.tensor_tensor(equal[:, :, :, 0:n], equal[:, :, :, 0:n], equal[:, :, :, n:2 * n], ALU.add))
                pool.tensor_tensor(rank_e[:, RB * b:RB * (b + 1)].rearrange("p c g e -> p (c g) e"), equal[:, :, :, 0], equal[:, :, :, 1],
                                   ALU.add).then_inc(pool_ranked, 1)

            for g in range(2, NC):
                expand(g)
                b = (g - RB - 3) // RB
                if b >= 0 and g == RB * b + RB + 3:
                    pool_rank(b)
            pool_rank(NB - 2)

            def gather(u):
                pool.indirect_dma_start(xg[:, u], None, xn_dram, bass.IndirectOffsetOnAxis(fetch[:, u:u + 1], 0)).then_inc(xg_ready[u], 16)

            pool.wait_ge(logit_ready, 2)
            for u in range(2):
                pool.dma_start(o_sb[:, u], consts[:, 0:DIM]).then_inc(o_free[u], 16)
            for i, rows in enumerate((slice(32, 64), slice(64, 128))):
                pool.memset(comb_t[rows], 0.0).then_inc(b2_zero, 1)
                pool.wait_ge(b2_zero, i + 3)
            pool.wait_ge(xn_stored, 16 * NC)
            pool.wait_ge(fetch_ready, 1)
            gather(0)
            pool.wait_ge(fetch_ready, 2)
            gather(1)
            pool.wait_ge(fetch_ready, 3)
            pool.wait_ge(xt_done, 1)
            gather(0)
            pool.wait_ge(table_ready, 1)
            def hold():
                pool.sem_inc(pool_turns, 1)

            n = pool.value_load(table[0:1, TABLE:TABLE + 1], min_val=0, max_val=TILES)
            with pool.Fori(0, TILES // STEP) as q:
                with ExitStack() as reached:
                    for pair in range(STEP // 2):
                        reached.enter_context(pool.If(q * STEP + 2 * pair < n))
                        for j in (2 * pair, 2 * pair + 1):
                            t = q * STEP + j
                            pool.wait_ge(fetch_ready, t + 4)
                            pool.wait_ge(xt_done, t + 2)
                            hold()
                            gather(ring_pos(j, 3, 2))
                            u = ring_pos(j, 0, 2)
                            r = ring_pos(j, 0, RING)
                            pool.wait_ge(o_ready, t + 3)
                            hold()
                            pool.indirect_dma_start(picks_dram, bass.IndirectOffsetOnAxis(store[:, r:r + 1], 0),
                                                    o_sb[:, u], None).then_inc(o_free[u], 16)
            for u in range(2):
                pool.wait_ge(xg_ready[u], 16)
            for part in range(2):
                pool.wait_ge(picks_ready[part], 16 * NC)
            mine = total[:, OWN_SUMS:]
            follow(pool.tensor_tensor(mine, picks[:, OWN_SUMS:, PE_SUMS], picks[:, OWN_SUMS:, PE_SUMS + 1], ALU.add))
            for k in range(PE_SUMS + 2, PICKS):
                last = pool.tensor_tensor(mine, mine, picks[:, OWN_SUMS:, k], ALU.add)
                if k < PICKS - 1:
                    follow(last)
            last.then_inc(pool_summed, 1)

        @block.vector
        def _(dve):
            count = [0]

            def link(ins):
                count[0] += 1
                ins.then_inc(dve_chain, 1)
                dve.wait_ge(dve_chain, count[0])

            def moments(g, ready):
                dve.wait_ge(ready, g + 1)
                link(dve.bn_stats(stats[:, g], h[:, g]))
                dve.bn_aggr(mv[:, g], stats[:, g]).then_inc(var_ready, 1)

            def normalise(g, norm):
                if norm < 2:
                    dve.wait_ge(std_ready, norm * NC + g + 1)
                    link(dve.reciprocal(rstd[:, g:g + 1], std[:, g:g + 1]))
                return dve.tensor_scalar(hn[:, g], h[:, g], mv[:, g, 0:1], rstd[:, g:g + 1], ALU.subtract, ALU.mult)

            dve.memset(wqkv_sb[DC:DC + 1, 0, :], 0.0).then_inc(rep_ready, 1)
            dve.wait_ge(rep_ready, 1)
            dve.wait_ge(ld_qkv, 32)
            for k in range(KC):
                shape = [DC + 1, 2, HC, HEAD_DIM]
                dve.tensor_copy(wkv_rep[:, k], wqkv_sb[:, k, DIM:].rearrange("p (v d) -> p v d", v=2).unsqueeze(2)
                                .to_broadcast(shape)).then_inc(rep_ready, 1)
            dve.wait_ge(ld_const, 16)
            dve.wait_ge(pos_proj, 1)
            dve.tensor_copy(pos_qt[:], ps[0:DC, 0, 0:KC * SEQ].rearrange("p (k s) -> p k s", k=KC)).then_inc(pos_in, 1)
            shape = [DC, HC, SEQ]
            dve.tensor_tensor(pos_kexp[:], ps[0:DC, 0, 2 * SEQ:3 * SEQ].unsqueeze(1).to_broadcast(shape),
                              headmask.unsqueeze(2).to_broadcast(shape), ALU.mult).then_inc(pos_in, 1)
            dve.tensor_copy(pos_v[:], ps[0:SEQ, 1, 0:DC]).then_inc(pos_in, 1)
            dve.wait_ge(pos_s, 1)
            shape = [SEQ, HC, SEQ]
            for m in range(KC):
                last = dve.tensor_tensor(pos_e[:, m * HC:(m + 1) * HC], ps[0:SEQ, 2 + m, 0:HC * SEQ].rearrange("p (h s) -> p h s", h=HC),
                                         c("causal", SEQ).unsqueeze(1).to_broadcast(shape), ALU.add)
                link(last)
            shape = [SEQ, HEADS, SEQ]
            link(dve.tensor_reduce(pos_max[:, 0], pos_e[:], X, ALU.max))
            dve.tensor_tensor(pos_e[:], pos_e[:], pos_max[:, 0].unsqueeze(2).to_broadcast(shape), ALU.subtract).then_inc(pos_sub, 1)
            dve.wait_ge(pos_exp, 1)
            link(dve.tensor_reduce(pos_max[:, 1], pos_e[:], X, ALU.add))
            link(dve.reciprocal(pos_max[:, 0], pos_max[:, 1]))
            dve.tensor_tensor(pos_e[:], pos_e[:], pos_max[:, 0].unsqueeze(2).to_broadcast(shape), ALU.mult).then_inc(pos_norm, 1)
            dve.wait_ge(ld_pixels, 16 * BATCH)
            cut(dve.tensor_copy, 2)
            dve.wait_ge(pos_tr, 1)
            dve.tensor_copy(pos_et[:], ps[0:SEQ, 0:KC, 0:HC * SEQ]).then_inc(pos_et_ready, 1)
            dve.wait_ge(pos_f_done, 1)
            for m in range(KC):
                link(dve.tensor_tensor(pos_f[:, m], ps[0:DC, 2 + m, 0:HC * SEQ].rearrange("p (h s) -> p h s", h=HC),
                                       headmask.unsqueeze(2).to_broadcast([DC, HC, SEQ]), ALU.mult))
            for m in range(KC):
                link(dve.tensor_reduce(pos_ot[:, m], pos_f[:, m].rearrange("p h s -> p s h"), X, ALU.add))
            dve.tensor_copy(pos_ot2[:], pos_ot[:].unsqueeze(2).to_broadcast([DC, KC, NP, SEQ])).then_inc(pos_o_ready, 1)
            dve.wait_ge(base_done, 1)
            dve.tensor_copy(base[:], ps[0:TC, 2, 0:DIM]).then_inc(base_ready, 1)
            dve.wait_ge(base_ready, 1)
            def affine(hf):
                dve.wait_ge(ld_ln, 32)
                dve.wait_ge(hnt_done, 4 * hf + 4)
                for k in range(KC):
                    dve.tensor_scalar(hn_t[:, k, hf * HALF:(hf + 1) * HALF], ps[0:DC, k + 2 * hf, 0:HALF],
                                      ln_gb[:, 0, k:k + 1], ln_gb[:, 1, k:k + 1], ALU.mult, ALU.add).then_inc(hnt_ready, 1)

            for g in range(NC):
                dve.wait_ge(tok_done, g + 1)
                dve.tensor_tensor(h[:, g], ps[0:TC, 4 + g % 4, 0:DIM], base[:], ALU.add).then_inc(h_ready, 1)
                moments(g, h_ready)
                if g >= 1:
                    normalise(g - 1, 0).then_inc(hn_ready, 1)
                if g == NC - 2:
                    affine(0)
            normalise(NC - 1, 0).then_inc(hn_ready, 1)

            for n in range(2 * MC):
                hf, m = divmod(n, MC)
                dve.wait_ge(silu_ready, n + 1)
                dve.wait_ge(up_done, 2 * n + 2)
                dve.tensor_tensor(u_t[:, m, hf * HALF:(hf + 1) * HALF], silu_sb[:, n % 2],
                                  ps[:, 5 + 2 * (n % 2), 0:HALF], ALU.mult).then_inc(u_ready, 1)
                if n == 1:
                    affine(1)
            for g in range(NC):
                dve.wait_ge(down_done, g + 1)
                dve.tensor_tensor(h[:, g], h[:, g], ps[0:TC, g % 4, 0:DIM], ALU.add).then_inc(h2_ready, 1)
                moments(g, h2_ready)
                if g >= 1:
                    normalise(g - 1, 1).then_inc(hn2_ready, 1)
            normalise(NC - 1, 1).then_inc(hn2_ready, 1)
            dve.wait_ge(ld_beta, 16)
            dve.tensor_tensor(beta_mask[:], beta_bc[:].rearrange("p (k h) -> p k h", k=KC),
                              headmask.unsqueeze(1).to_broadcast([DC, KC, HC]), ALU.mult).then_inc(bm_ready, 1)

            for k, v in ((earlier_bf, "earlier"), (ones_bf, "ones")):
                link(dve.tensor_copy(k[:], c(v, TC)[:, 0:TC]))
            link(dve.memset(list_src[:], 0.0))
            link(dve.tensor_copy(list_src[:, :, :, 0:3], c("token", TC).rearrange("p (c w) -> p c w", w=3).unsqueeze(1)
                                 .to_broadcast([TC, ALL_E, NC, 3])))
            dve.wait_ge(pad_zero, 5)

            def project(hf):
                for m in range(KC):
                    dve.wait_ge(proj_done, 4 * hf + 2 + m + 1)
                    dve.tensor_copy(k_t[:, m, 4 * hf:4 * hf + 4, 0:SPAN],
                                    ps[0:DC, 2 + m, 0:4 * SPAN].rearrange("p (g s) -> p g s", g=4)).then_inc(qk_ready[1], 1)

            def natural(g):
                dve.wait_ge(nat_done, g + 1)
                dve.tensor_copy(k_n[0:SEQ, g].rearrange("p a n -> p (a n)"), ps[0:SEQ, 5 + 2 * (g % 2), 0:NP * DIM]).then_inc(nat_ready[1], 1)

            project(0)
            natural(0)
            project(1)
            for g in range(1, NAT_FIRST):
                natural(g)

            def shift(g):
                dve.wait_ge(s_done, g + 1)
                if g >= 2:
                    dve.wait_ge(f_done, 4 * g - 6)
                s = ps[0:SPAN, 0:KC, 0:HC * SEQ].rearrange("p k (h s) -> p k h s", h=HC)
                mx = e_max[:].rearrange("p (k h) -> p k h", k=KC)
                link(dve.tensor_reduce(mx, s, X, ALU.max))
                for m in range(KC):
                    last = dve.tensor_tensor(e_sb[:, g % 2, m], s[:, m], mx[:, m].unsqueeze(2).to_broadcast([SPAN, HC, SEQ]), ALU.subtract)
                last.then_inc(sub_ready, 1)

            def odd_heads(g, w):
                kind, u = divmod(w, NP)
                n = 4 * g + w
                for b in range(HC // 2):
                    dve.wait_ge(even_ready, (HC // 2) * n + b + 1)
                    rows = slice(b * 32, b * 32 + 32)
                    o = vu_t[rows, g % 2, kind, :, u, :]
                    last = dve.scalar_tensor_tensor(out=o, in0=ps[rows, 4 + 2 * (n % 2):6 + 2 * (n % 2), (2 * b + 1) * SEQ:(2 * b + 2) * SEQ],
                                                    scalar=headmask[rows, 2 * b + 1:2 * b + 2], in1=o, op0=ALU.mult, op1=ALU.add)
                last.then_inc(vu_ready, 1)

            def residual(g):
                dve.wait_ge(t_done, g + 1)
                dve.tensor_tensor(h[:, g], h[:, g], ps[0:TC, 3, 0:DIM], ALU.add).then_inc(h3_ready, 1)
                moments(g, h3_ready)

            def norm(g):
                dve.wait_ge(exp_ready, g + 1)
                dve.wait_ge(sub_ready, g + 1)
                e_flat = e_sb[:, g % 2].rearrange("p k h s -> p (k h) s")
                link(dve.tensor_reduce(e_max[:], e_flat, X, ALU.add))
                link(dve.reciprocal(e_rz[:, g % 2], e_max[:]))
                dve.tensor_tensor(e_flat, e_flat, e_rz[:, g % 2].unsqueeze(2).to_broadcast([SPAN, HEADS, SEQ]),
                                  ALU.mult).then_inc(norm_ready, 1)

            def routing_rows(b):
                dve.wait_ge(std_ready, 2 * NC + b + 1)
                link(dve.reciprocal(rstd[:, RB * b:RB * (b + 1)], std[:, RB * b:RB * (b + 1)]))
                for g in range(RB * b, RB * (b + 1)):
                    normalise(g, 2).then_inc(xn_ready, 1)

            def routing_logits(b):
                chunks = slice(RB * b, RB * (b + 1))
                dve.wait_ge(ld_router, 80)
                dve.wait_ge(logit_done, b + 1)
                raw = ps[0:TC, 3, 0:RB * RW].rearrange("p (c w) -> p c w", w=RW)
                dve.tensor_tensor(logit_g[:, chunks], raw[:, :, 0:GROUPS], rb_sb[:, 0:GROUPS].unsqueeze(1).to_broadcast([TC, RB, GROUPS]),
                                  ALU.add).then_inc(raw_read, 1)
                dve.tensor_tensor(logit_e[:, chunks].rearrange("p c g e -> p c (g e)"), raw[:, :, GROUPS:],
                                  rb_sb[:, GROUPS:].unsqueeze(1).to_broadcast([TC, RB, ALL_E]), ALU.add).then_inc(raw_read, 1)
                dve.wait_ge(raw_read, 2 * b + 2)

            def compare(values, n, sets, buffers):
                shape = [TC, sets, n, n]
                other, own = values.unsqueeze(2).to_broadcast(shape), values.unsqueeze(3).to_broadcast(shape)
                return (dve.tensor_tensor(buffers[0][:], other, own, ALU.is_equal),
                        dve.tensor_tensor(buffers[1][:], other, own, ALU.is_gt))

            def compare_experts(b):
                for ins in compare(logit_e[:, RB * b:RB * (b + 1)].rearrange("p c g e -> p (c g) e"), EXPERTS, RB * GROUPS, cmp_p):
                    ins.then_inc(cmp_ready, 1)

            shift(0)
            for g in range(NAT_FIRST, NC):
                natural(g)
            norm(0)
            for g in range(NC):
                if g + 1 < NC:
                    shift(g + 1)
                if g % RB == 1 and g > RB:
                    routing_rows((g - RB - 1) // RB)
                odd_heads(g, 0)
                odd_heads(g, 1)
                if g + 1 < NC:
                    norm(g + 1)
                if g >= 1:
                    residual(g - 1)
                odd_heads(g, 2)
                odd_heads(g, 3)
                if g % RB == 1 and g > RB:
                    b = (g - RB - 1) // RB
                    routing_logits(b)
                    if b >= 1:
                        dve.wait_ge(pool_ranked, b)
                    compare_experts(b)
            residual(NC - 1)

            routing_rows(NB - 1)
            link(dve.memset(zeros[:], 0.0))
            link(dve.memset(sel[:, 0:1], 0.0))
            routing_logits(NB - 1)

            def both(*steps):
                for ins in steps:
                    count[0] += 1
                    ins.then_inc(dve_chain, 1)
                dve.wait_ge(dve_chain, count[0])

            final = slice(RB * (NB - 1), NC)

            def weigh(buffer, n, sets, tie):
                return dve.tensor_tensor(buffer[:], buffer[:], tie.rearrange("p (i j) -> p i j", i=n).unsqueeze(1)
                                         .to_broadcast([TC, sets, n, n]), ALU.mult)

            both(*compare(logit_g[:], GROUPS, NC, cmp_g),
                 *compare(logit_e[:, final].rearrange("p c g e -> p (c g) e"), EXPERTS, RB * GROUPS, cmp_v))
            both(weigh(cmp_g[0], GROUPS, NC, c("tie_g", TC)), weigh(cmp_v[0], EXPERTS, RB * GROUPS, c("tie_e", TC)))
            both(dve.tensor_tensor(cmp_g[0][:], cmp_g[0][:], cmp_g[1][:], ALU.add),
                 dve.tensor_tensor(cmp_v[0][:], cmp_v[0][:], cmp_v[1][:], ALU.add))
            both(dve.tensor_reduce(rank_g[:], cmp_g[0][:], X, ALU.add),
                 dve.tensor_reduce(rank_e[:, final].rearrange("p c g e -> p (c g) e"), cmp_v[0][:], X, ALU.add))

            wide = [TC, NC, GROUPS, EXPERTS]
            fg, fe = (lambda v: v.rearrange("p c g -> p (c g)")), (lambda v: v.rearrange("p c g e -> p (c g e)"))
            sel_e = sel[:, 1:]
            link(dve.tensor_scalar(sel_g[:], rank_g[:], float(TOP_G), None, ALU.is_lt))
            dve.wait_ge(pool_ranked, NB - 1)
            link(dve.scalar_tensor_tensor(out=sel_e.rearrange("p (a e) -> p a e", e=EXPERTS), in0=rank_e[:].rearrange("p c g e -> p (c g) e"),
                                          scalar=float(TOP_E), in1=fg(sel_g[:]).unsqueeze(2).to_broadcast([TC, NC * GROUPS, EXPERTS]),
                                          op0=ALU.is_lt, op1=ALU.mult))
            dve.tensor_copy(sel_bf[:], sel_e).then_inc(sel_ready, 1)
            both(dve.tensor_reduce(red_g[:], logit_g[:], X, ALU.max), dve.tensor_reduce(red_e[:], logit_e[:], X, ALU.max))
            dve.tensor_tensor(gate_g[:], logit_g[:], red_g[:].unsqueeze(2).to_broadcast([TC, NC, GROUPS]), ALU.subtract).then_inc(logit_ready, 1)
            dve.tensor_tensor(gate_e[:], logit_e[:], red_e[:].unsqueeze(3).to_broadcast(wide), ALU.subtract).then_inc(logit_ready, 1)
            part = [list_src[:, :, :, w].rearrange("p e c -> p c e") for w in range(LIST_W)]
            by_chunk = "p (c e) -> p c e"
            link(dve.tensor_tensor_scan(order[:], c("restart", TC), sel[:, 0:NC * ALL_E], 0.0, ALU.add, ALU.add))
            link(dve.tensor_copy(part[3], order[:].rearrange(by_chunk, e=ALL_E)))
            dve.wait_ge(rank_done, 1)
            dve.wait_ge(sp_zero, 2)
            rank_v = ps[0:TC, 1, 0:NC * ALL_E].rearrange("p (c e) -> p c e", e=ALL_E)
            sel_v = sel_e.rearrange(by_chunk, e=ALL_E)

            both(dve.scalar_tensor_tensor(out=slot_rel[:], in0=rank_v[:, :, 0], scalar=1.0, in1=sel_v[:, :, 0], op0=ALU.add, op1=ALU.mult),
                 dve.tensor_copy(list_col[:, 0], list_src[:, 0]))
            link(dve.tensor_scalar(slot_rel[:], slot_rel[:], -1.0, None, ALU.add))
            dve.tensor_tensor(place[:, 0], slot_rel[:].unsqueeze(2).to_broadcast([TC, NC, SLOTS]),
                              c("slot", TC).unsqueeze(1).to_broadcast([TC, NC, SLOTS]), ALU.is_equal).then_inc(first_place, 1)

            shape = [TC, ALL_E, MAX_STEPS]
            link(dve.tensor_tensor(tile_cmp[:], ps[0:TC, 1, NC * ALL_E:(NC + 1) * ALL_E].unsqueeze(2).to_broadcast(shape),
                                   c("steps", TC).unsqueeze(1).to_broadcast(shape), ALU.is_gt))
            link(dve.tensor_reduce(tiles_of[:], tile_cmp[:], X, ALU.add))
            dve.wait_ge(first_list, 1)
            both(dve.tensor_copy(list_sb[:, 0], ps[:, 5, 0:LIST_W]),
                 dve.tensor_tensor_scan(tiles_end[:], zeros[:, 0:ALL_E], tiles_of[:], 0.0, ALU.add, ALU.add))
            both(dve.scalar_tensor_tensor(out=fetch_f[:, 0:1], in0=list_sb[:, 0, 1:2], scalar=float(TC), in1=list_sb[:, 0, 0:1],
                                          op0=ALU.mult, op1=ALU.add),
                 dve.tensor_scalar(owner_cmp[:], tiles_end[0:TABLE], c("tile", TABLE), None, ALU.is_le))
            dve.tensor_copy(fetch[:, 0:1], fetch_f[:, 0:1]).then_inc(fetch_ready, 1)
            both(dve.tensor_reduce(owner[:], owner_cmp[:], X, ALU.add),
                 dve.tensor_tensor(first_slot[:], tiles_end[:], tiles_of[:], ALU.subtract))
            dve.tensor_scalar(owner[:], owner[:], float(ALL_E - 1), None, ALU.min).then_inc(owner_ready, 1)
            both(dve.tensor_scalar(first_slot[:], first_slot[:], float(SLOTS), 1.0, ALU.mult, ALU.add),
                 dve.tensor_copy(table[0:1, TABLE:TABLE + 1], tiles_end[0:1, ALL_E - 1:ALL_E]),
                 dve.tensor_scalar(pair_cmp[:], c("pairs", 1), tiles_end[0:1, ALL_E - 1:ALL_E], 2.0, ALU.is_lt, ALU.mult))
            both(dve.tensor_tensor(slot_tmp[:], rank_v, first_slot[:].unsqueeze(1).to_broadcast([TC, NC, ALL_E]), ALU.add),
                 dve.tensor_reduce(last_start[:], pair_cmp[:], X, ALU.add))
            both(dve.tensor_tensor(slot_tmp[:], slot_tmp[:], sel_v, ALU.mult),
                 dve.tensor_copy(table[0:1, TABLE + 1:TABLE + 2], last_start[:]))
            dve.wait_ge(owner_done, 1)
            dve.tensor_copy(table[0:1, 0:TABLE], ps[0:1, 2, 0:TABLE]).then_inc(table_ready, 1)
            link(dve.tensor_scalar(slot_of[:].rearrange("p e c -> p c e"), slot_tmp[:], -1.0, None, ALU.add))

            def copy_tokens(u):
                dve.tensor_copy(xt[0:DC, u], ps[0:DC, 4 + u, 0:KC * SLOTS].rearrange("p (k s) -> p k s", k=KC)).then_inc(xt_ready, 1)

            dve.wait_ge(gexp_ready, 2)
            both(dve.tensor_tensor(gate_g[:], gate_g[:], sel_g[:], ALU.mult),
                 dve.scalar_tensor_tensor(out=fe(gate_e[:]), in0=fe(rank_e[:]), scalar=float(TOP_E), in1=fe(gate_e[:]), op0=ALU.is_lt, op1=ALU.mult))
            both(dve.tensor_reduce(red_g[:], gate_g[:], X, ALU.add), dve.tensor_reduce(red_e[:], gate_e[:], X, ALU.add))
            both(dve.reciprocal(red_g[:], red_g[:]), dve.reciprocal(red_e[:], red_e[:]))
            both(dve.tensor_tensor(gate_g[:], gate_g[:], red_g[:].unsqueeze(2).to_broadcast([TC, NC, GROUPS]), ALU.mult),
                 dve.tensor_tensor(gate_e[:], gate_e[:], red_e[:].unsqueeze(3).to_broadcast(wide), ALU.mult))
            both(*(dve.scalar_tensor_tensor(out=v, in0=v, scalar=GATE_EPS, in1=v, op0=ALU.is_ge, op1=ALU.mult)
                   for v in (fg(gate_g[:]), fe(gate_e[:]))))
            dve.tensor_tensor(comb[:], gate_e[:], gate_g[:].unsqueeze(3).to_broadcast(wide), ALU.mult).then_inc(comb_ready, 1)
            dve.wait_ge(xt_done, 1)
            copy_tokens(0)
            comb_v = comb[:].rearrange("p c g e -> p c (g e)")
            dve.wait_ge(comb_ready, 1)
            link(dve.tensor_copy(part[4], comb_v))
            link(dve.tensor_tensor(rest[:], comb_v, part[4], ALU.subtract))
            link(dve.tensor_copy(part[5], rest[:]))
            link(dve.tensor_tensor(rest[:], rest[:], part[5], ALU.subtract))
            link(dve.tensor_copy(part[6], rest[:]))
            dve.wait_ge(comb_ready, 1)
            dve.wait_ge(table_ready, 1)

            def wait_small(base_count, ins, k):
                ins.then_inc(small_chain, 1)
                dve.wait_ge(small_chain, base_count + k)

            def make_place(tile_no, u, done):
                e = dve.value_load(table[0:1, bass.ds(tile_no, 1)], min_val=0, max_val=ALL_E - 1)
                a = AT["first"][0]
                wait_small(done, dve.tensor_scalar(slot_rel[:], slot_of[:, bass.ds(e, 1)].rearrange("p a c -> p (a c)"),
                                                   cst[0:TC, bass.ds(tile_no + a, 1)], None, ALU.subtract), 1)
                wait_small(done, dve.tensor_copy(list_col[:, u].rearrange("p c w -> p (c w)"),
                                                 list_src[:, bass.ds(e, 1)].rearrange("p a c w -> p (a c w)")), 2)
                shape = [TC, NC, SLOTS]
                dve.tensor_tensor(place[:, u], slot_rel[:].unsqueeze(2).to_broadcast(shape),
                                  c("slot", TC).unsqueeze(1).to_broadcast(shape), ALU.is_equal).then_inc(place_ready, 1)

            def read_list(u, done, first=False):
                l = list_sb[:, u]
                wait_small(done, dve.tensor_copy(l, ps[:, 4 + u, 0:LIST_W]), 1)
                if first:
                    dve.sem_inc(list_read, 1)
                    dve.sem_inc(small_chain, 1)
                    return
                wait_small(done, dve.scalar_tensor_tensor(out=fetch_f[:, u:u + 1], in0=l[:, 1:2], scalar=float(TC), in1=l[:, 0:1],
                                                          op0=ALU.mult, op1=ALU.add), 2)
                dve.tensor_copy(fetch[:, u:u + 1], fetch_f[:, u:u + 1]).then_inc(fetch_ready, 1)

            def read_meta(u, r, done):
                l = list_sb[:, u]
                spare = c("spare")[:, u:u + 1]
                wait_small(done, dve.scalar_tensor_tensor(out=store_f[:, u, 0:1], in0=l[:, 3:4], scalar=float(TOKENS), in1=fetch_f[:, u:u + 1],
                                                          op0=ALU.mult, op1=ALU.add), 1)
                wait_small(done, dve.scalar_tensor_tensor(out=store_f[:, u, 1:2], in0=l[:, 2:3], scalar=spare, in1=store_f[:, u, 0:1],
                                                          op0=ALU.mult, op1=ALU.subtract), 2)
                wait_small(done, dve.tensor_scalar(store[:, r:r + 1], store_f[:, u, 1:2], -1.0, spare, ALU.mult, ALU.add), 3)
                dve.scalar_tensor_tensor(out=gate[:, r:r + 1], in0=l[:, 6:7], scalar=l[:, 5:6], in1=l[:, 4:5],
                                         op0=ALU.add, op1=ALU.add).then_inc(meta_ready, 1)

            SMALL = 7
            dve.tensor_copy(list_col[:, 0], list_src[:, 0]).then_inc(place_ready, 1)
            make_place(1, 1, 0)
            dve.wait_ge(list_done, 1)
            read_list(0, 2, first=True)
            dve.wait_ge(list_done, 2)
            read_list(1, 4)
            read_meta(0, 0, 6)
            make_place(2, 0, 9)
            dve.wait_ge(xt_done, 2)
            copy_tokens(1)
            read_meta(1, 1, 11)
            dve.wait_ge(list_done, 3)
            read_list(0, 14)
            make_place(3, 1, 16)
            read_meta(0, 2, 18)
            n = dve.value_load(table[0:1, TABLE:TABLE + 1], min_val=0, max_val=TILES)
            with dve.Fori(0, TILES // STEP) as q:
                with ExitStack() as reached:
                    for pair in range(STEP // 2):
                        reached.enter_context(dve.If(q * STEP + 2 * pair < n))
                        for j in (2 * pair, 2 * pair + 1):
                            t = q * STEP + j
                            done = q * (STEP * SMALL) + (SMALL * 3 + SMALL * j)
                            dve.wait_ge(list_done, t + 4)
                            read_list(ring_pos(j, 3, 2), done)
                            dve.wait_ge(xt_done, t + 3)
                            copy_tokens(ring_pos(j, 2, 2))
                            make_place(t + 4, ring_pos(j, 4, 2), done + 2)
                            dve.wait_ge(o_ready, t + 2)
                            dve.wait_ge(o_free[ring_pos(j, 1, 2)], q * (8 * STEP) + 16 * ((j + 1) // 2 + 1))
                            read_meta(ring_pos(j, 3, 2), ring_pos(j, 3, RING), done + 4)

            dve.memset(zeros[:, 0:1], 0.0).then_inc(tiles_over, 1)

            def close(g):
                dve.wait_ge(base_sum_done, g // 2 + 1)
                dve.tensor_tensor(total[:, g], total[:, g], ps[0:TC, g // 2, (g % 2) * DIM:(g % 2 + 1) * DIM],
                                  ALU.add).then_inc(out_ready, 1)

            for g in range(OWN_SUMS):
                for part in range(2):
                    dve.wait_ge(picks_ready[part], 16 * NC)
                dve.tensor_reduce(total[:, g], picks[:, g, PE_SUMS:].rearrange("p k d -> p d k"), X, ALU.add).then_inc(picks_summed, 1)
                if g >= 1:
                    dve.wait_ge(picks_summed, g)
                    close(g - 1)
            dve.wait_ge(picks_summed, OWN_SUMS)
            close(OWN_SUMS - 1)
            dve.wait_ge(pool_summed, 1)
            for g in range(OWN_SUMS, NC):
                close(g)


_INS = ["x", "L0_tok_patch_w", "L0_tok_patch_b", "L0_tok_ln_g", "L0_tok_ln_b", "L0_tok_w1", "L0_tok_w2", "L0_tok_w3",
        "L0_tok_wqkv", "L0_tok_bqkv", "L0_tok_wo", "L0_tok_bo", "L0_attn_Wq", "L0_attn_Wk", "L0_attn_betas",
        "L0_ffn_Wg", "L0_ffn_bg", "L0_ffn_We", "L0_ffn_be", "L0_ffn_W1", "L0_ffn_b1", "L0_ffn_W2", "L0_ffn_b2"]

def kernel(**inputs):
    import numpy as _np
    import concourse.bacc as _bacc
    from concourse import mybir as _mybir
    from concourse.bass_utils import run_bass_kernel_spmd as _run

    nc = _bacc.Bacc("TRN2", target_bir_lowering=False, num_devices=1)
    arrays, args = {}, []
    for name in _INS:
        a = _np.ascontiguousarray(inputs[name])
        arrays[f"in_{name}_dram"] = a
        args.append(nc.dram_tensor(f"in_{name}_dram", a.shape, _mybir.dt.from_np(a.dtype), kind="ExternalInput").ap())
    arrays["in_constants_dram"] = constants()
    args.append(nc.dram_tensor("in_constants_dram", (128, CONST_W), _mybir.dt.float32, kind="ExternalInput").ap())
    args.append(nc.dram_tensor("out_0_dram", (BATCH, SEQ, DIM), _mybir.dt.float32, kind="ExternalOutput").ap())
    vit_moe_program(nc, *args)
    r = _run(nc, [arrays], core_ids=[0])
    return r.results[0]["out_0_dram"]
```
